# Optimizing a Trainium2 kernel written in Bass

```python
import numpy as np
import jax
import jax.numpy as jnp

def _softmax(x, axis=-1):
    return jax.nn.softmax(x, axis=axis)

def _gelu(x):
    return jax.nn.gelu(x, approximate=True)

def _silu(x):
    return jax.nn.silu(x)

def _sigmoid(x):
    return jax.nn.sigmoid(x)

def _layernorm(x, axis=-1, eps=1e-05):
    m = jnp.mean(x, axis=axis, keepdims=True)
    v = jnp.var(x, axis=axis, keepdims=True)
    return (x - m) / jnp.sqrt(v + eps)

def _scatter_add(tgt, idx, src, axis=0):
    return tgt.at[idx].add(src)

def _segment_sum(src, seg, n):
    return jax.ops.segment_sum(src, seg, n)
kernel_name = 'mk_gnn_resnorm_d4_gnn_r32_118aaa'

def setup_inputs(seed: int=0):
    np.random.seed(seed)
    _w = jnp.asarray

    def _rec_inputs():
        import jax
        import jax.numpy as jnp
        _gk = jax.random.key(seed)
        x = -0.0001006 + 1 * jax.random.normal(jax.random.fold_in(_gk, 1), (50000, 96), jnp.float32)
        src = jax.random.randint(jax.random.fold_in(_gk, 2), (50000,), 0, 50000, jnp.int32)
        dst = jax.random.randint(jax.random.fold_in(_gk, 3), (50000,), 0, 50000, jnp.int32)
        _o = jnp.argsort(dst, stable=True)
        src = src[_o]
        dst = dst[_o]
        edge_attr_32 = 0.000196303 + 1.00016 * jax.random.normal(jax.random.fold_in(_gk, 12), (50000, 32), jnp.float32)
        return (x, src, dst, edge_attr_32)
    x, src, dst, edge_attr_32 = _rec_inputs()

    def _L0_gnn_setup():
        import jax, jax.numpy as jnp
        import numpy as np
        N_NODES = 50000
        N_EDGES = 25000
        D_FEAT = 96
        OUT_DIM = 96
        key = jax.random.key(seed)
        k1, k2, k3, k4 = jax.random.split(key, 4)
        x = jax.random.normal(k1, (N_NODES, D_FEAT), dtype=jnp.float32)
        W = jax.random.normal(k2, (D_FEAT, OUT_DIM), dtype=jnp.float32) / np.sqrt(D_FEAT)
        b = jnp.zeros((OUT_DIM,), dtype=jnp.float32)
        src = jax.random.randint(k3, (N_EDGES,), 0, N_NODES, dtype=jnp.int64)
        dst = jax.random.randint(k4, (N_EDGES,), 0, N_NODES, dtype=jnp.int64)
        return {'x': x, 'W': W, 'b': b, 'src': src, 'dst': dst}
    _L0_gnn_all = _L0_gnn_setup()
    _L0_gnn_in = {k: v for k, v in _L0_gnn_all.items() if k in ('W', 'b')}
    del _L0_gnn_all

    def _L1_gnn_setup():
        import jax, jax.numpy as jnp
        import numpy as np
        N, E = (50000, 25000)
        DIN = DOUT = 96
        DE = 32

        def _egnn_conv(x, src, dst, edge_attr, W_msg, W_edge, W_root, b):
            msg = x[src] @ W_msg + edge_attr @ W_edge
            agg = jax.ops.segment_max(msg, dst, num_segments=x.shape[0])
            agg = jnp.where(jnp.isneginf(agg), 0.0, agg)
            return agg + x @ W_root + b
        key = jax.random.key(seed)
        ks = jax.random.split(key, 10)
        rn = lambda k, sh, sc: jax.random.normal(k, sh, jnp.float32) * sc
        return {'X': rn(ks[0], (N, DIN), 1.0), 'edge_index': jax.random.randint(ks[1], (2, E), 0, N, jnp.int32), 'edge_attr': rn(ks[2], (E, DE), 1.0), 'W1_msg': rn(ks[3], (DIN, DOUT), DIN ** (-0.5)), 'W1_edge': rn(ks[4], (DE, DOUT), DE ** (-0.5)), 'W1_root': rn(ks[5], (DIN, DOUT), DIN ** (-0.5)), 'b1': jnp.zeros((DOUT,), jnp.float32), 'W2_msg': rn(ks[6], (DOUT, DOUT), DOUT ** (-0.5)), 'W2_edge': rn(ks[7], (DE, DOUT), DE ** (-0.5)), 'W2_root': rn(ks[8], (DOUT, DOUT), DOUT ** (-0.5)), 'b2': jnp.zeros((DOUT,), jnp.float32)}
    _L1_gnn_all = _L1_gnn_setup()
    _L1_gnn_in = {k: v for k, v in _L1_gnn_all.items() if k in ('W1_msg', 'W1_edge', 'W1_root', 'b1', 'W2_msg', 'W2_edge', 'W2_root', 'b2')}
    del _L1_gnn_all

    def _L2_gnn_setup():
        import jax, jax.numpy as jnp
        import numpy as np
        EPS = 1e-07
        BETA = 1.0
        key = jax.random.key(seed)
        k1, k2, k3, k4 = jax.random.split(key, 4)
        N, E, D_IN, D_OUT = (50000, 25000, 96, 96)
        feat = jax.random.normal(k1, (N, D_IN), dtype=jnp.float32)
        src = jax.random.randint(k2, (E,), 0, N, dtype=jnp.int32)
        dst = jax.random.randint(k3, (E,), 0, N, dtype=jnp.int32)
        W = jax.random.normal(k4, (D_IN, D_OUT), dtype=jnp.float32) / np.sqrt(D_IN)
        b = jnp.zeros((D_OUT,), dtype=jnp.float32)
        return {'feat': feat, 'src': src, 'dst': dst, 'W': W, 'b': b}
    _L2_gnn_all = _L2_gnn_setup()
    _L2_gnn_in = {k: v for k, v in _L2_gnn_all.items() if k in ('W', 'b')}
    del _L2_gnn_all

    def _L3_gnn_setup():
        import jax, jax.numpy as jnp
        import numpy as np
        N_NODES = 50000
        N_EDGES = 25000
        D_IN = 96
        D_OUT = 96
        NEG_SLOPE = 0.2
        key = jax.random.key(seed)
        k1, k2, k3, k4, k5 = jax.random.split(key, 5)
        x = jax.random.normal(k1, (N_NODES, D_IN), dtype=jnp.float32)
        W = jax.random.normal(k2, (D_IN, D_OUT), dtype=jnp.float32) * (1.0 / np.sqrt(D_IN))
        att_src = jax.random.normal(k3, (D_OUT,), dtype=jnp.float32) * 0.1
        att_dst = jax.random.normal(k4, (D_OUT,), dtype=jnp.float32) * 0.1
        bias = jnp.zeros((D_OUT,), dtype=jnp.float32)
        edge_index = jax.random.randint(k5, (2, N_EDGES), 0, N_NODES, dtype=jnp.int64)
        return {'x': x, 'W': W, 'att_src': att_src, 'att_dst': att_dst, 'bias': bias, 'edge_index': edge_index}
    _L3_gnn_all = _L3_gnn_setup()
    _L3_gnn_in = {k: v for k, v in _L3_gnn_all.items() if k in ('W', 'att_src', 'att_dst', 'bias')}
    del _L3_gnn_all
    return {'x': x, 'src': src, 'dst': dst, 'edge_attr_32': edge_attr_32, 'L0_gnn_W': _L0_gnn_in['W'], 'L0_gnn_b': _L0_gnn_in['b'], 'L1_gnn_W1_msg': _L1_gnn_in['W1_msg'], 'L1_gnn_W1_edge': _L1_gnn_in['W1_edge'], 'L1_gnn_W1_root': _L1_gnn_in['W1_root'], 'L1_gnn_b1': _L1_gnn_in['b1'], 'L1_gnn_W2_msg': _L1_gnn_in['W2_msg'], 'L1_gnn_W2_edge': _L1_gnn_in['W2_edge'], 'L1_gnn_W2_root': _L1_gnn_in['W2_root'], 'L1_gnn_b2': _L1_gnn_in['b2'], 'L2_gnn_W': _L2_gnn_in['W'], 'L2_gnn_b': _L2_gnn_in['b'], 'L3_gnn_W': _L3_gnn_in['W'], 'L3_gnn_att_src': _L3_gnn_in['att_src'], 'L3_gnn_att_dst': _L3_gnn_in['att_dst'], 'L3_gnn_bias': _L3_gnn_in['bias']}

def reference(x, src, dst, edge_attr_32, L0_gnn_W, L0_gnn_b, L1_gnn_W1_msg, L1_gnn_W1_edge, L1_gnn_W1_root, L1_gnn_b1, L1_gnn_W2_msg, L1_gnn_W2_edge, L1_gnn_W2_root, L1_gnn_b2, L2_gnn_W, L2_gnn_b, L3_gnn_W, L3_gnn_att_src, L3_gnn_att_dst, L3_gnn_bias):
    import jax
    import jax.numpy as jnp

    def _L0_gnn_ref(x, W, b, src, dst):
        import jax, jax.numpy as jnp
        import numpy as np
        N_NODES = 50000
        N_EDGES = 25000
        D_FEAT = 96
        OUT_DIM = 96
        ones = jnp.ones(src.shape[0], dtype=x.dtype)
        deg_out = jax.ops.segment_sum(ones, src, num_segments=N_NODES)
        deg_in = jax.ops.segment_sum(ones, dst, num_segments=N_NODES)
        inv_sqrt_out = jnp.where(deg_out > 0, jax.lax.rsqrt(deg_out), 0.0)
        inv_sqrt_in = jnp.where(deg_in > 0, jax.lax.rsqrt(deg_in), 0.0)
        h = x @ W
        coef = inv_sqrt_out[src] * inv_sqrt_in[dst]
        msg = h[src] * coef[:, None]
        agg = jax.ops.segment_sum(msg, dst, num_segments=N_NODES)
        return agg + b

    def _L1_gnn_ref(X, edge_index, edge_attr, W1_msg, W1_edge, W1_root, b1, W2_msg, W2_edge, W2_root, b2):
        import jax, jax.numpy as jnp
        import numpy as np
        N, E = (50000, 25000)
        DIN = DOUT = 96
        DE = 32

        def _egnn_conv(x, src, dst, edge_attr, W_msg, W_edge, W_root, b):
            msg = x[src] @ W_msg + edge_attr @ W_edge
            agg = jax.ops.segment_max(msg, dst, num_segments=x.shape[0])
            agg = jnp.where(jnp.isneginf(agg), 0.0, agg)
            return agg + x @ W_root + b
        src, dst = (edge_index[0], edge_index[1])
        c1 = jax.nn.leaky_relu(_egnn_conv(X, src, dst, edge_attr, W1_msg, W1_edge, W1_root, b1))
        c2 = jax.nn.leaky_relu(_egnn_conv(c1, src, dst, edge_attr, W2_msg, W2_edge, W2_root, b2))
        return c2

    def _L2_gnn_ref(feat, src, dst, W, b):
        import jax, jax.numpy as jnp
        import numpy as np
        EPS = 1e-07
        BETA = 1.0
        N = feat.shape[0]
        m = jax.nn.relu(feat[src]) + EPS
        logits = BETA * m
        seg_max = jax.ops.segment_max(logits, dst, num_segments=N)
        ex = jnp.exp(logits - seg_max[dst])
        denom = jax.ops.segment_sum(ex, dst, num_segments=N)
        a = ex / denom[dst]
        msg = jax.ops.segment_sum(a * m, dst, num_segments=N)
        feats = feat + msg
        return feats @ W + b

    def _L3_gnn_ref(x, W, att_src, att_dst, bias, edge_index):
        import jax, jax.numpy as jnp
        import numpy as np
        N_NODES = 50000
        N_EDGES = 25000
        D_IN = 96
        D_OUT = 96
        NEG_SLOPE = 0.2
        N = x.shape[0]
        h = x @ W
        loops = jnp.arange(N, dtype=edge_index.dtype)
        src = jnp.concatenate([edge_index[0], loops])
        dst = jnp.concatenate([edge_index[1], loops])
        a_src = h @ att_src
        a_dst = h @ att_dst
        e = jax.nn.leaky_relu(a_src[src] + a_dst[dst], NEG_SLOPE)
        m = jax.ops.segment_max(e, dst, num_segments=N)
        e = jnp.exp(e - m[dst])
        denom = jax.ops.segment_sum(e, dst, num_segments=N)
        alpha = e / (denom[dst] + 1e-16)
        out = jax.ops.segment_sum(h[src] * alpha[:, None], dst, num_segments=N)
        return jnp.tanh(out + bias)
    edge_index = jnp.stack([src, dst])
    x = _layernorm(x + _L0_gnn_ref(x, L0_gnn_W, L0_gnn_b, src, dst), axis=-1)
    x = _layernorm(x + _L1_gnn_ref(x, edge_index, edge_attr_32, L1_gnn_W1_msg, L1_gnn_W1_edge, L1_gnn_W1_root, L1_gnn_b1, L1_gnn_W2_msg, L1_gnn_W2_edge, L1_gnn_W2_root, L1_gnn_b2), axis=-1)
    x = _layernorm(x + _L2_gnn_ref(x, src, dst, L2_gnn_W, L2_gnn_b), axis=-1)
    x = _layernorm(x + _L3_gnn_ref(x, L3_gnn_W, L3_gnn_att_src, L3_gnn_att_dst, L3_gnn_bias, edge_index), axis=-1)
    return x

_drawn_inputs = setup_inputs


def setup_inputs(seed=0):
    import zlib

    import numpy as np

    out = dict(_drawn_inputs(seed))
    spreads = {'L0_gnn_b': (0.0, 0.1),
     'L1_gnn_b1': (0.0, 0.1),
     'L1_gnn_b2': (0.0, 0.1),
     'L2_gnn_b': (0.0, 0.1),
     'L3_gnn_bias': (0.0, 0.1)}
    factors = {}
    for name, (base, spread) in spreads.items():
        noise = np.random.default_rng([zlib.crc32(name.encode()), seed]).standard_normal(out[name].shape)
        drawn = base * np.exp(spread * noise) if base else spread * noise
        out[name] = jnp.asarray(drawn.astype(out[name].dtype))
    for name, factor in factors.items():
        out[name] = (out[name] * factor).astype(out[name].dtype)
    return out
```

```python
import numpy as np
import concourse.bass as bass
from concourse import mybir
from contextlib import ExitStack

F32 = mybir.dt.float32
I32 = mybir.dt.int32
BF16 = mybir.dt.bfloat16
F16 = mybir.dt.float16
ALU = mybir.AluOpType
ACT = mybir.ActivationFunctionType

D = 96
DE = 32
Q = 8
H = Q // 2
CH = 128 * Q
N_NODES = 50000
N_EDGES = 50000
NCH = -(-N_NODES // CH)
NP = NCH * CH
EP = NCH * CH
ROWS = EP + NP
J = EP // 128
LO = 512
HI = NP // LO
XW = 100
POS, INV_OUT, INV_IN = 96, 97, 98
BIG = 3.0e38
FAR = 1 << 20
LN_EPS = 1e-5
MSG_EPS = 1e-7
LEAK = 0.01
LEAK_ATT = 0.2
assert NCH % 2 == 1 and NCH >= 9 and HI <= 128


def chunks(eng, *stages):
    deep = max(lag for _, lag in stages)

    def step(c):
        for stage, lag in stages:
            if 0 <= c - lag < NCH:
                stage(c - lag, (c - lag) // 2, (c - lag) % 2, c - lag >= 2)

    start = (deep + 3) // 2
    for c in range(2 * start):
        step(c)
    with eng.Fori(start, NCH // 2) as i:
        for odd in range(2):
            for stage, lag in stages:
                stage(i * 2 + (odd - lag), i + (odd - lag) // 2, (odd - lag) % 2, True)
    for c in range(NCH - 1, NCH + deep):
        step(c)


def wait(eng, sem, value):
    eng.wait_ge(sem, value)
    if not isinstance(value, int):
        eng.nop(nofuse=True)


def rows_of(table, c, base=0):
    if isinstance(c, int):
        part = table[base + c * CH:base + c * CH + CH, :]
    else:
        part = table[bass.ds(c * CH + base, CH), :]
    return part.rearrange("(a p r) d -> p a (r d)", a=2, r=H)


def halves(tile):
    return tile.rearrange("p (a r) d -> p a (r d)", a=2)


def scalars_of(row, c):
    part = row[:, c * CH:(c + 1) * CH] if isinstance(c, int) else row[:, bass.ds(c * CH, CH)]
    return part.rearrange("o (a p r) -> (o p) a r", a=2, r=H)


def tile_columns(q):
    at = q // H * 512 + q % H
    return slice(at, at + 509, H)


def span(view, c, width):
    if isinstance(c, int):
        return view[:, c * width:(c + 1) * width]
    return view[:, bass.ds(c * width, width)]


def one(view, c):
    part = view[c:c + 1] if isinstance(c, int) else view[bass.ds(c, 1)]
    return part.rearrange("a p q -> p (a q)")


def clear(nc, sems):
    numbers = [s.num for s in sems]
    assert numbers == list(range(numbers[0], numbers[0] + len(numbers)))
    block = nc.Block()
    with block:
        @block.sync
        def _(sp):
            sp.sem_clear(range(numbers[0], numbers[-1] + 1))

        @block.scalar
        def _(act):
            act.nop()

        @block.vector
        def _(dve):
            dve.nop()

        @block.gpsimd
        def _(pool):
            pool.nop()

        @block.tensor
        def _(pe):
            pe.nop()


def segment_kernel(nc, x, ids, dst_ext, edge_t, W0, b0, W1m, W1e, W1r, b1, W2m, W2e, W2r, b2, Wg, bg,
                   Wa, att_s, att_d, ba, out):
    ctx = ExitStack()
    with ctx:
        def sb(name, shape, dt=F32):
            return ctx.enter_context(nc.sbuf_tensor(name, shape, dt))

        dram = lambda name, shape, dt=F32: nc.dram_tensor(name, shape, dt).ap()
        xa = dram("xa", (NP, XW))
        info = dram("info", (3, NP))
        mask_d = dram("mask_d", (1, EP), BF16)
        next_d = dram("next_d", (1, EP))
        scat_d = dram("scat_d", (1, EP), I32)
        src_rows = dram("src_rows", (NCH, 128, Q), I32)
        t1 = dram("t1", (ROWS, D))
        tc = dram("tc", (ROWS, D))
        t2 = dram("t2", (ROWS, D))
        t3 = dram("t3", (ROWS, D))
        ad_d = dram("ad_d", (1, EP))
        ads_d = dram("ads_d", (1, EP))

        ident = sb("ident", [128, 128])
        eps = sb("eps", [128, 1])

        degrees(nc, x, ids, dst_ext, xa, info, mask_d, next_d, scat_d, ident, eps)
        with nc.sbuf_tensor("mask", [D, EP], BF16) as mask:
            layer0(nc, x, ids, xa, src_rows, t1, tc, W0, b0, W1r, b1, mask, mask_d, ident, eps)
            layer1(nc, "a", t1, t1, tc, src_rows, edge_t, W1m, W1e, W1r, b1, mask, ident, eps,
                   node=(tc, t1, t2, W2r, b2))
            layer1(nc, "b", tc, t1, t2, src_rows, edge_t, W2m, W2e, W2r, b2, mask, ident, eps,
                   node=(t2, t2, t3, Wg, bg))
        layer2(nc, t2, t3, src_rows, ad_d, Wg, bg, Wa, att_d, mask_d, ident, eps, node=(t3, out, Wa, ba))
        spread(nc, ad_d, next_d, ads_d, ident)
        layer3(nc, t3, src_rows, scat_d, ads_d, mask_d, out, Wa, att_s, att_d, ba, ident, eps)


def degrees(nc, x, ids, dst_ext, xa, info, mask_d, next_d, scat_d, ident, eps):
    K = 4
    JK = J // K
    ctx, sems = ExitStack(), ExitStack()
    with sems, ctx:
        def sb(name, shape, dt=F32):
            return ctx.enter_context(nc.sbuf_tensor(name, shape, dt))

        used = []

        def sem(name):
            used.append(sems.enter_context(nc.semaphore("dg_" + name)))
            return used[-1]

        idall = sb("idall", [128, NCH, 2 * Q], I32)
        shifted = sb("shifted", [128, NCH, 2 * Q], I32)
        hi = sb("hi", [128, NCH, 2 * Q], BF16)
        lo = sb("lo", [128, NCH, 2 * Q])
        iota_lo = sb("iota_lo", [128, LO], F16)
        iota_hi = sb("iota_hi", [128, HI], BF16)
        hot_lo = sb("hot_lo", [128, 2, 2 * Q, LO], BF16)
        hot_hi = sb("hot_hi", [128, 2, 2 * Q, HI], BF16)
        zero = sb("zero", [128, LO], BF16)
        before = sb("before", [HI, HI])
        nid = sb("nid", [HI, LO])
        ends = sb("ends", [HI, LO])
        offs = sb("offs", [HI, 1])
        has = sb("has", [HI, 2, LO])
        root = sb("root", [HI, 2, LO])
        fac = sb("fac", [HI, 3, LO])
        inf = sb("inf", [128, 3, J])
        dprev = sb("dprev", [128, J], I32)
        dcur = sb("dcur", [128, J], I32)
        dnext = sb("dnext", [128, J], I32)
        same = sb("same", [128, J], BF16)
        same_next = sb("same_next", [128, J])
        scat = sb("scat", [128, J], I32)
        xt = sb("xt", [128, 2, JK, XW])
        counts = ctx.enter_context(nc.psum_tensor("counts", [128, 2, LO], F32))
        off_ps = ctx.enter_context(nc.psum_tensor("off_ps", [128, LO], F32))

        ids_in = sem("ids_in")
        dst_in = sem("dst_in")
        x_in = [sem("x_in0"), sem("x_in1")]
        x_out = [sem("x_out0"), sem("x_out1")]
        consts = sem("consts")
        id_zero = sem("id_zero")
        split = sem("split")
        hot_ready = sem("hot_ready")
        counted = sem("counted")
        totals = sem("totals")
        offsets = sem("offsets")
        rooted_in = sem("rooted_in")
        rooted = sem("rooted")
        facs = sem("facs")
        info_out = sem("info_out")
        info_in = sem("info_in")
        flags = sem("flags")
        flags_out = sem("flags_out")
        filled = sem("filled")
        block = ctx.enter_context(nc.Block())
        xv = x.rearrange("(p j) d -> p j d", p=128)
        xav = xa.rearrange("(p j) d -> p j d", p=128)
        flat = lambda at: dst_ext[at:at + EP].rearrange("(p j) -> p j", p=128)

        @block.sync
        def _(sp):
            sp.dma_start(idall[:, :, :], ids.rearrange("c p q -> p c q")).then_inc(ids_in, 16)
            sp.dma_start(dprev[:, :], flat(0)).then_inc(dst_in, 16)
            sp.dma_start(dcur[:, :], flat(1)).then_inc(dst_in, 16)
            sp.dma_start(dnext[:, :], flat(2)).then_inc(dst_in, 16)
            for k in range(2):
                sp.dma_start(xt[:, k, :, 0:D], xv[:, k * JK:(k + 1) * JK, :]).then_inc(x_in[k], 16)
            sp.wait_ge(flags, 3)
            sp.dma_start(mask_d.rearrange("a (p j) -> (a p) j", p=128), same[:, :]).then_inc(flags_out, 16)
            sp.dma_start(next_d.rearrange("a (p j) -> (a p) j", p=128), same_next[:, :])\
              .then_inc(flags_out, 16)
            sp.dma_start(scat_d.rearrange("a (p j) -> (a p) j", p=128), scat[:, :])\
              .then_inc(flags_out, 16)
            sp.wait_ge(facs, 3)
            sp.dma_start(info.rearrange("k (h l) -> h k l", l=LO), fac[:, :, :]).then_inc(info_out, 16)
            sp.wait_ge(info_out, 16)
            sp.dma_start(inf[:, :, :], info.rearrange("k (p j) -> p k j", p=128)).then_inc(info_in, 16)
            for k in range(K):
                u = k % 2
                sp.wait_ge(filled, k + 1)
                sp.dma_start(xav[:, k * JK:(k + 1) * JK, :], xt[:, u, :, :]).then_inc(x_out[u], 16)
                if k + 2 < K:
                    sp.wait_ge(x_out[u], 16 * (k // 2 + 1))
                    sp.dma_start(xt[:, u, :, 0:D], xv[:, (k + 2) * JK:(k + 3) * JK, :])\
                      .then_inc(x_in[u], 16)
            for s in x_out:
                sp.wait_ge(s, 16 * K // 2)
            sp.wait_ge(flags_out, 48)

        @block.gpsimd
        def _(pool):
            pool.iota(iota_lo[:, :], [[1, LO]], base=0, channel_multiplier=0,
                      allow_small_or_imprecise_dtypes=True).then_inc(consts, 1)
            pool.iota(iota_hi[:, :], [[1, HI]], base=0, channel_multiplier=0,
                      allow_small_or_imprecise_dtypes=True).then_inc(consts, 1)
            pool.iota(nid[:, :], [[1, LO]], base=EP, channel_multiplier=LO,
                      allow_small_or_imprecise_dtypes=True).then_inc(consts, 1)
            pool.memset(ident[:, :], 0.0).then_inc(id_zero, 1)
            pool.memset(before[:, :], 1.0).then_inc(id_zero, 1)
            pool.wait_ge(id_zero, 2)
            pool.affine_select(out=ident[:, :], in_=ident[:, :], compare_op=ALU.not_equal, fill=1.0,
                               base=0, pattern=[[-1, 128]], channel_multiplier=1).then_inc(consts, 1)
            pool.affine_select(out=before[:, :], in_=before[:, :], compare_op=ALU.is_gt, fill=0.0,
                               base=0, pattern=[[1, HI]], channel_multiplier=-1).then_inc(consts, 1)

        @block.vector
        def _(dve):
            dve.memset(zero[:, :], 0.0)
            dve.memset(eps[:, :], LN_EPS)
            for u in range(2):
                dve.memset(xt[:, u, :, D:XW], 0.0)
            dve.wait_ge(ids_in, 16)
            dve.tensor_scalar(shifted[:, :, :], idall[:, :, :], 9, None, ALU.logical_shift_right)
            dve.drain()
            dve.tensor_copy(hi[:, :, :], shifted[:, :, :]).then_inc(split, 1)
            dve.drain()
            dve.tensor_scalar(shifted[:, :, :], idall[:, :, :], LO - 1, None, ALU.bitwise_and)
            dve.drain()
            dve.tensor_copy(lo[:, :, :], shifted[:, :, :]).then_inc(split, 1)
            dve.drain()
            dve.wait_ge(dst_in, 48)
            dve.tensor_tensor(same[:, :], dcur[:, :], dprev[:, :], ALU.is_equal).then_inc(flags, 1)
            dve.tensor_tensor(same_next[:, :], dcur[:, :], dnext[:, :], ALU.is_equal).then_inc(flags, 1)
            dve.drain()
            dve.scalar_tensor_tensor(scat[:, :], same_next[:, :], float(FAR), dcur[:, :],
                                     ALU.mult, ALU.add).then_inc(flags, 1)
            dve.wait_ge(consts, 5)

            def head(c, i, u, warm):
                if warm:
                    dve.wait_ge(counted, c)
                for q in range(2 * Q):
                    l = lo[:, c, q:q + 1] if isinstance(c, int) else \
                        lo[:, bass.ds(c, 1), q:q + 1].rearrange("p a q -> p (a q)")
                    dve.tensor_scalar(hot_lo[:, u, q, :], iota_lo[:, :], l, None, ALU.is_equal)
                h = hi[:, c:c + 1, :] if isinstance(c, int) else hi[:, bass.ds(c, 1), :]
                h = h.rearrange("p a q -> p (a q)").unsqueeze(2).to_broadcast([128, 2 * Q, HI])
                dve.tensor_tensor(hot_hi[:, u, :, :], h,
                                  iota_hi[:, :].unsqueeze(1).to_broadcast([128, 2 * Q, HI]),
                                  ALU.is_equal).then_inc(hot_ready, 1)
            chunks(dve, (head, 0))

            dve.wait_ge(counted, NCH + 1)
            dve.tensor_scalar(root[:, :, :], counts[0:HI, :, :], 1.0, None, ALU.max).then_inc(rooted_in, 1)
            dve.tensor_scalar(has[:, :, :], counts[0:HI, :, :], 0.0, None, ALU.is_gt)
            dve.drain()
            dve.tensor_tensor_scan(ends[:, :], zero[0:HI, :], counts[0:HI, 1, :], 0.0,
                                   ALU.add, ALU.add).then_inc(totals, 1)
            dve.wait_ge(offsets, 1)
            dve.tensor_scalar(offs[:, :], off_ps[0:HI, 0:1], -1.0, None, ALU.add)
            dve.drain()
            dve.scalar_tensor_tensor(ends[:, :], ends[:, :], offs[:, 0:1], nid[:, :],
                                     ALU.add, ALU.subtract)
            dve.drain()
            dve.tensor_tensor(ends[:, :], ends[:, :], has[:, 1, :], ALU.mult)
            dve.drain()
            dve.tensor_tensor(fac[:, 0, :], ends[:, :], nid[:, :], ALU.add).then_inc(facs, 1)
            dve.wait_ge(rooted, 1)
            dve.reciprocal(root[:, :, :], root[:, :, :])
            dve.drain()
            for k in range(2):
                dve.tensor_tensor(fac[:, 1 + k, :], root[:, k, :], has[:, k, :], ALU.mult)\
                   .then_inc(facs, 1)
            dve.wait_ge(info_in, 16)
            for k in range(K):
                dve.wait_ge(x_in[k % 2], 16 * (k // 2 + 1))
                dve.tensor_copy(xt[:, k % 2, :, D:D + 3],
                                inf[:, :, k * JK:(k + 1) * JK].rearrange("p k j -> p j k"))\
                   .then_inc(filled, 1)

        @block.scalar
        def _(act):
            act.wait_ge(rooted_in, 1)
            act.activation(root[:, :, :], root[:, :, :], ACT.Sqrt).then_inc(rooted, 1)

        @block.tensor
        def _(pe):
            pe.wait_ge(consts, 5)
            pe.wait_ge(split, 2)
            for k in range(2):
                last = pe.matmul(counts[0:HI, k, :], zero[:, 0:HI], zero[:, :], start=True, stop=False,
                                 skip_group_check=True)
            last.then_inc(counted, 1)

            def head(c, i, u, warm):
                pe.wait_ge(hot_ready, c + 1)
                for q in range(2 * Q):
                    last = pe.matmul(counts[0:HI, q // Q, :], hot_hi[:, u, q, :], hot_lo[:, u, q, :],
                                     start=False, stop=False, skip_group_check=True)
                last.then_inc(counted, 1)
            chunks(pe, (head, 0))
            pe.wait_ge(totals, 1)
            pe.matmul(off_ps[0:HI, 0:1], before[:, :], ends[:, LO - 1:LO], start=True, stop=True)\
              .then_inc(offsets, 1)
        ctx.close()
        clear(nc, used)


def norm_stats(dve, tiles, st, mv, done):
    for k, t in enumerate(tiles):
        dve.bn_stats(st[:, k, :], t)
    dve.drain()
    for k in range(len(tiles)):
        last = dve.bn_aggr(mv[:, k, :], st[:, k, :])
    last.then_inc(done, 1)


def norm_apply(dve, tiles, outs, mv, rstd):
    n = len(tiles)
    dve.reciprocal(rstd[:, 0:n], rstd[:, 0:n])
    dve.drain()
    for k, (t, o) in enumerate(zip(tiles, outs)):
        last = dve.tensor_scalar(o, t, mv[:, k, 0:1], rstd[:, k:k + 1], ALU.subtract, ALU.mult)
    return last


def gather(pool, tile, u, table, idx, done):
    for q in range(Q):
        pool.indirect_dma_start(tile[:, u, q, :], None, table,
                                bass.IndirectOffsetOnAxis(idx[:, u, q:q + 1], 0)).then_inc(done[u], 16)


def turn(pe, psum, tile, ident, by_edge):
    for q in range(Q):
        to = psum[0:D, tile_columns(q)] if by_edge else psum[0:D, q * 128:(q + 1) * 128]
        last = pe.transpose(to, tile[:, q, :], ident[:, :])
    return last


def layer0(nc, x, ids, xa, src_rows, t1, tc, W0, b0, W1r, b1, mask, mask_d, ident, eps):
    ctx, sems = ExitStack(), ExitStack()
    with sems, ctx:
        def sb(name, shape, dt=F32):
            return ctx.enter_context(nc.sbuf_tensor("l0_" + name, shape, dt))

        def ps(name):
            return ctx.enter_context(nc.psum_tensor("l0_" + name, [128, 2 * 512], F32))

        used = []

        def sem(name):
            used.append(sems.enter_context(nc.semaphore("l0_" + name)))
            return used[-1]

        w0 = sb("w0", [D, D])
        wr = sb("wr", [D + 1, D])
        b0r = sb("b0r", [128, D])
        idx = sb("idx", [128, 2, 2 * Q], I32)
        gs = sb("gs", [128, 2, Q, XW])
        gd = sb("gd", [128, 2, Q, XW])
        xn = sb("xn", [128, 2, Q, D])
        y = sb("y", [128, 2, Q, D])
        S = sb("S", [D, 2, CH])
        he = sb("he", [128, Q, D])
        hn = sb("hn", [128, Q, D])
        st = sb("st", [128, 2 * Q, 6])
        mv = sb("mv", [128, 2 * Q, 2])
        rstd = sb("rstd", [128, 2 * Q])
        xe_out = sb("xe_out", [128, 2, Q, D])
        xn_out = sb("xn_out", [128, 2, Q, D])
        cn_out = sb("cn_out", [128, 2, Q, D])
        cn_small = sb("cn_small", [128, Q, D])
        row_out = sb("row_out", [128, 2, Q], I32)
        xnT = sb("xnT", [D + 1, CH])
        psT, psA, psX, psN = ps("psT"), ps("psA"), ps("psX"), ps("psN")
        A = psA[:, :].rearrange("p (q d) -> p q d", q=Q)
        N = psN[:, :].rearrange("p (q d) -> p q d", q=Q)

        gs_in = [sem("gs_in0"), sem("gs_in1")]
        gd_in = [sem("gd_in0"), sem("gd_in1")]
        used.clear()
        ready = sem("ready")
        scaled = sem("scaled")
        turned = sem("turned")
        scanned = sem("scanned")
        multiplied = sem("multiplied")
        summed_n = sem("summed_n")
        summed_e = sem("summed_e")
        measured = sem("measured")
        rooted = sem("rooted")
        normed_n = sem("normed_n")
        normed_e = sem("normed_e")
        turned_n = sem("turned_n")
        copied_n = sem("copied_n")
        rooted_n = sem("rooted_n")
        small_n = sem("small_n")
        conv_n = sem("conv_n")
        weights = sem("weights")
        idx_in = [sem("idx_in0"), sem("idx_in1")]
        xn_in = [sem("xn_in0"), sem("xn_in1")]
        stored = [sem("stored0"), sem("stored1")]
        stored_n = [sem("stored_n0"), sem("stored_n1")]
        block = ctx.enter_context(nc.Block())

        @block.sync
        def _(sp):
            sp.dma_start(w0[:, :], W0).then_inc(weights, 16)
            sp.dma_start(wr[0:D, :], W1r).then_inc(weights, 16)
            sp.dma_start(wr[D:D + 1, :], b1).then_inc(weights, 16)
            sp.dma_start(b0r[:, :], b0.to_broadcast([128, D])).then_inc(weights, 16)
            sp.dma_start(mask[:, :], mask_d.to_broadcast([D, EP])).then_inc(weights, 16)

            def head(c, i, u, warm):
                if warm:
                    wait(sp, gs_in[u], 128 * i)
                    wait(sp, gd_in[u], 128 * i)
                sp.dma_start(idx[:, u, :], one(ids, c)).then_inc(idx_in[u], 16)
                if warm:
                    wait(sp, summed_n, c - 1)
                sp.dma_start(halves(xn[:, u, :, :]), rows_of(x, c))\
                  .then_inc(xn_in[u], 16)

            def tail(c, i, u, warm):
                wait(sp, normed_n, c + 1)
                sp.dma_start(rows_of(t1, c, EP), halves(xn_out[:, u, :, :]))\
                  .then_inc(stored[u], 16)
                wait(sp, normed_e, c + 1)
                sp.dma_start(rows_of(t1, c), halves(xe_out[:, u, :, :]))\
                  .then_inc(stored[u], 16)
                sp.dma_start(one(src_rows, c), row_out[:, u, :]).then_inc(stored[u], 16)

            def last(c, i, u, warm):
                wait(sp, conv_n, c + 1)
                sp.dma_start(rows_of(tc, c, EP), halves(cn_out[:, u, :, :]))\
                  .then_inc(stored_n[u], 16)
            chunks(sp, (head, 0), (tail, 2), (last, 3))
            for u in range(2):
                sp.wait_ge(stored[u], 48 * (NCH // 2 + 1 - u))
                sp.wait_ge(stored_n[u], 16 * (NCH // 2 + 1 - u))

        @block.gpsimd
        def _(pool):
            def head(c, i, u, warm):
                wait(pool, idx_in[u], 16 * (i + 1))
                if warm:
                    wait(pool, scaled, c - 1)
                for q in range(Q):
                    pool.indirect_dma_start(gs[:, u, q, :], None, xa,
                                            bass.IndirectOffsetOnAxis(idx[:, u, q:q + 1], 0))\
                        .then_inc(gs_in[u], 16)
                if warm:
                    wait(pool, summed_e, c - 1)
                for q in range(Q):
                    pool.indirect_dma_start(gd[:, u, q, :], None, xa,
                                            bass.IndirectOffsetOnAxis(idx[:, u, Q + q:Q + q + 1], 0))\
                        .then_inc(gd_in[u], 16)
            chunks(pool, (head, 0))

        @block.vector
        def _(dve):
            dve.memset(S[:, 1, CH - 1:CH], 0.0)
            dve.memset(xnT[D:D + 1, :], 1.0).then_inc(ready, 1)
            dve.wait_ge(weights, 80)

            def head(c, i, u, warm):
                dve.wait_ge(gs_in[u], 128 * (i + 1))
                if warm:
                    dve.wait_ge(turned, c - 1)
                    dve.wait_ge(stored[u], 48 * i)
                dve.tensor_copy(row_out[:, u, :], gs[:, u, :, POS])
                dve.tensor_tensor(y[:, u, :, :], gs[:, u, :, 0:D],
                                  gs[:, u, :, INV_OUT:INV_OUT + 1].to_broadcast([128, Q, D]),
                                  ALU.mult).then_inc(scaled, 1)

            def tail(c, i, u, warm):
                dve.wait_ge(turned, c + 1)
                if warm:
                    dve.wait_ge(multiplied, c - 1)
                dve.tensor_tensor_scan(S[:, u, :], span(mask, c, CH), psT[0:D, :],
                                       S[:, 1 - u, CH - 1:CH], ALU.mult, ALU.add).then_inc(scanned, 1)
                dve.wait_ge(xn_in[u], 16 * (i + 1))
                dve.tensor_tensor(hn[:, :, :], xn[:, u, :, :],
                                  b0r[:, :].unsqueeze(1).to_broadcast([128, Q, D]), ALU.add)\
                   .then_inc(summed_n, 1)
                dve.wait_ge(gd_in[u], 128 * (i + 1))
                dve.wait_ge(multiplied, c + 1)
                for q in range(Q):
                    dve.scalar_tensor_tensor(he[:, q, :], A[:, q, 0:D], gd[:, u, q, INV_IN:INV_IN + 1],
                                             gd[:, u, q, 0:D], ALU.mult, ALU.add)
                dve.drain()
                dve.tensor_tensor(he[:, :, :], he[:, :, :],
                                  b0r[:, :].unsqueeze(1).to_broadcast([128, Q, D]), ALU.add)\
                   .then_inc(summed_e, 1)
                dve.drain()
                tiles = [hn[:, q, :] for q in range(Q)] + [he[:, q, :] for q in range(Q)]
                norm_stats(dve, tiles, st, mv, measured)
                if warm:
                    dve.wait_ge(stored[u], 48 * i)
                    dve.wait_ge(turned_n, c - 1)
                dve.wait_ge(rooted, c + 1)
                dve.reciprocal(rstd[:, :], rstd[:, :])
                dve.drain()
                for k in range(2 * Q):
                    to = xn_out[:, u, k, :] if k < Q else xe_out[:, u, k - Q, :]
                    last = dve.tensor_scalar(to, tiles[k], mv[:, k, 0:1], rstd[:, k:k + 1],
                                             ALU.subtract, ALU.mult)
                    if k == Q - 1:
                        last.then_inc(normed_n, 1)
                last.then_inc(normed_e, 1)
                dve.drain()

            def leaky(c, i, u, warm):
                dve.wait_ge(small_n, c + 1)
                if warm:
                    dve.wait_ge(stored_n[u], 16 * i)
                dve.tensor_tensor(cn_out[:, u, :, :], N[:, :, 0:D], cn_small[:, :, :], ALU.max)\
                   .then_inc(conv_n, 1)
            chunks(dve, (leaky, 2), (tail, 1), (head, 0))

        @block.scalar
        def _(act):
            act.wait_ge(ready, 1)

            def tail(c, i, u, warm):
                act.wait_ge(measured, c + 1)
                act.activation(rstd[:, :], mv[:, :, 1], ACT.Sqrt, bias=eps[:, :]).then_inc(rooted, 1)

            def last(c, i, u, warm):
                act.wait_ge(turned_n, c + 1)
                if warm or c == 1:
                    act.wait_ge(rooted_n, c)
                act.activation(xnT[0:D, :], psX[0:D, :], ACT.Copy).then_inc(copied_n, 1)
                if warm or c == 1:
                    act.wait_ge(conv_n, c)
                act.wait_ge(rooted_n, c + 1)
                act.activation(cn_small[:, :, :], N[:, :, 0:D], ACT.Copy, scale=LEAK)\
                   .then_inc(small_n, 1)
            chunks(act, (last, 2), (tail, 1))

        @block.tensor
        def _(pe):
            pe.wait_ge(weights, 80)

            def head(c, i, u, warm):
                pe.wait_ge(scaled, c + 1)
                if warm or c == 1:
                    pe.wait_ge(scanned, c)
                turn(pe, psT, y[:, u, :, :], ident, True).then_inc(turned, 1)

            def tail(c, i, u, warm):
                pe.wait_ge(scanned, c + 1)
                if warm or c == 1:
                    pe.wait_ge(summed_e, c)
                for q in range(Q):
                    last = pe.matmul(A[:, q, 0:D], S[:, u, tile_columns(q)], w0[:, :], start=True, stop=True)
                last.then_inc(multiplied, 1)

            def root(c, i, u, warm):
                pe.wait_ge(normed_n, c + 1)
                if warm or c == 1:
                    pe.wait_ge(copied_n, c)
                turn(pe, psX, xn_out[:, u, :, :], ident, False).then_inc(turned_n, 1)
                pe.wait_ge(copied_n, c + 1)
                if warm or c == 1:
                    pe.wait_ge(conv_n, c)
                for q in range(Q):
                    last = pe.matmul(N[:, q, 0:D], xnT[:, q * 128:(q + 1) * 128], wr[:, :],
                                     start=True, stop=True)
                last.then_inc(rooted_n, 1)
            chunks(pe, (root, 2), (tail, 1), (head, 0))
        ctx.close()
        clear(nc, used)


def layer1(nc, name, table, own, to, src_rows, edge_t, Wm, We, Wr, b, mask, ident, eps, node):
    first = name == "a"
    n_rows, n_res, n_to, Wn, bn = node
    LOADS = 4
    ctx = ExitStack()
    with ctx:
        def sb(tag, shape, dt=F32):
            return ctx.enter_context(nc.sbuf_tensor(f"l1{name}_{tag}", shape, dt))

        def ps(tag):
            return ctx.enter_context(nc.psum_tensor(f"l1{name}_{tag}", [128, 2 * 512], F32))

        def sem(tag):
            return ctx.enter_context(nc.semaphore(f"l1{name}_{tag}"))

        wm = sb("wm", [D, D])
        we = sb("we", [DE, D])
        wr = sb("wr", [D + 1, D])
        wn = sb("wn", [D + 1, D])
        idx = sb("idx", [128, 2, Q], I32)
        G = sb("G", [128, 2, Q, D])
        xs = sb("xs", [128, 2, Q, D])
        res = sb("res", [128, 2, Q, D])
        xn = sb("xn", [128, 2, Q, D])
        et = sb("et", [DE, 2, CH])
        gT = sb("gT", [D, CH])
        xT = sb("xT", [D + 1, 2, CH])
        nT = sb("nT", [D + 1, CH])
        restart = sb("restart", [D, CH], BF16)
        S = sb("S", [D, 2, CH])
        small_e = sb("small_e", [128, Q, D])
        small_n = sb("small_n", [128, Q, D])
        he = sb("he", [128, Q, D])
        hn = sb("hn", [128, Q, D])
        e_out = sb("e_out", [128, 2, Q, D])
        n_out = sb("n_out", [128, 2, Q, D])
        NT = Q if first else 2 * Q
        st = sb("st", [128, NT, 6])
        mv = sb("mv", [128, NT, 2])
        rstd = sb("rstd", [128, NT])
        psT, psA, psX, psN = ps("psT"), ps("psA"), ps("psX"), ps("psN")
        A = psA[:, :].rearrange("p (q d) -> p q d", q=Q)
        N = psN[:, :].rearrange("p (q d) -> p q d", q=Q)

        weights = sem("weights")
        ready = sem("ready")
        idx_in = [sem("idx_in0"), sem("idx_in1")]
        rows_in = [sem("rows_in0"), sem("rows_in1")]
        gathered = [sem("gathered0"), sem("gathered1")]
        stored = [sem("stored0"), sem("stored1")]
        turned = sem("turned")
        turned_x = sem("turned_x")
        turned_n = sem("turned_n")
        copied = sem("copied")
        copied_x = sem("copied_x")
        copied_n = sem("copied_n")
        messages = sem("messages")
        rooted_n = sem("rooted_n")
        scanned = sem("scanned")
        multiplied = sem("multiplied")
        scaled_e = sem("scaled_e")
        scaled_n = sem("scaled_n")
        leaked = sem("leaked")
        noded = sem("noded")
        summed = sem("summed")
        measured = sem("measured")
        rooted = sem("rooted")
        normed = sem("normed")
        block = ctx.enter_context(nc.Block())

        @block.sync
        def _(sp):
            for t, w in ((wm[:, :], Wm), (we[:, :], We), (wr[0:D, :], Wr), (wr[D:D + 1, :], b),
                         (wn[0:D, :], Wn), (wn[D:D + 1, :], bn)):
                sp.dma_start(t, w).then_inc(weights, 16)

            def head(c, i, u, warm):
                if warm:
                    wait(sp, gathered[u], 128 * i)
                sp.dma_start(idx[:, u, :], one(src_rows, c)).then_inc(idx_in[u], 16)
                if warm:
                    wait(sp, summed, c - 1)
                sp.dma_start(halves(xs[:, u, :, :]), rows_of(own if first else table, c))\
                  .then_inc(rows_in[u], 16)
                sp.dma_start(et[:, u, :], span(edge_t, c, CH)).then_inc(rows_in[u], 16)
                sp.dma_start(halves(xn[:, u, :, :]), rows_of(n_rows, c, EP)).then_inc(rows_in[u], 16)
                sp.dma_start(halves(res[:, u, :, :]), rows_of(n_res, c, EP) if first else rows_of(own, c))\
                  .then_inc(rows_in[u], 16)

            def tail(c, i, u, warm):
                if first:
                    wait(sp, leaked, c + 1)
                wait(sp, normed, c + 1)
                sp.dma_start(rows_of(to, c), halves(e_out[:, u, :, :])).then_inc(stored[u], 16)
                sp.dma_start(rows_of(n_to, c, EP), halves(n_out[:, u, :, :])).then_inc(stored[u], 16)
            chunks(sp, (head, 0), (tail, 2))
            for u in range(2):
                sp.wait_ge(stored[u], 32 * (NCH // 2 + 1 - u))

        @block.gpsimd
        def _(pool):
            def head(c, i, u, warm):
                wait(pool, idx_in[u], 16 * (i + 1))
                if warm:
                    wait(pool, turned, c - 1)
                gather(pool, G, u, table, idx, gathered)
            chunks(pool, (head, 0))

        @block.vector
        def _(dve):
            dve.memset(S[:, 1, CH - 1:CH], 0.0)
            dve.memset(nT[D:D + 1, :], 1.0)
            dve.memset(xT[D:D + 1, :, :], 1.0).then_inc(ready, 1)

            def head(c, i, u, warm):
                dve.tensor_scalar(restart[:, :], span(mask, c, CH), -1.0, BIG, ALU.add, ALU.mult)
                dve.drain()
                if warm:
                    dve.wait_ge(multiplied, c - 1)
                dve.wait_ge(messages, c + 1)
                dve.tensor_tensor_scan(S[:, u, :], restart[:, :], psT[0:D, :], S[:, 1 - u, CH - 1:CH],
                                       ALU.add, ALU.max).then_inc(scanned, 1)

            def tail(c, i, u, warm):
                if warm:
                    dve.wait_ge(stored[u], 32 * i)
                dve.wait_ge(rows_in[u], 16 * LOADS * (i + 1))
                if first:
                    dve.wait_ge(scaled_n, c + 1)
                    dve.tensor_tensor(hn[:, :, :], N[:, :, 0:D], small_n[:, :, :], ALU.max)\
                       .then_inc(noded, 1)
                    dve.drain()
                    dve.tensor_tensor(hn[:, :, :], hn[:, :, :], res[:, u, :, :], ALU.add)\
                       .then_inc(summed, 1)
                else:
                    dve.wait_ge(rooted_n, c + 1)
                    dve.tensor_tensor(hn[:, :, :], N[:, :, 0:D], xn[:, u, :, :], ALU.add)\
                       .then_inc(noded, 1)
                dve.wait_ge(scaled_e, c + 1)
                dve.tensor_tensor(e_out[:, u, :, :] if first else he[:, :, :], A[:, :, 0:D],
                                  small_e[:, :, :], ALU.max).then_inc(leaked, 1)
                dve.drain()
                if not first:
                    dve.tensor_tensor(he[:, :, :], he[:, :, :], res[:, u, :, :], ALU.add)\
                       .then_inc(summed, 1)
                    dve.drain()
                tiles = [hn[:, q, :] for q in range(Q)]
                outs = [n_out[:, u, q, :] for q in range(Q)]
                if not first:
                    tiles += [he[:, q, :] for q in range(Q)]
                    outs += [e_out[:, u, q, :] for q in range(Q)]
                norm_stats(dve, tiles, st, mv, measured)
                dve.wait_ge(rooted, c + 1)
                norm_apply(dve, tiles, outs, mv, rstd).then_inc(normed, 1)
                dve.drain()
            chunks(dve, (tail, 1), (head, 0))

        @block.scalar
        def _(act):
            act.wait_ge(ready, 1)

            def head(c, i, u, warm):
                act.wait_ge(turned, c + 1)
                if warm or c == 1:
                    act.wait_ge(messages, c)
                act.activation(gT[:, :], psT[0:D, :], ACT.Copy).then_inc(copied, 1)
                act.wait_ge(turned_x, c + 1)
                if warm:
                    act.wait_ge(multiplied, c - 1)
                act.activation(xT[0:D, u, :], psX[0:D, :], ACT.Copy).then_inc(copied_x, 1)
                act.wait_ge(turned_n, c + 1)
                if warm or c == 1:
                    act.wait_ge(rooted_n, c)
                act.activation(nT[0:D, :], psN[0:D, :], ACT.Copy).then_inc(copied_n, 1)
                if first:
                    act.wait_ge(rooted_n, c + 1)
                    if warm or c == 1:
                        act.wait_ge(noded, c)
                    act.activation(small_n[:, :, :], N[:, :, 0:D], ACT.Copy, scale=LEAK)\
                       .then_inc(scaled_n, 1)

            def tail(c, i, u, warm):
                act.wait_ge(multiplied, c + 1)
                if warm or c == 1:
                    act.wait_ge(leaked, c)
                act.activation(small_e[:, :, :], A[:, :, 0:D], ACT.Copy, scale=LEAK).then_inc(scaled_e, 1)
                act.wait_ge(measured, c + 1)
                act.activation(rstd[:, :], mv[:, :, 1], ACT.Sqrt, bias=eps[:, :]).then_inc(rooted, 1)
            chunks(act, (tail, 1), (head, 0))

        @block.tensor
        def _(pe):
            pe.wait_ge(weights, 96)

            def head(c, i, u, warm):
                pe.wait_ge(gathered[u], 128 * (i + 1))
                if warm or c == 1:
                    pe.wait_ge(scanned, c)
                turn(pe, psT, G[:, u, :, :], ident, True).then_inc(turned, 1)
                pe.wait_ge(rows_in[u], 16 * LOADS * (i + 1))
                if warm or c == 1:
                    pe.wait_ge(copied_x, c)
                turn(pe, psX, xs[:, u, :, :], ident, False).then_inc(turned_x, 1)
                pe.wait_ge(copied, c + 1)
                for h in range(2):
                    part = slice(h * 512, h * 512 + 512)
                    pe.matmul(psT[0:D, part], wm[:, :], gT[:, part], start=True, stop=False)
                    last = pe.matmul(psT[0:D, part], we[:, :], et[:, u, part], start=False, stop=True)
                last.then_inc(messages, 1)
                if warm or c == 1:
                    pe.wait_ge(noded, c)
                turn(pe, psN, xn[:, u, :, :], ident, False).then_inc(turned_n, 1)
                pe.wait_ge(copied_n, c + 1)
                for q in range(Q):
                    last = pe.matmul(N[:, q, 0:D], nT[:, q * 128:(q + 1) * 128], wn[:, :],
                                     start=True, stop=True)
                last.then_inc(rooted_n, 1)

            def tail(c, i, u, warm):
                pe.wait_ge(scanned, c + 1)
                pe.wait_ge(copied_x, c + 1)
                if warm or c == 1:
                    pe.wait_ge(leaked, c)
                for q in range(Q):
                    pe.matmul(A[:, q, 0:D], S[:, u, tile_columns(q)], ident[0:D, 0:D],
                              start=True, stop=False)
                    last = pe.matmul(A[:, q, 0:D], xT[:, u, q * 128:(q + 1) * 128], wr[:, :],
                                     start=False, stop=True)
                last.then_inc(multiplied, 1)
            chunks(pe, (tail, 1), (head, 0))


def running_softmax(dve, mask_c, restart, values, R, dd, u, differed):
    dve.tensor_scalar(restart[:, :], mask_c, -1.0, BIG, ALU.add, ALU.mult)
    dve.tensor_copy(R[:, u, 0:1], R[:, 1 - u, CH:CH + 1])
    dve.drain()
    dve.tensor_tensor_scan(R[:, u, 1:CH + 1], restart[:, :], values, R[:, u, 0:1], ALU.add, ALU.max)
    dve.drain()
    dve.tensor_tensor(dd[:, 0, :], R[:, u, 0:CH], restart[:, :], ALU.add)
    dve.tensor_tensor(dd[:, 1, :], values, R[:, u, 1:CH + 1], ALU.subtract)
    dve.drain()
    dve.tensor_tensor(dd[:, 0, :], dd[:, 0, :], R[:, u, 1:CH + 1], ALU.subtract).then_inc(differed, 1)


def running_sums(dve, P, values, S, T, u, mixed):
    dve.tensor_tensor_scan(S[:, u, :], P[:, u, 0, :], P[:, u, 1, :], S[:, 1 - u, CH - 1:CH],
                           ALU.mult, ALU.add)
    dve.drain()
    dve.tensor_tensor(P[:, u, 1, :], P[:, u, 1, :], values, ALU.mult)
    dve.drain()
    dve.tensor_tensor_scan(T[:, u, :], P[:, u, 0, :], P[:, u, 1, :], T[:, 1 - u, CH - 1:CH],
                           ALU.mult, ALU.add).then_inc(mixed, 1)


def layer2(nc, t2, t3, src_rows, ad_d, Wg, bg, Wa, att_d, mask_d, ident, eps, node):
    n_rows, n_to, Wn, bn = node
    LOADS = 2
    ctx = ExitStack()
    with ctx:
        def sb(tag, shape, dt=F32):
            return ctx.enter_context(nc.sbuf_tensor(f"l2_{tag}", shape, dt))

        def ps(tag):
            return ctx.enter_context(nc.psum_tensor(f"l2_{tag}", [128, 2 * 512], F32))

        def sem(tag):
            return ctx.enter_context(nc.semaphore(f"l2_{tag}"))

        wg = sb("wg", [D + 1, D])
        wn = sb("wn", [D + 1, D])
        ad = sb("ad", [D, 1])
        ad_wide = sb("ad_wide", [D, 128])
        wnT = sb("wnT", [D, D])
        wd = sb("wd", [128, D])
        eps_col = sb("eps_col", [D, D + 1])
        idx = sb("idx", [128, 2, Q], I32)
        G = sb("G", [128, 2, Q, D])
        mask = sb("mask", [D, 2, CH], BF16)
        xs = sb("xs", [128, 2, Q, D])
        xn = sb("xn", [128, 2, Q, D])
        m = sb("m", [D, 2, CH])
        restart = sb("restart", [D, CH], BF16)
        R = sb("R", [D, 2, CH + 1])
        dd = sb("dd", [D, 2, CH])
        P = sb("P", [D, 2, 2, CH])
        S = sb("S", [D, 2, CH])
        T = sb("T", [D, 2, CH])
        inv = sb("inv", [D, 2, CH])
        xT = sb("xT", [D + 1, CH])
        nT = sb("nT", [D + 1, CH])
        e_out = sb("e_out", [128, 2, Q, D])
        n_out = sb("n_out", [128, 2, Q, D])
        weighted = sb("weighted", [128, Q, D])
        ad_out = sb("ad_out", [128, 2, Q])
        st = sb("st", [128, 2 * Q, 6])
        mv = sb("mv", [128, 2 * Q, 2])
        rstd = sb("rstd", [128, 2 * Q])
        psT, psA, psX, psN = ps("psT"), ps("psA"), ps("psX"), ps("psN")
        A = psA[:, :].rearrange("p (q d) -> p q d", q=Q)
        N = psN[:, :].rearrange("p (q d) -> p q d", q=Q)

        weights = sem("weights")
        ready = sem("ready")
        set_up = sem("set_up")
        widened = sem("widened")
        idx_in = [sem("idx_in0"), sem("idx_in1")]
        mask_in = [sem("mask_in0"), sem("mask_in1")]
        rows_in = [sem("rows_in0"), sem("rows_in1")]
        gathered = [sem("gathered0"), sem("gathered1")]
        stored = [sem("stored0"), sem("stored1")]
        turned = sem("turned")
        rectified = sem("rectified")
        differed = sem("differed")
        exped = sem("exped")
        mixed = sem("mixed")
        inverted = sem("inverted")
        averaged = sem("averaged")
        turned_x = sem("turned_x")
        turned_n = sem("turned_n")
        copied_x = sem("copied_x")
        copied_n = sem("copied_n")
        rooted_n = sem("rooted_n")
        tanhed = sem("tanhed")
        multiplied = sem("multiplied")
        summed = sem("summed")
        measured = sem("measured")
        rooted = sem("rooted")
        normed = sem("normed")
        block = ctx.enter_context(nc.Block())

        @block.sync
        def _(sp):
            for t, w in ((wg[0:D, :], Wg), (wg[D:D + 1, :], bg), (wn[0:D, :], Wn), (wn[D:D + 1, :], bn),
                         (ad[:, :], att_d)):
                sp.dma_start(t, w).then_inc(weights, 16)

            def head(c, i, u, warm):
                if warm:
                    wait(sp, gathered[u], 128 * i)
                sp.dma_start(idx[:, u, :], one(src_rows, c)).then_inc(idx_in[u], 16)
                if warm:
                    wait(sp, differed, c - 1)
                sp.dma_start(mask[:, u, :], span(mask_d, c, CH).to_broadcast([D, CH]))\
                  .then_inc(mask_in[u], 16)

            def rows(c, i, u, warm):
                if warm:
                    wait(sp, summed, c - 1)
                sp.dma_start(halves(xs[:, u, :, :]), rows_of(t2, c)).then_inc(rows_in[u], 16)
                sp.dma_start(halves(xn[:, u, :, :]), rows_of(n_rows, c, EP)).then_inc(rows_in[u], 16)

            def tail(c, i, u, warm):
                wait(sp, normed, c + 1)
                sp.dma_start(rows_of(t3, c), halves(e_out[:, u, :, :])).then_inc(stored[u], 16)
                sp.dma_start(rows_of(n_to, c), halves(n_out[:, u, :, :])).then_inc(stored[u], 16)
                sp.dma_start(scalars_of(ad_d, c), ad_out[:, u, :].rearrange("p (a r) -> p a r", a=2))\
                  .then_inc(stored[u], 16)
            chunks(sp, (head, 0), (rows, 1), (tail, 3))
            for u in range(2):
                sp.wait_ge(stored[u], 48 * (NCH // 2 + 1 - u))

        @block.gpsimd
        def _(pool):
            def head(c, i, u, warm):
                wait(pool, idx_in[u], 16 * (i + 1))
                if warm:
                    wait(pool, turned, c - 1)
                gather(pool, G, u, t2, idx, gathered)

            def average(c, i, u, warm):
                wait(pool, inverted, c + 1)
                pool.tensor_tensor(inv[:, u, :], T[:, u, :], inv[:, u, :], ALU.mult).then_inc(averaged, 1)
            chunks(pool, (head, 0), (average, 2))

        @block.vector
        def _(dve):
            dve.memset(R[:, 1, CH:CH + 1], 0.0)
            dve.memset(S[:, 1, CH - 1:CH], 0.0)
            dve.memset(T[:, 1, CH - 1:CH], 0.0)
            dve.memset(eps_col[:, 0:D], 0.0)
            dve.memset(eps_col[:, D:D + 1], MSG_EPS)
            dve.memset(xT[D:D + 1, :], 1.0)
            dve.memset(nT[D:D + 1, :], 1.0)
            dve.wait_ge(weights, 80)
            dve.tensor_copy(ad_wide[:, :], ad[:, 0:1].to_broadcast([D, 128])).then_inc(ready, 1)
            dve.wait_ge(set_up, 1)
            dve.tensor_tensor(wg[D:D + 1, :], wg[D:D + 1, :], psA[D:D + 1, 0:D], ALU.add)
            dve.tensor_copy(wnT[:, :], psX[0:D, 0:D]).then_inc(widened, 1)
            dve.wait_ge(set_up, 2)
            dve.tensor_copy(wd[:, :], psN[:, 0:D]).then_inc(widened, 1)
            dve.drain()

            def head(c, i, u, warm):
                dve.wait_ge(mask_in[u], 16 * (i + 1))
                dve.wait_ge(rectified, c + 1)
                if warm or c == 1:
                    dve.wait_ge(exped, c)
                running_softmax(dve, mask[:, u, :], restart, m[:, u, :], R, dd, u, differed)

            def sums(c, i, u, warm):
                dve.wait_ge(exped, c + 1)
                if warm:
                    dve.wait_ge(averaged, c - 1)
                    dve.wait_ge(inverted, c - 1)
                running_sums(dve, P, m[:, u, :], S, T, u, mixed)

            def tail(c, i, u, warm):
                dve.wait_ge(rows_in[u], 16 * LOADS * (i + 1))
                dve.wait_ge(tanhed, c + 1)
                dve.tensor_tensor(n_out[:, u, :, :], n_out[:, u, :, :], xn[:, u, :, :], ALU.add)
                if warm:
                    dve.wait_ge(stored[u], 48 * i)
                dve.wait_ge(multiplied, c + 1)
                dve.tensor_tensor(e_out[:, u, :, :], A[:, :, 0:D], xs[:, u, :, :], ALU.add)\
                   .then_inc(summed, 1)
                dve.drain()
                tiles = [n_out[:, u, q, :] for q in range(Q)] + [e_out[:, u, q, :] for q in range(Q)]
                norm_stats(dve, tiles, st, mv, measured)
                dve.wait_ge(rooted, c + 1)
                norm_apply(dve, tiles, tiles, mv, rstd)
                dve.drain()
                dve.tensor_tensor(weighted[:, :, :], e_out[:, u, :, :],
                                  wd[:, :].unsqueeze(1).to_broadcast([128, Q, D]), ALU.mult)
                dve.drain()
                dve.tensor_reduce(ad_out[:, u, :], weighted[:, :, :], mybir.AxisListType.X, ALU.add)\
                   .then_inc(normed, 1)
                dve.drain()
            chunks(dve, (head, 0), (sums, 1), (tail, 2))

        @block.scalar
        def _(act):
            act.wait_ge(ready, 1)

            def rectify(c, i, u, warm):
                act.wait_ge(turned, c + 1)
                if warm:
                    act.wait_ge(mixed, c - 1)
                act.activation(m[:, u, :], psT[0:D, :], ACT.Relu).then_inc(rectified, 1)

            def own(c, i, u, warm):
                act.wait_ge(turned_x, c + 1)
                if warm or c == 1:
                    act.wait_ge(multiplied, c)
                act.activation(xT[0:D, :], psX[0:D, :], ACT.Copy).then_inc(copied_x, 1)
                act.wait_ge(turned_n, c + 1)
                if warm or c == 1:
                    act.wait_ge(rooted_n, c)
                act.activation(nT[0:D, :], psN[0:D, :], ACT.Copy).then_inc(copied_n, 1)
                act.wait_ge(rooted_n, c + 1)
                if warm:
                    act.wait_ge(stored[u], 48 * i)
                act.activation(n_out[:, u, :, :], N[:, :, 0:D], ACT.Tanh).then_inc(tanhed, 1)

            def exps(c, i, u, warm):
                act.wait_ge(differed, c + 1)
                if warm:
                    act.wait_ge(mixed, c - 1)
                act.activation(P[:, u, :, :], dd[:, :, :], ACT.Exp).then_inc(exped, 1)

            def invert(c, i, u, warm):
                act.wait_ge(mixed, c + 1)
                if warm:
                    act.wait_ge(multiplied, c - 1)
                act.activation(inv[:, u, :], S[:, u, :], ACT.Ln)
                act.drain()
                act.activation(inv[:, u, :], inv[:, u, :], ACT.Exp, scale=-1.0).then_inc(inverted, 1)

            def root(c, i, u, warm):
                act.wait_ge(measured, c + 1)
                act.activation(rstd[:, :], mv[:, :, 1], ACT.Sqrt, bias=eps[:, :]).then_inc(rooted, 1)
            chunks(act, (rectify, 0), (own, 2), (exps, 0), (invert, 1), (root, 2))

        @block.tensor
        def _(pe):
            pe.wait_ge(weights, 80)
            pe.wait_ge(ready, 1)
            pe.matmul(psA[0:D + 1, 0:D], eps_col[:, :], wg[0:D, :], start=True, stop=True)
            pe.transpose(psX[0:D, 0:D], wn[0:D, :], ident[0:D, 0:D]).then_inc(set_up, 1)
            pe.wait_ge(widened, 1)
            pe.matmul(psN[:, 0:D], ad_wide[:, :], wnT[:, :], start=True, stop=True).then_inc(set_up, 1)
            pe.wait_ge(widened, 2)

            def head(c, i, u, warm):
                pe.wait_ge(gathered[u], 128 * (i + 1))
                if warm or c == 1:
                    pe.wait_ge(rectified, c)
                turn(pe, psT, G[:, u, :, :], ident, True).then_inc(turned, 1)

            def tail(c, i, u, warm):
                pe.wait_ge(rows_in[u], 16 * LOADS * (i + 1))
                if warm or c == 1:
                    pe.wait_ge(copied_x, c)
                turn(pe, psX, xs[:, u, :, :], ident, False).then_inc(turned_x, 1)
                if warm or c == 1:
                    pe.wait_ge(tanhed, c)
                turn(pe, psN, xn[:, u, :, :], ident, False).then_inc(turned_n, 1)
                pe.wait_ge(copied_n, c + 1)
                for q in range(Q):
                    last = pe.matmul(N[:, q, 0:D], nT[:, q * 128:(q + 1) * 128], wn[:, :],
                                     start=True, stop=True)
                last.then_inc(rooted_n, 1)
                pe.wait_ge(averaged, c + 1)
                pe.wait_ge(copied_x, c + 1)
                if warm or c == 1:
                    pe.wait_ge(summed, c)
                for q in range(Q):
                    pe.matmul(A[:, q, 0:D], inv[:, u, tile_columns(q)], wg[0:D, :], start=True, stop=False)
                    last = pe.matmul(A[:, q, 0:D], xT[:, q * 128:(q + 1) * 128], wg[:, :],
                                     start=False, stop=True)
                last.then_inc(multiplied, 1)
            chunks(pe, (head, 0), (tail, 2))


def spread(nc, ad_d, next_d, ads_d, ident):
    ctx = ExitStack()
    with ctx:
        def sb(tag, shape, dt=F32):
            return ctx.enter_context(nc.sbuf_tensor(f"sp_{tag}", shape, dt))

        def sem(tag):
            return ctx.enter_context(nc.semaphore(f"sp_{tag}"))

        a = sb("a", [128, J])
        nxt = sb("nxt", [128, J])
        only = sb("only", [128, J])
        ones = sb("ones", [128, J])
        keep = sb("keep", [128, J])
        found = sb("found", [128, J])
        rows = sb("rows", [1, 2, 128])
        carry = sb("carry", [1, 129])
        res = sb("res", [128, J])
        carried = sb("carried", [128, 1])
        ps = ctx.enter_context(nc.psum_tensor("sp_ps", [128, 512], F32))
        filled = sem("filled")
        loaded = sem("loaded")
        scanned = sem("scanned")
        turned = sem("turned")
        chained = sem("chained")
        returned = sem("returned")
        copied = sem("copied")
        done = sem("done")
        stored = sem("stored")
        block = ctx.enter_context(nc.Block())

        @block.sync
        def _(sp):
            sp.dma_start(a[:, :], ad_d.rearrange("a (p j) -> (a p) j", p=128)).then_inc(loaded, 16)
            sp.dma_start(nxt[:, :], next_d.rearrange("a (p j) -> (a p) j", p=128)).then_inc(loaded, 16)
            sp.wait_ge(done, 1)
            sp.dma_start(ads_d.rearrange("a (p j) -> (a p) j", p=128), res[:, :]).then_inc(stored, 16)
            sp.wait_ge(stored, 16)

        @block.vector
        def _(dve):
            dve.wait_ge(filled, 2)
            dve.wait_ge(loaded, 32)
            dve.tensor_tensor(only[:, :], nxt[:, :], a[:, :], ALU.mult)
            dve.drain()
            dve.tensor_tensor(only[:, :], a[:, :], only[:, :], ALU.subtract)
            dve.tensor_tensor_scan(keep[:, ::-1], nxt[:, ::-1], ones[:, ::-1], 1.0, ALU.mult, ALU.mult)
            dve.drain()
            dve.tensor_tensor_scan(found[:, ::-1], nxt[:, ::-1], only[:, ::-1], 0.0, ALU.mult, ALU.add)\
               .then_inc(scanned, 1)
            dve.wait_ge(turned, 1)
            dve.tensor_copy(rows[:, :, :], ps[0:1, 0:256].rearrange("p (a m) -> p a m", a=2))
            dve.drain()
            dve.tensor_tensor_scan(carry[:, 127::-1], rows[:, 0, ::-1], rows[:, 1, ::-1], 0.0,
                                   ALU.mult, ALU.add).then_inc(chained, 1)
            dve.wait_ge(copied, 1)
            dve.scalar_tensor_tensor(res[:, :], keep[:, :], carried[:, 0:1], found[:, :],
                                     ALU.mult, ALU.add).then_inc(done, 1)

        @block.scalar
        def _(act):
            act.wait_ge(returned, 1)
            act.activation(carried[:, :], ps[:, 256:257], ACT.Copy).then_inc(copied, 1)

        @block.gpsimd
        def _(pool):
            pool.memset(ones[:, :], 1.0).then_inc(filled, 1)
            pool.memset(carry[:, :], 0.0).then_inc(filled, 1)

        @block.tensor
        def _(pe):
            pe.wait_ge(scanned, 1)
            pe.transpose(ps[0:1, 0:128], keep[:, 0:1], ident[:, :])
            pe.transpose(ps[0:1, 128:256], found[:, 0:1], ident[:, :]).then_inc(turned, 1)
            pe.wait_ge(chained, 1)
            pe.matmul(ps[:, 256:257], carry[:, 1:129], ident[0:1, 0:1], start=True, stop=True)\
              .then_inc(returned, 1)


def layer3(nc, t3, src_rows, scat_d, ads_d, mask_d, out, Wa, att_s, att_d, ba, ident, eps):
    LOADS = 2
    ctx = ExitStack()
    with ctx:
        def sb(tag, shape, dt=F32):
            return ctx.enter_context(nc.sbuf_tensor(f"l3_{tag}", shape, dt))

        def ps(tag):
            return ctx.enter_context(nc.psum_tensor(f"l3_{tag}", [128, 2 * 512], F32))

        def sem(tag):
            return ctx.enter_context(nc.semaphore(f"l3_{tag}"))

        wa = sb("wa", [D, D + 1])
        att = sb("att", [D, 2])
        att_wide = sb("att_wide", [D, D])
        waT = sb("waT", [D, D])
        ws_wide = sb("ws_wide", [D, D])
        bar = sb("bar", [128, D])
        ones = sb("ones", [1, D])
        idx = sb("idx", [128, 2, Q], I32)
        sidx = sb("sidx", [128, 2, Q], I32)
        G = sb("G", [128, 2, Q, D])
        mask = sb("mask", [D, 2, CH], BF16)
        ads = sb("ads", [1, 2, CH])
        xs = sb("xs", [128, 2, Q, D])
        gT = sb("gT", [D, 2, CH])
        small_z = sb("small_z", [D, CH])
        score = sb("score", [D, CH])
        restart = sb("restart", [D, CH], BF16)
        R = sb("R", [D, 2, CH + 1])
        R_row = sb("R_row", [1, 2, CH])
        dd = sb("dd", [D, 2, CH])
        P = sb("P", [D, 2, 2, CH])
        S = sb("S", [D, 2, CH])
        T = sb("T", [D, 2, CH])
        xT = sb("xT", [D, CH])
        small_s = sb("small_s", [128, Q])
        own = sb("own", [128, Q])
        top = sb("top", [128, Q])
        less = sb("less", [128, 2, Q])
        share = sb("share", [128, 2, Q])
        total = sb("total", [128, Q])
        e_out = sb("e_out", [128, 2, Q, D])
        st = sb("st", [128, Q, 6])
        mv = sb("mv", [128, Q, 2])
        rstd = sb("rstd", [128, Q])
        psT, psA, psX, psH = ps("psT"), ps("psA"), ps("psX"), ps("psH")
        A = psA[:, :].rearrange("p (q d) -> p q d", q=Q)
        Hp = psH[:, :].rearrange("p (q d) -> p q d", q=Q)

        weights = sem("weights")
        ready = sem("ready")
        set_up = sem("set_up")
        widened = sem("widened")
        idx_in = [sem("idx_in0"), sem("idx_in1")]
        mask_in = [sem("mask_in0"), sem("mask_in1")]
        rows_in = [sem("rows_in0"), sem("rows_in1")]
        gathered = [sem("gathered0"), sem("gathered1")]
        scattered = [sem("scattered0"), sem("scattered1")]
        turned = sem("turned")
        copied = sem("copied")
        scored = sem("scored")
        scaled_z = sem("scaled_z")
        leaked = sem("leaked")
        differed = sem("differed")
        exped = sem("exped")
        mixed = sem("mixed")
        turned_x = sem("turned_x")
        copied_x = sem("copied_x")
        own_ready = sem("own_ready")
        multiplied = sem("multiplied")
        scaled_s = sem("scaled_s")
        lessened = sem("lessened")
        shares = sem("shares")
        joined = sem("joined")
        biased = sem("biased")
        tanhed = sem("tanhed")
        summed = sem("summed")
        measured = sem("measured")
        rooted = sem("rooted")
        normed = sem("normed")
        block = ctx.enter_context(nc.Block())

        @block.sync
        def _(sp):
            for t, w in ((wa[:, 0:D], Wa), (att[:, 0:1], att_s), (att[:, 1:2], att_d),
                         (bar[:, :], ba.to_broadcast([128, D]))):
                sp.dma_start(t, w).then_inc(weights, 16)

            def head(c, i, u, warm):
                if warm:
                    wait(sp, gathered[u], 128 * i)
                sp.dma_start(idx[:, u, :], one(src_rows, c)).then_inc(idx_in[u], 16)
                if warm:
                    wait(sp, differed, c - 1)
                sp.dma_start(mask[:, u, :], span(mask_d, c, CH).to_broadcast([D, CH]))\
                  .then_inc(mask_in[u], 16)
                sp.dma_start(ads[:, u, :], span(ads_d, c, CH)).then_inc(mask_in[u], 16)

            def rows(c, i, u, warm):
                if warm:
                    wait(sp, scattered[u], 128 * i)
                sp.dma_start(halves(xs[:, u, :, :]), rows_of(t3, c)).then_inc(rows_in[u], 16)
                sp.dma_start(sidx[:, u, :].rearrange("p (a r) -> p a r", a=2), scalars_of(scat_d, c))\
                  .then_inc(rows_in[u], 16)
            chunks(sp, (head, 0), (rows, 1))

        @block.gpsimd
        def _(pool):
            def head(c, i, u, warm):
                wait(pool, idx_in[u], 16 * (i + 1))
                if warm:
                    wait(pool, turned, c - 1)
                gather(pool, G, u, t3, idx, gathered)

            def scatter(c, i, u, warm):
                wait(pool, rows_in[u], 16 * LOADS * (i + 1))
                wait(pool, normed, c + 1)
                for q in range(Q):
                    pool.indirect_dma_start(out, bass.IndirectOffsetOnAxis(sidx[:, u, q:q + 1], 0),
                                            e_out[:, u, q, :], None, bounds_check=NP - 1,
                                            oob_is_err=False).then_inc(scattered[u], 16)
            chunks(pool, (head, 0), (scatter, 3))
            for u in range(2):
                pool.wait_ge(scattered[u], 128 * (NCH // 2 + 1 - u))

        @block.vector
        def _(dve):
            dve.memset(R[:, 1, CH:CH + 1], 0.0)
            dve.memset(S[:, 1, CH - 1:CH], 0.0)
            dve.memset(T[:, 1, CH - 1:CH], 0.0)
            dve.memset(ones[:, :], 1.0)
            dve.wait_ge(weights, 64)
            dve.tensor_copy(att_wide[:, :], att[:, 0:1].to_broadcast([D, D])).then_inc(ready, 1)
            dve.wait_ge(set_up, 1)
            dve.tensor_copy(waT[:, :], psX[0:D, 0:D]).then_inc(widened, 1)
            dve.wait_ge(set_up, 2)
            dve.tensor_copy(ws_wide[:, :], psA[0:D, 0:D])
            dve.tensor_copy(wa[:, D:D + 1], psH[0:D, 0:1]).then_inc(widened, 1)

            def head(c, i, u, warm):
                dve.wait_ge(scaled_z, c + 1)
                dve.tensor_tensor(score[:, :], psT[0:D, :], small_z[:, :], ALU.max).then_inc(leaked, 1)
                dve.drain()
                dve.wait_ge(mask_in[u], 32 * (i + 1))
                if warm or c == 1:
                    dve.wait_ge(exped, c)
                running_softmax(dve, mask[:, u, :], restart, score[:, :], R, dd, u, differed)

            def sums(c, i, u, warm):
                dve.wait_ge(exped, c + 1)
                if warm:
                    dve.wait_ge(multiplied, c - 1)
                dve.tensor_copy(R_row[:, u, :], R[0:1, u, 1:CH + 1])
                running_sums(dve, P, gT[:, u, :], S, T, u, mixed)

            def tail(c, i, u, warm):
                dve.wait_ge(multiplied, c + 1)
                dve.wait_ge(scaled_s, c + 1)
                dve.tensor_tensor(own[:, :], Hp[:, :, D], small_s[:, :], ALU.max)
                dve.drain()
                dve.tensor_tensor(top[:, :], own[:, :], A[:, :, D + 1], ALU.max)
                dve.drain()
                dve.tensor_tensor(less[:, 0, :], A[:, :, D + 1], top[:, :], ALU.subtract)
                dve.tensor_tensor(less[:, 1, :], own[:, :], top[:, :], ALU.subtract).then_inc(lessened, 1)
                dve.wait_ge(shares, c + 1)
                dve.tensor_tensor(total[:, :], A[:, :, D], share[:, 0, :], ALU.mult)
                dve.drain()
                dve.scalar_tensor_tensor(total[:, :], total[:, :], 1e-16, share[:, 1, :], ALU.add, ALU.add)
                dve.drain()
                dve.reciprocal(total[:, :], total[:, :])
                dve.drain()
                dve.tensor_tensor(share[:, :, :], share[:, :, :],
                                  total[:, :].unsqueeze(1).to_broadcast([128, 2, Q]), ALU.mult)
                dve.drain()
                if warm:
                    dve.wait_ge(scattered[u], 128 * i)
                for q in range(Q):
                    dve.tensor_scalar(e_out[:, u, q, :], A[:, q, 0:D], share[:, 0, q:q + 1], None, ALU.mult)
                dve.drain()
                for q in range(Q):
                    last = dve.scalar_tensor_tensor(e_out[:, u, q, :], Hp[:, q, 0:D], share[:, 1, q:q + 1],
                                                    e_out[:, u, q, :], ALU.mult, ALU.add)
                last.then_inc(joined, 1)
                dve.drain()
                dve.tensor_tensor(e_out[:, u, :, :], e_out[:, u, :, :],
                                  bar[:, :].unsqueeze(1).to_broadcast([128, Q, D]), ALU.add)\
                   .then_inc(biased, 1)
                dve.drain()
                dve.wait_ge(tanhed, c + 1)
                dve.wait_ge(rows_in[u], 16 * LOADS * (i + 1))
                dve.tensor_tensor(e_out[:, u, :, :], e_out[:, u, :, :], xs[:, u, :, :], ALU.add)\
                   .then_inc(summed, 1)
                dve.drain()
                tiles = [e_out[:, u, q, :] for q in range(Q)]
                norm_stats(dve, tiles, st, mv, measured)
                dve.wait_ge(rooted, c + 1)
                norm_apply(dve, tiles, tiles, mv, rstd).then_inc(normed, 1)
                dve.drain()
            chunks(dve, (head, 0), (sums, 1), (tail, 2))

        @block.scalar
        def _(act):
            def copy(c, i, u, warm):
                act.wait_ge(turned, c + 1)
                if warm:
                    act.wait_ge(mixed, c - 1)
                act.activation(gT[:, u, :], psT[0:D, :], ACT.Copy).then_inc(copied, 1)
                act.wait_ge(scored, c + 1)
                if warm or c == 1:
                    act.wait_ge(leaked, c)
                act.activation(small_z[:, :], psT[0:D, :], ACT.Copy, scale=LEAK_ATT).then_inc(scaled_z, 1)

            def own_rows(c, i, u, warm):
                act.wait_ge(turned_x, c + 1)
                if warm or c == 1:
                    act.wait_ge(own_ready, c)
                act.activation(xT[:, :], psX[0:D, :], ACT.Copy).then_inc(copied_x, 1)
                act.wait_ge(own_ready, c + 1)
                if warm or c == 1:
                    act.wait_ge(lessened, c)
                act.activation(small_s[:, :], Hp[:, :, D], ACT.Copy, scale=LEAK_ATT).then_inc(scaled_s, 1)

            def exps(c, i, u, warm):
                act.wait_ge(differed, c + 1)
                if warm:
                    act.wait_ge(mixed, c - 1)
                act.activation(P[:, u, :, :], dd[:, :, :], ACT.Exp).then_inc(exped, 1)

            def tail(c, i, u, warm):
                act.wait_ge(lessened, c + 1)
                if warm or c == 1:
                    act.wait_ge(joined, c)
                act.activation(share[:, :, :], less[:, :, :], ACT.Exp).then_inc(shares, 1)
                act.wait_ge(biased, c + 1)
                act.activation(e_out[:, u, :, :], e_out[:, u, :, :], ACT.Tanh).then_inc(tanhed, 1)
                act.wait_ge(measured, c + 1)
                act.activation(rstd[:, :], mv[:, :, 1], ACT.Sqrt, bias=eps[:, :]).then_inc(rooted, 1)
            chunks(act, (copy, 0), (own_rows, 2), (exps, 0), (tail, 2))

        @block.tensor
        def _(pe):
            pe.wait_ge(weights, 64)
            pe.wait_ge(ready, 1)
            pe.transpose(psX[0:D, 0:D], wa[:, 0:D], ident[0:D, 0:D]).then_inc(set_up, 1)
            pe.wait_ge(widened, 1)
            pe.matmul(psA[0:D, 0:D], waT[:, :], att_wide[:, :], start=True, stop=True)
            pe.matmul(psH[0:D, 0:1], waT[:, :], att[:, 0:1], start=True, stop=False)
            pe.matmul(psH[0:D, 0:1], waT[:, :], att[:, 1:2], start=False, stop=True).then_inc(set_up, 1)
            pe.wait_ge(widened, 2)

            def head(c, i, u, warm):
                pe.wait_ge(gathered[u], 128 * (i + 1))
                if warm or c == 1:
                    pe.wait_ge(leaked, c)
                turn(pe, psT, G[:, u, :, :], ident, True).then_inc(turned, 1)
                pe.wait_ge(copied, c + 1)
                pe.wait_ge(mask_in[u], 32 * (i + 1))
                for h in range(2):
                    part = slice(h * 512, h * 512 + 512)
                    pe.matmul(psT[0:D, part], ws_wide[:, :], gT[:, u, part], start=True, stop=False)
                    last = pe.matmul(psT[0:D, part], ones[:, :], ads[:, u, part], start=False, stop=True)
                last.then_inc(scored, 1)

            def tail(c, i, u, warm):
                pe.wait_ge(rows_in[u], 16 * LOADS * (i + 1))
                if warm or c == 1:
                    pe.wait_ge(copied_x, c)
                turn(pe, psX, xs[:, u, :, :], ident, False).then_inc(turned_x, 1)
                pe.wait_ge(copied_x, c + 1)
                if warm or c == 1:
                    pe.wait_ge(joined, c)
                for q in range(Q):
                    last = pe.matmul(Hp[:, q, 0:D + 1], xT[:, q * 128:(q + 1) * 128], wa[:, :],
                                     start=True, stop=True)
                last.then_inc(own_ready, 1)
                pe.wait_ge(mixed, c + 1)
                for q in range(Q):
                    at = tile_columns(q)
                    pe.matmul(A[:, q, 0:D], T[:, u, at], wa[:, 0:D], start=True, stop=True)
                    pe.matmul(A[:, q, D:D + 1], S[0:1, u, at], ones[0:1, 0:1], start=True, stop=True)
                    last = pe.matmul(A[:, q, D + 1:D + 2], R_row[0:1, u, at], ones[0:1, 0:1],
                                     start=True, stop=True)
                last.then_inc(multiplied, 1)
            chunks(pe, (head, 0), (tail, 2))


def kernel(**inputs):
    import concourse.bacc as bacc
    from concourse.bass_utils import run_bass_kernel_spmd

    nc = bacc.Bacc("TRN2", target_bir_lowering=False, num_devices=1)
    arrays = {}

    def put(name, array):
        arrays[name] = np.ascontiguousarray(array)
        return nc.dram_tensor(name, arrays[name].shape, mybir.dt.from_np(arrays[name].dtype),
                              kind="ExternalInput").ap()

    src, dst = (np.concatenate([np.asarray(inputs[k]), np.full(EP - N_EDGES, N_NODES, np.int32)])
                for k in ("src", "dst"))
    x = np.concatenate([np.asarray(inputs["x"]), np.zeros((NP - N_NODES, D), np.float32)])
    ids = np.concatenate([a.reshape(NCH, 2, 128, H).transpose(0, 2, 1, 3).reshape(NCH, 128, Q)
                          for a in (src, dst)], axis=2)
    dst_ext = np.concatenate([np.full(1, -1, np.int32), dst, np.full(1, NP, np.int32)])
    attr = np.concatenate([np.asarray(inputs["edge_attr_32"]), np.zeros((EP - N_EDGES, DE), np.float32)])
    args = [put("x_pad", x), put("ids", ids), put("dst_ext", dst_ext), put("edge_t", attr.T)]
    for name in ("L0_gnn_W", "L0_gnn_b", "L1_gnn_W1_msg", "L1_gnn_W1_edge", "L1_gnn_W1_root", "L1_gnn_b1",
                 "L1_gnn_W2_msg", "L1_gnn_W2_edge", "L1_gnn_W2_root", "L1_gnn_b2", "L2_gnn_W", "L2_gnn_b",
                 "L3_gnn_W", "L3_gnn_att_src", "L3_gnn_att_dst", "L3_gnn_bias"):
        a = np.asarray(inputs[name])
        if a.ndim == 1:
            a = a.reshape((D, 1) if "att" in name else (1, D))
        args.append(put(name, a))
    out = nc.dram_tensor("out", (NP, D), F32, kind="ExternalOutput").ap()
    segment_kernel(nc, *args, out)
    run = run_bass_kernel_spmd(nc, [arrays], core_ids=[0])
    return run.results[0]["out"][:N_NODES]
```

```python
import numpy as np
import concourse.bass as bass
from concourse import mybir
from contextlib import ExitStack

F32 = mybir.dt.float32
I32 = mybir.dt.int32
BF16 = mybir.dt.bfloat16
F16 = mybir.dt.float16
ALU = mybir.AluOpType
ACT = mybir.ActivationFunctionType

D = 96
DE = 32
Q = 8
H = Q // 2
CH = 128 * Q
N_NODES = 50000
N_EDGES = 50000
NCH = -(-N_NODES // CH)
NP = NCH * CH
EP = NCH * CH
ROWS = EP + NP
J = EP // 128
LO = 512
HI = NP // LO
XW = 100
POS, INV_OUT, INV_IN = 96, 97, 98
BIG = 3.0e38
FAR = 1 << 20
LN_EPS = 1e-5
MSG_EPS = 1e-7
LEAK = 0.01
LEAK_ATT = 0.2
assert NCH % 2 == 1 and NCH >= 9 and HI <= 128


def chunks(eng, *stages):
    deep = max(lag for _, lag in stages)

    def step(c):
        for stage, lag in stages:
            if 0 <= c - lag < NCH:
                stage(c - lag, (c - lag) // 2, (c - lag) % 2, c - lag >= 2)

    start = (deep + 3) // 2
    for c in range(2 * start):
        step(c)
    with eng.Fori(start, NCH // 2) as i:
        for odd in range(2):
            for stage, lag in stages:
                stage(i * 2 + (odd - lag), i + (odd - lag) // 2, (odd - lag) % 2, True)
    for c in range(NCH - 1, NCH + deep):
        step(c)


def wait(eng, sem, value):
    eng.wait_ge(sem, value)
    if not isinstance(value, int):
        eng.nop(nofuse=True)


def rows_of(table, c, base=0):
    if isinstance(c, int):
        part = table[base + c * CH:base + c * CH + CH, :]
    else:
        part = table[bass.ds(c * CH + base, CH), :]
    return part.rearrange("(a p r) d -> p a (r d)", a=2, r=H)


def halves(tile):
    return tile.rearrange("p (a r) d -> p a (r d)", a=2)


def scalars_of(row, c):
    part = row[:, c * CH:(c + 1) * CH] if isinstance(c, int) else row[:, bass.ds(c * CH, CH)]
    return part.rearrange("o (a p r) -> (o p) a r", a=2, r=H)


def tile_columns(q):
    at = q // H * 512 + q % H
    return slice(at, at + 509, H)


def span(view, c, width):
    if isinstance(c, int):
        return view[:, c * width:(c + 1) * width]
    return view[:, bass.ds(c * width, width)]


def one(view, c):
    part = view[c:c + 1] if isinstance(c, int) else view[bass.ds(c, 1)]
    return part.rearrange("a p q -> p (a q)")


def clear(nc, sems):
    numbers = [s.num for s in sems]
    assert numbers == list(range(numbers[0], numbers[0] + len(numbers)))
    block = nc.Block()
    with block:
        @block.sync
        def _(sp):
            sp.sem_clear(range(numbers[0], numbers[-1] + 1))

        @block.scalar
        def _(act):
            act.nop()

        @block.vector
        def _(dve):
            dve.nop()

        @block.gpsimd
        def _(pool):
            pool.nop()

        @block.tensor
        def _(pe):
            pe.nop()


def segment_kernel(nc, x, ids, dst_ext, edge_t, W0, b0, W1m, W1e, W1r, b1, W2m, W2e, W2r, b2, Wg, bg,
                   Wa, att_s, att_d, ba, out):
    ctx = ExitStack()
    with ctx:
        def sb(name, shape, dt=F32):
            return ctx.enter_context(nc.sbuf_tensor(name, shape, dt))

        dram = lambda name, shape, dt=F32: nc.dram_tensor(name, shape, dt).ap()
        xa = dram("xa", (NP, XW))
        info = dram("info", (3, NP))
        mask_d = dram("mask_d", (1, EP), BF16)
        restart_d = dram("restart_d", (1, EP), BF16)
        next_d = dram("next_d", (1, EP))
        scat_d = dram("scat_d", (1, EP), I32)
        src_rows = dram("src_rows", (NCH, 128, Q), I32)
        t1 = dram("t1", (ROWS, D))
        tc = dram("tc", (ROWS, D))
        tcT = dram("tcT", (D, EP))
        t2 = dram("t2", (ROWS, D))
        t3 = dram("t3", (ROWS, D))
        ad_d = dram("ad_d", (1, EP))
        ads_d = dram("ads_d", (1, EP))

        ident = sb("ident", [128, 128])
        eps = sb("eps", [128, 1])

        degrees(nc, x, ids, dst_ext, xa, info, mask_d, restart_d, next_d, scat_d, ident, eps)
        layer0(nc, x, ids, xa, src_rows, t1, tc, W0, b0, W1r, b1, mask_d, ident, eps)
        layer1(nc, "a", t1, t1, tc, tcT, src_rows, edge_t, W1m, W1e, W1r, b1, restart_d, ident, eps,
               node=(tc, t1, t2, W2r, b2))
        layer1(nc, "b", tc, t1, t2, tcT, src_rows, edge_t, W2m, W2e, W2r, b2, restart_d, ident, eps,
               node=(t2, t2, t3, Wg, bg))
        layer2(nc, t2, t3, src_rows, ad_d, Wg, bg, Wa, att_d, restart_d, ident, eps,
               node=(t3, out, Wa, ba))
        spread(nc, ad_d, next_d, ads_d, ident)
        layer3(nc, t3, src_rows, scat_d, ads_d, restart_d, out, Wa, att_s, att_d, ba, ident, eps)


def degrees(nc, x, ids, dst_ext, xa, info, mask_d, restart_d, next_d, scat_d, ident, eps):
    K = 4
    JK = J // K
    ctx, sems = ExitStack(), ExitStack()
    with sems, ctx:
        def sb(name, shape, dt=F32):
            return ctx.enter_context(nc.sbuf_tensor(name, shape, dt))

        used = []

        def sem(name):
            used.append(sems.enter_context(nc.semaphore("dg_" + name)))
            return used[-1]

        idall = sb("idall", [128, NCH, 2 * Q], I32)
        shifted = sb("shifted", [128, NCH, 2 * Q], I32)
        hi = sb("hi", [128, NCH, 2 * Q], BF16)
        lo = sb("lo", [128, NCH, 2 * Q])
        iota_lo = sb("iota_lo", [128, LO], F16)
        iota_hi = sb("iota_hi", [128, HI], BF16)
        hot_lo = sb("hot_lo", [128, 2, 2 * Q, LO], BF16)
        hot_hi = sb("hot_hi", [128, 2, 2 * Q, HI], BF16)
        zero = sb("zero", [128, LO], BF16)
        before = sb("before", [HI, HI])
        nid = sb("nid", [HI, LO])
        ends = sb("ends", [HI, LO])
        offs = sb("offs", [HI, 1])
        has = sb("has", [HI, 2, LO])
        root = sb("root", [HI, 2, LO])
        fac = sb("fac", [HI, 3, LO])
        inf = sb("inf", [128, 3, J])
        dprev = sb("dprev", [128, J], I32)
        dcur = sb("dcur", [128, J], I32)
        dnext = sb("dnext", [128, J], I32)
        same = sb("same", [128, J], BF16)
        restart = sb("restart", [128, J], BF16)
        same_next = sb("same_next", [128, J])
        scat = sb("scat", [128, J], I32)
        xt = sb("xt", [128, 2, JK, XW])
        counts = ctx.enter_context(nc.psum_tensor("counts", [128, 2, LO], F32))
        off_ps = ctx.enter_context(nc.psum_tensor("off_ps", [128, LO], F32))

        ids_in = sem("ids_in")
        dst_in = sem("dst_in")
        x_in = [sem("x_in0"), sem("x_in1")]
        x_out = [sem("x_out0"), sem("x_out1")]
        consts = sem("consts")
        id_zero = sem("id_zero")
        split = sem("split")
        hot_ready = sem("hot_ready")
        counted = sem("counted")
        totals = sem("totals")
        offsets = sem("offsets")
        rooted_in = sem("rooted_in")
        rooted = sem("rooted")
        facs = sem("facs")
        info_out = sem("info_out")
        info_in = sem("info_in")
        flags = sem("flags")
        flags_out = sem("flags_out")
        filled = sem("filled")
        block = ctx.enter_context(nc.Block())
        xv = x.rearrange("(p j) d -> p j d", p=128)
        xav = xa.rearrange("(p j) d -> p j d", p=128)
        flat = lambda at: dst_ext[at:at + EP].rearrange("(p j) -> p j", p=128)

        @block.sync
        def _(sp):
            sp.dma_start(idall[:, :, :], ids.rearrange("c p q -> p c q")).then_inc(ids_in, 16)
            sp.dma_start(dprev[:, :], flat(0)).then_inc(dst_in, 16)
            sp.dma_start(dcur[:, :], flat(1)).then_inc(dst_in, 16)
            sp.dma_start(dnext[:, :], flat(2)).then_inc(dst_in, 16)
            for k in range(2):
                sp.dma_start(xt[:, k, :, 0:D], xv[:, k * JK:(k + 1) * JK, :]).then_inc(x_in[k], 16)
            sp.wait_ge(flags, 4)
            sp.dma_start(restart_d.rearrange("a (p j) -> (a p) j", p=128), restart[:, :])\
              .then_inc(flags_out, 16)
            sp.dma_start(mask_d.rearrange("a (p j) -> (a p) j", p=128), same[:, :]).then_inc(flags_out, 16)
            sp.dma_start(next_d.rearrange("a (p j) -> (a p) j", p=128), same_next[:, :])\
              .then_inc(flags_out, 16)
            sp.dma_start(scat_d.rearrange("a (p j) -> (a p) j", p=128), scat[:, :])\
              .then_inc(flags_out, 16)
            sp.wait_ge(facs, 3)
            sp.dma_start(info.rearrange("k (h l) -> h k l", l=LO), fac[:, :, :]).then_inc(info_out, 16)
            sp.wait_ge(info_out, 16)
            sp.dma_start(inf[:, :, :], info.rearrange("k (p j) -> p k j", p=128)).then_inc(info_in, 16)
            for k in range(K):
                u = k % 2
                sp.wait_ge(filled, k + 1)
                sp.dma_start(xav[:, k * JK:(k + 1) * JK, :], xt[:, u, :, :]).then_inc(x_out[u], 16)
                if k + 2 < K:
                    sp.wait_ge(x_out[u], 16 * (k // 2 + 1))
                    sp.dma_start(xt[:, u, :, 0:D], xv[:, (k + 2) * JK:(k + 3) * JK, :])\
                      .then_inc(x_in[u], 16)
            for s in x_out:
                sp.wait_ge(s, 16 * K // 2)
            sp.wait_ge(flags_out, 64)

        @block.gpsimd
        def _(pool):
            pool.iota(iota_lo[:, :], [[1, LO]], base=0, channel_multiplier=0,
                      allow_small_or_imprecise_dtypes=True).then_inc(consts, 1)
            pool.iota(iota_hi[:, :], [[1, HI]], base=0, channel_multiplier=0,
                      allow_small_or_imprecise_dtypes=True).then_inc(consts, 1)
            pool.iota(nid[:, :], [[1, LO]], base=EP, channel_multiplier=LO,
                      allow_small_or_imprecise_dtypes=True).then_inc(consts, 1)
            pool.memset(ident[:, :], 0.0).then_inc(id_zero, 1)
            pool.memset(before[:, :], 1.0).then_inc(id_zero, 1)
            pool.wait_ge(id_zero, 2)
            pool.affine_select(out=ident[:, :], in_=ident[:, :], compare_op=ALU.not_equal, fill=1.0,
                               base=0, pattern=[[-1, 128]], channel_multiplier=1).then_inc(consts, 1)
            pool.affine_select(out=before[:, :], in_=before[:, :], compare_op=ALU.is_gt, fill=0.0,
                               base=0, pattern=[[1, HI]], channel_multiplier=-1).then_inc(consts, 1)

        @block.vector
        def _(dve):
            dve.memset(zero[:, :], 0.0)
            dve.memset(eps[:, :], LN_EPS)
            for u in range(2):
                dve.memset(xt[:, u, :, D:XW], 0.0)
            dve.wait_ge(ids_in, 16)
            dve.tensor_scalar(shifted[:, :, :], idall[:, :, :], 9, None, ALU.logical_shift_right)
            dve.drain()
            dve.tensor_copy(hi[:, :, :], shifted[:, :, :]).then_inc(split, 1)
            dve.drain()
            dve.tensor_scalar(shifted[:, :, :], idall[:, :, :], LO - 1, None, ALU.bitwise_and)
            dve.drain()
            dve.tensor_copy(lo[:, :, :], shifted[:, :, :]).then_inc(split, 1)
            dve.drain()
            dve.wait_ge(dst_in, 48)
            dve.tensor_tensor(same[:, :], dcur[:, :], dprev[:, :], ALU.is_equal).then_inc(flags, 1)
            dve.tensor_tensor(same_next[:, :], dcur[:, :], dnext[:, :], ALU.is_equal).then_inc(flags, 1)
            dve.drain()
            dve.scalar_tensor_tensor(scat[:, :], same_next[:, :], float(FAR), dcur[:, :],
                                     ALU.mult, ALU.add).then_inc(flags, 1)
            dve.tensor_scalar(restart[:, :], same[:, :], -1.0, BIG, ALU.add, ALU.mult).then_inc(flags, 1)
            dve.wait_ge(consts, 5)

            def head(c, i, u, warm):
                if warm:
                    dve.wait_ge(counted, c)
                for q in range(2 * Q):
                    l = lo[:, c, q:q + 1] if isinstance(c, int) else \
                        lo[:, bass.ds(c, 1), q:q + 1].rearrange("p a q -> p (a q)")
                    dve.tensor_scalar(hot_lo[:, u, q, :], iota_lo[:, :], l, None, ALU.is_equal)
                h = hi[:, c:c + 1, :] if isinstance(c, int) else hi[:, bass.ds(c, 1), :]
                h = h.rearrange("p a q -> p (a q)").unsqueeze(2).to_broadcast([128, 2 * Q, HI])
                dve.tensor_tensor(hot_hi[:, u, :, :], h,
                                  iota_hi[:, :].unsqueeze(1).to_broadcast([128, 2 * Q, HI]),
                                  ALU.is_equal).then_inc(hot_ready, 1)
            chunks(dve, (head, 0))

            dve.wait_ge(counted, NCH + 1)
            dve.tensor_scalar(root[:, :, :], counts[0:HI, :, :], 1.0, None, ALU.max).then_inc(rooted_in, 1)
            dve.tensor_scalar(has[:, :, :], counts[0:HI, :, :], 0.0, None, ALU.is_gt)
            dve.drain()
            dve.tensor_tensor_scan(ends[:, :], zero[0:HI, :], counts[0:HI, 1, :], 0.0,
                                   ALU.add, ALU.add).then_inc(totals, 1)
            dve.wait_ge(offsets, 1)
            dve.tensor_scalar(offs[:, :], off_ps[0:HI, 0:1], -1.0, None, ALU.add)
            dve.drain()
            dve.scalar_tensor_tensor(ends[:, :], ends[:, :], offs[:, 0:1], nid[:, :],
                                     ALU.add, ALU.subtract)
            dve.drain()
            dve.tensor_tensor(ends[:, :], ends[:, :], has[:, 1, :], ALU.mult)
            dve.drain()
            dve.tensor_tensor(fac[:, 0, :], ends[:, :], nid[:, :], ALU.add).then_inc(facs, 1)
            dve.wait_ge(rooted, 1)
            dve.reciprocal(root[:, :, :], root[:, :, :])
            dve.drain()
            for k in range(2):
                dve.tensor_tensor(fac[:, 1 + k, :], root[:, k, :], has[:, k, :], ALU.mult)\
                   .then_inc(facs, 1)
            dve.wait_ge(info_in, 16)
            for k in range(K):
                dve.wait_ge(x_in[k % 2], 16 * (k // 2 + 1))
                dve.tensor_copy(xt[:, k % 2, :, D:D + 3],
                                inf[:, :, k * JK:(k + 1) * JK].rearrange("p k j -> p j k"))\
                   .then_inc(filled, 1)

        @block.scalar
        def _(act):
            act.wait_ge(rooted_in, 1)
            act.activation(root[:, :, :], root[:, :, :], ACT.Sqrt).then_inc(rooted, 1)

        @block.tensor
        def _(pe):
            pe.wait_ge(consts, 5)
            pe.wait_ge(split, 2)
            for k in range(2):
                last = pe.matmul(counts[0:HI, k, :], zero[:, 0:HI], zero[:, :], start=True, stop=False,
                                 skip_group_check=True)
            last.then_inc(counted, 1)

            def head(c, i, u, warm):
                pe.wait_ge(hot_ready, c + 1)
                for q in range(2 * Q):
                    last = pe.matmul(counts[0:HI, q // Q, :], hot_hi[:, u, q, :], hot_lo[:, u, q, :],
                                     start=False, stop=False, skip_group_check=True)
                last.then_inc(counted, 1)
            chunks(pe, (head, 0))
            pe.wait_ge(totals, 1)
            pe.matmul(off_ps[0:HI, 0:1], before[:, :], ends[:, LO - 1:LO], start=True, stop=True)\
              .then_inc(offsets, 1)
        ctx.close()
        clear(nc, used)


def norm_stats(dve, tiles, st, mv, u, done):
    for k, t in enumerate(tiles):
        dve.bn_stats(st[:, k, :], t)
    dve.drain()
    for k in range(len(tiles)):
        last = dve.bn_aggr(mv[:, u, k, :], st[:, k, :])
    last.then_inc(done, 1)


def norm_apply(dve, tiles, mv, rstd, u):
    dve.reciprocal(rstd[:, u, :], rstd[:, u, :])
    dve.drain()
    for k, t in enumerate(tiles):
        last = dve.tensor_scalar(t, t, mv[:, u, k, 0:1], rstd[:, u, k:k + 1], ALU.subtract, ALU.mult)
    return last


def gather(pool, tile, u, table, idx, done):
    for q in range(Q):
        pool.indirect_dma_start(tile[:, u, q, :], None, table,
                                bass.IndirectOffsetOnAxis(idx[:, u, q:q + 1], 0)).then_inc(done[u], 16)


def turn(pe, psum, tile, ident, by_edge):
    for q in range(Q):
        to = psum[0:D, tile_columns(q)] if by_edge else psum[0:D, q * 128:(q + 1) * 128]
        last = pe.transpose(to, tile[:, q, :], ident[:, :])
    return last


def layer0(nc, x, ids, xa, src_rows, t1, tc, W0, b0, W1r, b1, mask_d, ident, eps):
    ctx, sems = ExitStack(), ExitStack()
    with sems, ctx:
        def sb(name, shape, dt=F32):
            return ctx.enter_context(nc.sbuf_tensor("l0_" + name, shape, dt))

        def ps(name):
            return ctx.enter_context(nc.psum_tensor("l0_" + name, [128, 2 * 512], F32))

        used = []

        def sem(name):
            used.append(sems.enter_context(nc.semaphore("l0_" + name)))
            return used[-1]

        w0 = sb("w0", [D, D])
        wr = sb("wr", [D + 1, D])
        b0r = sb("b0r", [128, D])
        idx = sb("idx", [128, 2, 2 * Q], I32)
        gs = sb("gs", [128, 2, Q, XW])
        gd = sb("gd", [128, 2, Q, XW])
        xn = sb("xn", [128, 2, Q, D])
        y = sb("y", [128, 2, Q, D])
        S = sb("S", [D, 2, CH])
        mask = sb("mask", [D, 2, CH], BF16)
        st = sb("st", [128, 2 * Q, 6])
        mv = sb("mv", [128, 2, 2 * Q, 2])
        rstd = sb("rstd", [128, 2, 2 * Q])
        xe_out = sb("xe_out", [128, 2, Q, D])
        xn_out = sb("xn_out", [128, 2, Q, D])
        cn_out = sb("cn_out", [128, 2, Q, D])
        cn_small = sb("cn_small", [128, Q, D])
        row_out = sb("row_out", [128, 2, Q], I32)
        xnT = sb("xnT", [D + 1, CH])
        psT, psA, psX, psN = ps("psT"), ps("psA"), ps("psX"), ps("psN")
        A = psA[:, :].rearrange("p (q d) -> p q d", q=Q)
        N = psN[:, :].rearrange("p (q d) -> p q d", q=Q)

        gs_in = [sem("gs_in0"), sem("gs_in1")]
        gd_in = [sem("gd_in0"), sem("gd_in1")]
        used.clear()
        ready = sem("ready")
        scaled = sem("scaled")
        turned = sem("turned")
        scanned = sem("scanned")
        multiplied = sem("multiplied")
        summed_n = sem("summed_n")
        summed_e = sem("summed_e")
        measured = sem("measured")
        rooted = sem("rooted")
        normed = sem("normed")
        turned_n = sem("turned_n")
        copied_n = sem("copied_n")
        rooted_n = sem("rooted_n")
        small_n = sem("small_n")
        conv_n = sem("conv_n")
        weights = sem("weights")
        idx_in = [sem("idx_in0"), sem("idx_in1")]
        mask_in = [sem("mask_in0"), sem("mask_in1")]
        xn_in = [sem("xn_in0"), sem("xn_in1")]
        stored = [sem("stored0"), sem("stored1")]
        stored_n = [sem("stored_n0"), sem("stored_n1")]
        rows_stored = [sem("rows_stored0"), sem("rows_stored1")]
        block = ctx.enter_context(nc.Block())

        @block.sync
        def _(sp):
            sp.dma_start(w0[:, :], W0).then_inc(weights, 16)
            sp.dma_start(wr[0:D, :], W1r).then_inc(weights, 16)
            sp.dma_start(wr[D:D + 1, :], b1).then_inc(weights, 16)
            sp.dma_start(b0r[:, :], b0.to_broadcast([128, D])).then_inc(weights, 16)

            def head(c, i, u, warm):
                if warm:
                    wait(sp, gs_in[u], 128 * i)
                    wait(sp, gd_in[u], 128 * i)
                sp.dma_start(idx[:, u, :], one(ids, c)).then_inc(idx_in[u], 16)
                if warm:
                    wait(sp, scanned, c - 1)
                sp.dma_start(mask[:, u, :], span(mask_d, c, CH).to_broadcast([D, CH]))\
                  .then_inc(mask_in[u], 16)
                if warm:
                    wait(sp, summed_n, c - 1)
                sp.dma_start(halves(xn[:, u, :, :]), rows_of(x, c))\
                  .then_inc(xn_in[u], 16)

            def tail(c, i, u, warm):
                wait(sp, normed, c + 1)
                sp.dma_start(rows_of(t1, c, EP), halves(xn_out[:, u, :, :]))\
                  .then_inc(stored[u], 16)
                sp.dma_start(rows_of(t1, c), halves(xe_out[:, u, :, :]))\
                  .then_inc(stored[u], 16)

            def rows(c, i, u, warm):
                wait(sp, scaled, c + 1)
                sp.dma_start(one(src_rows, c), row_out[:, u, :]).then_inc(rows_stored[u], 16)

            def last(c, i, u, warm):
                wait(sp, conv_n, c + 1)
                sp.dma_start(rows_of(tc, c, EP), halves(cn_out[:, u, :, :]))\
                  .then_inc(stored_n[u], 16)
            chunks(sp, (head, 0), (rows, 1), (tail, 3), (last, 4))
            for u in range(2):
                sp.wait_ge(rows_stored[u], 16 * (NCH // 2 + 1 - u))
                sp.wait_ge(stored[u], 32 * (NCH // 2 + 1 - u))
                sp.wait_ge(stored_n[u], 16 * (NCH // 2 + 1 - u))

        @block.gpsimd
        def _(pool):
            def head(c, i, u, warm):
                wait(pool, idx_in[u], 16 * (i + 1))
                if warm:
                    wait(pool, scaled, c - 1)
                for q in range(Q):
                    pool.indirect_dma_start(gs[:, u, q, :], None, xa,
                                            bass.IndirectOffsetOnAxis(idx[:, u, q:q + 1], 0))\
                        .then_inc(gs_in[u], 16)
                if warm:
                    wait(pool, summed_e, c - 1)
                for q in range(Q):
                    pool.indirect_dma_start(gd[:, u, q, :], None, xa,
                                            bass.IndirectOffsetOnAxis(idx[:, u, Q + q:Q + q + 1], 0))\
                        .then_inc(gd_in[u], 16)
            chunks(pool, (head, 0))

        @block.vector
        def _(dve):
            dve.memset(S[:, 1, CH - 1:CH], 0.0)
            dve.memset(xnT[D:D + 1, :], 1.0).then_inc(ready, 1)
            dve.wait_ge(weights, 64)

            def scale(c, i, u, warm):
                dve.wait_ge(gs_in[u], 128 * (i + 1))
                if warm:
                    dve.wait_ge(turned, c - 1)
                    dve.wait_ge(rows_stored[u], 16 * i)
                dve.tensor_copy(row_out[:, u, :], gs[:, u, :, POS])
                dve.tensor_tensor(y[:, u, :, :], gs[:, u, :, 0:D],
                                  gs[:, u, :, INV_OUT:INV_OUT + 1].to_broadcast([128, Q, D]),
                                  ALU.mult).then_inc(scaled, 1)

            def scan(c, i, u, warm):
                dve.wait_ge(turned, c + 1)
                dve.wait_ge(mask_in[u], 16 * (i + 1))
                if warm:
                    dve.wait_ge(multiplied, c - 1)
                dve.tensor_tensor_scan(S[:, u, :], mask[:, u, :], psT[0:D, :],
                                       S[:, 1 - u, CH - 1:CH], ALU.mult, ALU.add).then_inc(scanned, 1)

            def tiles_of(u):
                return [xn_out[:, u, q, :] for q in range(Q)] + [xe_out[:, u, q, :] for q in range(Q)]

            def stats(c, i, u, warm):
                dve.wait_ge(xn_in[u], 16 * (i + 1))
                if warm:
                    dve.wait_ge(stored[u], 32 * i)
                    dve.wait_ge(turned_n, c - 1)
                dve.tensor_tensor(xn_out[:, u, :, :], xn[:, u, :, :],
                                  b0r[:, :].unsqueeze(1).to_broadcast([128, Q, D]), ALU.add)\
                   .then_inc(summed_n, 1)
                dve.wait_ge(gd_in[u], 128 * (i + 1))
                dve.wait_ge(multiplied, c + 1)
                for q in range(Q):
                    dve.scalar_tensor_tensor(xe_out[:, u, q, :], A[:, q, 0:D],
                                             gd[:, u, q, INV_IN:INV_IN + 1], gd[:, u, q, 0:D],
                                             ALU.mult, ALU.add)
                dve.drain()
                dve.tensor_tensor(xe_out[:, u, :, :], xe_out[:, u, :, :],
                                  b0r[:, :].unsqueeze(1).to_broadcast([128, Q, D]), ALU.add)\
                   .then_inc(summed_e, 1)
                dve.drain()
                norm_stats(dve, tiles_of(u), st, mv, u, measured)

            def apply(c, i, u, warm):
                dve.wait_ge(rooted, c + 1)
                norm_apply(dve, tiles_of(u), mv, rstd, u).then_inc(normed, 1)

            def leaky(c, i, u, warm):
                dve.wait_ge(small_n, c + 1)
                if warm:
                    dve.wait_ge(stored_n[u], 16 * i)
                dve.tensor_tensor(cn_out[:, u, :, :], N[:, :, 0:D], cn_small[:, :, :], ALU.max)\
                   .then_inc(conv_n, 1)
            chunks(dve, (scan, 1), (scale, 0), (apply, 2), (leaky, 3), (stats, 1))

        @block.scalar
        def _(act):
            act.wait_ge(ready, 1)

            def tail(c, i, u, warm):
                act.wait_ge(measured, c + 1)
                act.activation(rstd[:, u, :], mv[:, u, :, 1], ACT.Sqrt, bias=eps[:, :]).then_inc(rooted, 1)

            def last(c, i, u, warm):
                act.wait_ge(turned_n, c + 1)
                if warm or c == 1:
                    act.wait_ge(rooted_n, c)
                act.activation(xnT[0:D, :], psX[0:D, :], ACT.Copy).then_inc(copied_n, 1)
                if warm or c == 1:
                    act.wait_ge(conv_n, c)
                act.wait_ge(rooted_n, c + 1)
                act.activation(cn_small[:, :, :], N[:, :, 0:D], ACT.Copy, scale=LEAK)\
                   .then_inc(small_n, 1)
            chunks(act, (tail, 2), (last, 2))

        @block.tensor
        def _(pe):
            pe.wait_ge(weights, 64)

            def head(c, i, u, warm):
                pe.wait_ge(scaled, c + 1)
                if warm or c == 1:
                    pe.wait_ge(scanned, c)
                turn(pe, psT, y[:, u, :, :], ident, True).then_inc(turned, 1)

            def tail(c, i, u, warm):
                pe.wait_ge(scanned, c + 1)
                if warm or c == 1:
                    pe.wait_ge(summed_e, c)
                for q in range(Q):
                    last = pe.matmul(A[:, q, 0:D], S[:, u, tile_columns(q)], w0[:, :], start=True, stop=True)
                last.then_inc(multiplied, 1)

            def root(c, i, u, warm):
                pe.wait_ge(normed, c + 1)
                if warm or c == 1:
                    pe.wait_ge(copied_n, c)
                turn(pe, psX, xn_out[:, u, :, :], ident, False).then_inc(turned_n, 1)
                pe.wait_ge(copied_n, c + 1)
                if warm or c == 1:
                    pe.wait_ge(conv_n, c)
                for q in range(Q):
                    last = pe.matmul(N[:, q, 0:D], xnT[:, q * 128:(q + 1) * 128], wr[:, :],
                                     start=True, stop=True)
                last.then_inc(rooted_n, 1)
            chunks(pe, (tail, 1), (head, 0), (root, 2))
        ctx.close()
        clear(nc, used)


def layer1(nc, name, table, own, to, ownT, src_rows, edge_t, Wm, We, Wr, b, restart_d,
           ident, eps, node):
    first = name == "a"
    n_rows, n_res, n_to, Wn, bn = node
    LOADS = 4
    ctx = ExitStack()
    with ctx:
        def sb(tag, shape, dt=F32):
            return ctx.enter_context(nc.sbuf_tensor(f"l1{name}_{tag}", shape, dt))

        def ps(tag):
            return ctx.enter_context(nc.psum_tensor(f"l1{name}_{tag}", [128, 2 * 512], F32))

        def sem(tag):
            return ctx.enter_context(nc.semaphore(f"l1{name}_{tag}"))

        wme = sb("wme", [D + DE, D])
        wr = sb("wr", [D + 1, D])
        wn = sb("wn", [D + 1, D])
        idx = sb("idx", [128, 2, Q], I32)
        G = sb("G", [128, 2, Q, D])
        xs = sb("xs", [128, 2, Q, D])
        res = sb("res", [128, 2, Q, D])
        xn = sb("xn", [128, 2, Q, D])
        geT = sb("geT", [D + DE, 2, CH])
        xT = sb("xT", [D + 1, 2, CH])
        nT = sb("nT", [D + 1, CH])
        restart = sb("restart", [D, 2, CH], BF16)
        S = sb("S", [D, 2, CH])
        z = sb("z", [D, CH])
        conv = sb("conv", [D, 2, CH])
        e_out = sb("e_out", [128, 2, Q, D])
        n_out = sb("n_out", [128, 2, Q, D])
        NT = Q if first else 2 * Q
        st = sb("st", [128, NT, 6])
        mv = sb("mv", [128, 2, NT, 2])
        rstd = sb("rstd", [128, 2, NT])
        psT, psA, psX, psN = ps("psT"), ps("psA"), ps("psX"), ps("psN")
        A = psA[:, :].rearrange("p (q d) -> p q d", q=Q)
        N = psN[:, :].rearrange("p (q d) -> p q d", q=Q)

        weights = sem("weights")
        ready = sem("ready")
        idx_in = [sem("idx_in0"), sem("idx_in1")]
        rows_in = [sem("rows_in0"), sem("rows_in1")]
        gathered = [sem("gathered0"), sem("gathered1")]
        res_in = [sem("res_in0"), sem("res_in1")]
        stored = [sem("stored0"), sem("stored1")]
        kept = [sem("kept0"), sem("kept1")]
        turned = sem("turned")
        turned_x = sem("turned_x")
        turned_n = sem("turned_n")
        copied = sem("copied")
        copied_x = sem("copied_x")
        copied_n = sem("copied_n")
        messages = sem("messages")
        own_ready = sem("own_ready")
        rooted_n = sem("rooted_n")
        scanned = sem("scanned")
        added = sem("added")
        leaked = sem("leaked")
        returned = sem("returned")
        taken = sem("taken")
        noded = sem("noded")
        summed = sem("summed")
        measured = sem("measured")
        rooted = sem("rooted")
        normed = sem("normed")
        STORES = 1 if first else 2
        block = ctx.enter_context(nc.Block())

        @block.sync
        def _(sp):
            for t, w in ((wme[0:D, :], Wm), (wme[D:D + DE, :], We), (wr[0:D, :], Wr), (wr[D:D + 1, :], b),
                         (wn[0:D, :], Wn), (wn[D:D + 1, :], bn)):
                sp.dma_start(t, w).then_inc(weights, 16)

            def head(c, i, u, warm):
                if warm:
                    wait(sp, gathered[u], 128 * i)
                sp.dma_start(idx[:, u, :], one(src_rows, c)).then_inc(idx_in[u], 16)
                if warm:
                    wait(sp, scanned, c - 1)
                    wait(sp, own_ready, c - 1)
                sp.dma_start(restart[:, u, :], span(restart_d, c, CH).to_broadcast([D, CH]))\
                  .then_inc(rows_in[u], 16)
                sp.dma_start(geT[D:D + DE, u, :], span(edge_t, c, CH)).then_inc(rows_in[u], 16)
                if first:
                    sp.dma_start(halves(xs[:, u, :, :]), rows_of(own, c)).then_inc(rows_in[u], 16)
                else:
                    sp.dma_start(xT[0:D, u, :], span(ownT, c, CH)).then_inc(rows_in[u], 16)
                if warm:
                    wait(sp, turned_n, c - 1)
                sp.dma_start(halves(xn[:, u, :, :]), rows_of(n_rows, c, EP)).then_inc(rows_in[u], 16)

            def residual(c, i, u, warm):
                if warm:
                    wait(sp, summed, c - 1)
                rows = rows_of(n_res, c, EP) if first else rows_of(own, c)
                sp.dma_start(halves(res[:, u, :, :]), rows).then_inc(res_in[u], 16)

            def keep(c, i, u, warm):
                wait(sp, leaked, c + 1)
                sp.dma_start(span(ownT, c, CH), conv[:, u, :]).then_inc(kept[u], 16)
                wait(sp, taken, c + 1)
                sp.dma_start(rows_of(to, c), halves(e_out[:, u, :, :])).then_inc(kept[u], 16)

            def tail(c, i, u, warm):
                wait(sp, normed, c + 1)
                sp.dma_start(rows_of(n_to, c, EP), halves(n_out[:, u, :, :])).then_inc(stored[u], 16)
                if not first:
                    sp.dma_start(rows_of(to, c), halves(e_out[:, u, :, :])).then_inc(stored[u], 16)
            if first:
                chunks(sp, (head, 0), (residual, 0), (keep, 2), (tail, 3))
            else:
                chunks(sp, (head, 0), (residual, 0), (tail, 3))
            for u in range(2):
                sp.wait_ge(stored[u], 16 * STORES * (NCH // 2 + 1 - u))
                if first:
                    sp.wait_ge(kept[u], 32 * (NCH // 2 + 1 - u))

        @block.gpsimd
        def _(pool):
            def head(c, i, u, warm):
                wait(pool, idx_in[u], 16 * (i + 1))
                if warm:
                    wait(pool, turned, c - 1)
                gather(pool, G, u, table, idx, gathered)
            chunks(pool, (head, 0))

        @block.vector
        def _(dve):
            dve.memset(S[:, 1, CH - 1:CH], 0.0)
            dve.memset(nT[D:D + 1, :], 1.0)
            dve.memset(xT[D:D + 1, :, :], 1.0).then_inc(ready, 1)
            dve.wait_ge(weights, 96)
            if not first:
                dve.tensor_tensor(wn[0:D, :], wn[0:D, :], ident[0:D, 0:D], ALU.add)
            dve.drain().then_inc(ready, 1)

            def head(c, i, u, warm):
                dve.wait_ge(rows_in[u], 16 * LOADS * (i + 1))
                dve.wait_ge(messages, c + 1)
                dve.tensor_tensor_scan(S[:, u, :], restart[:, u, :], psT[0:D, :], S[:, 1 - u, CH - 1:CH],
                                       ALU.add, ALU.max).then_inc(scanned, 1)
                dve.drain()
                dve.wait_ge(own_ready, c + 1)
                dve.tensor_tensor(z[:, :], S[:, u, :], psX[0:D, :], ALU.add).then_inc(added, 1)
                dve.drain()
                if warm:
                    dve.wait_ge(returned, c - 1)
                    if first:
                        dve.wait_ge(kept[u], 32 * i)
                dve.scalar_tensor_tensor(conv[:, u, :], z[:, :], LEAK, z[:, :], ALU.mult, ALU.max)\
                   .then_inc(leaked, 1)

            def tiles_of(u):
                tiles = [n_out[:, u, q, :] for q in range(Q)]
                return tiles if first else tiles + [e_out[:, u, q, :] for q in range(Q)]

            def stats(c, i, u, warm):
                dve.wait_ge(res_in[u], 16 * (i + 1))
                if warm and not first:
                    dve.wait_ge(stored[u], 16 * STORES * i)
                dve.wait_ge(noded, c + 1)
                if first:
                    dve.scalar_tensor_tensor(n_out[:, u, :, :], n_out[:, u, :, :], LEAK,
                                             n_out[:, u, :, :], ALU.mult, ALU.max)
                    dve.drain()
                    dve.tensor_tensor(n_out[:, u, :, :], n_out[:, u, :, :], res[:, u, :, :], ALU.add)\
                       .then_inc(summed, 1)
                else:
                    dve.wait_ge(returned, c + 1)
                    dve.tensor_tensor(e_out[:, u, :, :], A[:, :, 0:D], res[:, u, :, :], ALU.add)\
                       .then_inc(summed, 1)
                dve.drain()
                norm_stats(dve, tiles_of(u), st, mv, u, measured)

            def apply(c, i, u, warm):
                dve.wait_ge(rooted, c + 1)
                norm_apply(dve, tiles_of(u), mv, rstd, u).then_inc(normed, 1)
            chunks(dve, (apply, 2), (stats, 1), (head, 0))

        @block.scalar
        def _(act):
            act.wait_ge(ready, 2)

            def root(c, i, u, warm):
                act.wait_ge(measured, c + 1)
                act.activation(rstd[:, u, :], mv[:, u, :, 1], ACT.Sqrt, bias=eps[:, :]).then_inc(rooted, 1)

            def take(c, i, u, warm):
                act.wait_ge(returned, c + 1)
                if warm:
                    act.wait_ge(kept[u], 32 * i)
                act.activation(e_out[:, u, :, :], A[:, :, 0:D], ACT.Copy).then_inc(taken, 1)

            def head(c, i, u, warm):
                act.wait_ge(turned, c + 1)
                if warm:
                    act.wait_ge(messages, c - 1)
                act.activation(geT[0:D, u, :], psT[0:D, :], ACT.Copy).then_inc(copied, 1)
                act.wait_ge(turned_n, c + 1)
                if warm or c == 1:
                    act.wait_ge(rooted_n, c)
                act.activation(nT[0:D, :], psN[0:D, :], ACT.Copy).then_inc(copied_n, 1)
                if first:
                    act.wait_ge(turned_x, c + 1)
                    if warm:
                        act.wait_ge(own_ready, c - 1)
                    act.activation(xT[0:D, u, :], psX[0:D, :], ACT.Copy).then_inc(copied_x, 1)

            def nodes(c, i, u, warm):
                act.wait_ge(rooted_n, c + 1)
                if warm:
                    act.wait_ge(stored[u], 16 * STORES * i)
                act.activation(n_out[:, u, :, :], N[:, :, 0:D], ACT.Copy).then_inc(noded, 1)
            if first:
                chunks(act, (root, 2), (head, 0), (take, 1), (nodes, 0))
            else:
                chunks(act, (root, 2), (head, 0), (nodes, 0))

        @block.tensor
        def _(pe):
            pe.wait_ge(weights, 96)
            pe.wait_ge(ready, 2)

            def back(c, i, u, warm):
                pe.wait_ge(leaked, c + 1)
                if warm or c == 1:
                    pe.wait_ge(taken if first else summed, c)
                for q in range(Q):
                    last = pe.transpose(A[:, q, 0:D], conv[:, u, tile_columns(q)], ident[0:D, 0:D])
                last.then_inc(returned, 1)

            def head(c, i, u, warm):
                pe.wait_ge(gathered[u], 128 * (i + 1))
                if warm or c == 1:
                    pe.wait_ge(scanned, c)
                turn(pe, psT, G[:, u, :, :], ident, True).then_inc(turned, 1)
                pe.wait_ge(rows_in[u], 16 * LOADS * (i + 1))
                if warm or c == 1:
                    pe.wait_ge(noded, c)
                turn(pe, psN, xn[:, u, :, :], ident, False).then_inc(turned_n, 1)
                if first:
                    if warm or c == 1:
                        pe.wait_ge(added, c)
                    turn(pe, psX, xs[:, u, :, :], ident, True).then_inc(turned_x, 1)

            def products(c, i, u, warm):
                pe.wait_ge(copied, c + 1)
                for h in range(2):
                    part = slice(h * 512, h * 512 + 512)
                    last = pe.matmul(psT[0:D, part], wme[:, :], geT[:, u, part], start=True, stop=True)
                last.then_inc(messages, 1)
                if first:
                    pe.wait_ge(copied_x, c + 1)
                else:
                    pe.wait_ge(rows_in[u], 16 * LOADS * (i + 1))
                    if warm or c == 1:
                        pe.wait_ge(added, c)
                for h in range(2):
                    part = slice(h * 512, h * 512 + 512)
                    last = pe.matmul(psX[0:D, part], wr[:, :], xT[:, u, part], start=True, stop=True)
                last.then_inc(own_ready, 1)
                pe.wait_ge(copied_n, c + 1)
                for q in range(Q):
                    last = pe.matmul(N[:, q, 0:D], nT[:, q * 128:(q + 1) * 128], wn[:, :],
                                     start=True, stop=True)
                last.then_inc(rooted_n, 1)
            chunks(pe, (head, 0), (back, 1), (products, 0))


def running_softmax(dve, restart, values, R, dd, u, differed):
    dve.tensor_copy(R[:, u, 0:1], R[:, 1 - u, CH:CH + 1])
    dve.drain()
    dve.tensor_tensor_scan(R[:, u, 1:CH + 1], restart, values, R[:, u, 0:1], ALU.add, ALU.max)
    dve.drain()
    dve.tensor_tensor(dd[:, 0, :], R[:, u, 0:CH], restart, ALU.add)
    dve.tensor_tensor(dd[:, 1, :], values, R[:, u, 1:CH + 1], ALU.subtract)
    dve.drain()
    dve.tensor_tensor(dd[:, 0, :], dd[:, 0, :], R[:, u, 1:CH + 1], ALU.subtract).then_inc(differed, 1)


def layer2(nc, t2, t3, src_rows, ad_d, Wg, bg, Wa, att_d, restart_d, ident, eps, node):
    n_rows, n_to, Wn, bn = node
    LOADS = 2
    ctx = ExitStack()
    with ctx:
        def sb(tag, shape, dt=F32):
            return ctx.enter_context(nc.sbuf_tensor(f"l2_{tag}", shape, dt))

        def ps(tag):
            return ctx.enter_context(nc.psum_tensor(f"l2_{tag}", [128, 2 * 512], F32))

        def sem(tag):
            return ctx.enter_context(nc.semaphore(f"l2_{tag}"))

        wg = sb("wg", [D, D + 1])
        wx = sb("wx", [D + 1, D + 1])
        wn = sb("wn", [D + 1, D])
        ad = sb("ad", [D, 1])
        v = sb("v", [D, 1])
        v_sum = sb("v_sum", [128, 1])
        wnT = sb("wnT", [D, D])
        wgT = sb("wgT", [D, D])
        wxT = sb("wxT", [D, D + 1])
        eps_col = sb("eps_col", [D, D + 1])
        ones = sb("ones", [D, 128])
        idx = sb("idx", [128, 2, Q], I32)
        G = sb("G", [128, 2, Q, D])
        restart = sb("restart", [D, 2, CH], BF16)
        xs = sb("xs", [128, 2, Q, D])
        xn = sb("xn", [128, 2, Q, D])
        m = sb("m", [D, 2, CH])
        R = sb("R", [D, 2, CH + 1])
        dd = sb("dd", [D, 2, CH])
        P = sb("P", [D, 2, CH])
        S = sb("S", [D, 2, CH])
        T = sb("T", [D, 2, CH])
        inv = sb("inv", [D, 2, CH])
        xT = sb("xT", [D + 1, CH])
        nT = sb("nT", [D + 1, CH])
        e_out = sb("e_out", [128, 2, Q, D])
        n_out = sb("n_out", [128, 2, Q, D])
        ad_raw = sb("ad_raw", [128, 2, Q])
        shift = sb("shift", [128, Q])
        ad_out = sb("ad_out", [128, 2, Q])
        st = sb("st", [128, 2 * Q, 6])
        mv = sb("mv", [128, 2, 2 * Q, 2])
        rstd = sb("rstd", [128, 2, 2 * Q])
        psT, psA, psX, psN = ps("psT"), ps("psA"), ps("psX"), ps("psN")
        A = psA[:, :].rearrange("p (q d) -> p q d", q=Q)
        N = psN[:, :].rearrange("p (q d) -> p q d", q=Q)

        weights = sem("weights")
        ready = sem("ready")
        set_up = sem("set_up")
        widened = sem("widened")
        idx_in = [sem("idx_in0"), sem("idx_in1")]
        restart_in = [sem("restart_in0"), sem("restart_in1")]
        rows_in = [sem("rows_in0"), sem("rows_in1")]
        gathered = [sem("gathered0"), sem("gathered1")]
        stored = [sem("stored0"), sem("stored1")]
        turned = sem("turned")
        rectified = sem("rectified")
        differed = sem("differed")
        exped = sem("exped")
        totalled = sem("totalled")
        mixed = sem("mixed")
        inverted = sem("inverted")
        averaged = sem("averaged")
        turned_x = sem("turned_x")
        turned_n = sem("turned_n")
        copied_x = sem("copied_x")
        copied_n = sem("copied_n")
        rooted_n = sem("rooted_n")
        tanhed = sem("tanhed")
        multiplied = sem("multiplied")
        taken = sem("taken")
        summed = sem("summed")
        measured = sem("measured")
        rooted = sem("rooted")
        normed = sem("normed")
        block = ctx.enter_context(nc.Block())

        @block.sync
        def _(sp):
            for t, w in ((wg[:, 0:D], Wg), (wx[D:D + 1, 0:D], bg), (wn[0:D, :], Wn), (wn[D:D + 1, :], bn),
                         (ad[:, :], att_d)):
                sp.dma_start(t, w).then_inc(weights, 16)

            def head(c, i, u, warm):
                if warm:
                    wait(sp, gathered[u], 128 * i)
                sp.dma_start(idx[:, u, :], one(src_rows, c)).then_inc(idx_in[u], 16)
                if warm:
                    wait(sp, differed, c - 1)
                sp.dma_start(restart[:, u, :], span(restart_d, c, CH).to_broadcast([D, CH]))\
                  .then_inc(restart_in[u], 16)

            def rows(c, i, u, warm):
                if warm:
                    wait(sp, turned_n, c - 1)
                    wait(sp, turned_x, c - 1)
                    wait(sp, summed, c - 1)
                sp.dma_start(halves(xn[:, u, :, :]), rows_of(n_rows, c, EP)).then_inc(rows_in[u], 16)
                sp.dma_start(halves(xs[:, u, :, :]), rows_of(t2, c)).then_inc(rows_in[u], 16)

            def tail(c, i, u, warm):
                wait(sp, normed, c + 1)
                sp.dma_start(rows_of(t3, c), halves(e_out[:, u, :, :])).then_inc(stored[u], 16)
                sp.dma_start(rows_of(n_to, c), halves(n_out[:, u, :, :])).then_inc(stored[u], 16)
                sp.dma_start(scalars_of(ad_d, c), ad_out[:, u, :].rearrange("p (a r) -> p a r", a=2))\
                  .then_inc(stored[u], 16)
            chunks(sp, (head, 0), (rows, 2), (tail, 5))
            for u in range(2):
                sp.wait_ge(stored[u], 48 * (NCH // 2 + 1 - u))

        @block.gpsimd
        def _(pool):
            def head(c, i, u, warm):
                wait(pool, idx_in[u], 16 * (i + 1))
                if warm:
                    wait(pool, turned, c - 1)
                gather(pool, G, u, t2, idx, gathered)

            def average(c, i, u, warm):
                wait(pool, inverted, c + 1)
                wait(pool, mixed, c + 1)
                pool.tensor_tensor(inv[:, u, :], T[:, u, :], inv[:, u, :], ALU.mult).then_inc(averaged, 1)
            chunks(pool, (head, 0), (average, 2))

        @block.vector
        def _(dve):
            dve.memset(R[:, 1, CH:CH + 1], 0.0)
            dve.memset(S[:, 1, CH - 1:CH], 0.0)
            dve.memset(T[:, 1, CH - 1:CH], 0.0)
            dve.memset(eps_col[:, 0:D], 0.0)
            dve.memset(eps_col[:, D:D + 1], MSG_EPS)
            dve.memset(ones[:, :], 1.0)
            dve.memset(xT[D:D + 1, :], 1.0)
            dve.memset(nT[D:D + 1, :], 1.0)
            dve.wait_ge(weights, 80)
            dve.tensor_tensor(wx[0:D, 0:D], wg[:, 0:D], ident[0:D, 0:D], ALU.add).then_inc(ready, 1)
            dve.wait_ge(set_up, 1)
            dve.tensor_tensor(wx[D:D + 1, 0:D], wx[D:D + 1, 0:D], psA[D:D + 1, 0:D], ALU.add)
            dve.tensor_copy(wnT[:, :], psX[0:D, 0:D])
            dve.tensor_copy(wgT[:, :], psN[0:D, 0:D]).then_inc(widened, 1)
            dve.wait_ge(set_up, 2)
            dve.tensor_copy(v[:, :], psA[0:D, 0:1])
            dve.tensor_copy(wxT[:, :], psX[0:D, 0:D + 1]).then_inc(widened, 1)
            dve.wait_ge(set_up, 3)
            dve.tensor_copy(wg[:, D:D + 1], psA[0:D, 0:1])
            dve.tensor_copy(wx[:, D:D + 1], psX[0:D + 1, 0:1])
            dve.tensor_copy(v_sum[:, :], psN[:, 0:1]).then_inc(widened, 1)
            dve.drain()

            def head(c, i, u, warm):
                dve.wait_ge(restart_in[u], 16 * (i + 1))
                dve.wait_ge(rectified, c + 1)
                running_softmax(dve, restart[:, u, :], m[:, u, :], R, dd, u, differed)

            def stats(c, i, u, warm):
                dve.wait_ge(tanhed, c + 1)
                dve.tensor_tensor(n_out[:, u, :, :], n_out[:, u, :, :], xn[:, u, :, :], ALU.add)\
                   .then_inc(summed, 1)
                dve.drain()
                dve.wait_ge(taken, c + 1)
                norm_stats(dve, tiles_of(u), st, mv, u, measured)

            def sums(c, i, u, warm):
                dve.wait_ge(exped, c + 1)
                if warm:
                    dve.wait_ge(averaged, c - 1)
                dve.tensor_tensor_scan(S[:, u, :], P[:, 0, :], P[:, 1, :], S[:, 1 - u, CH - 1:CH],
                                       ALU.mult, ALU.add).then_inc(totalled, 1)
                dve.drain()
                dve.tensor_tensor(P[:, 1, :], P[:, 1, :], m[:, u, :], ALU.mult)
                dve.drain()
                dve.tensor_tensor_scan(T[:, u, :], P[:, 0, :], P[:, 1, :], T[:, 1 - u, CH - 1:CH],
                                       ALU.mult, ALU.add).then_inc(mixed, 1)

            def tiles_of(u):
                return [n_out[:, u, q, :] for q in range(Q)] + [e_out[:, u, q, :] for q in range(Q)]

            def apply(c, i, u, warm):
                dve.wait_ge(rooted, c + 1)
                dve.tensor_tensor(shift[:, :], mv[:, u, Q:2 * Q, 0], v_sum[:, 0:1].to_broadcast([128, Q]),
                                  ALU.mult)
                norm_apply(dve, tiles_of(u), mv, rstd, u)
                dve.tensor_tensor(shift[:, :], ad_raw[:, u, :], shift[:, :], ALU.subtract)
                dve.drain()
                dve.tensor_tensor(ad_out[:, u, :], shift[:, :], rstd[:, u, Q:2 * Q], ALU.mult)\
                   .then_inc(normed, 1)
            chunks(dve, (head, 1), (stats, 4), (sums, 1), (apply, 4))

        @block.scalar
        def _(act):
            act.wait_ge(ready, 1)

            def own(c, i, u, warm):
                act.wait_ge(turned_n, c + 1)
                if warm or c == 1:
                    act.wait_ge(rooted_n, c)
                act.activation(nT[0:D, :], psN[0:D, :], ACT.Copy).then_inc(copied_n, 1)
                act.wait_ge(turned_x, c + 1)
                if warm or c == 1:
                    act.wait_ge(multiplied, c)
                act.activation(xT[0:D, :], psX[0:D, :], ACT.Copy).then_inc(copied_x, 1)

            def exps(c, i, u, warm):
                act.wait_ge(differed, c + 1)
                if warm or c == 1:
                    act.wait_ge(mixed, c)
                act.activation(P[:, :, :], dd[:, :, :], ACT.Exp).then_inc(exped, 1)

            def rectify(c, i, u, warm):
                act.wait_ge(turned, c + 1)
                if warm:
                    act.wait_ge(mixed, c - 1)
                act.activation(m[:, u, :], psT[0:D, :], ACT.Relu).then_inc(rectified, 1)

            def take(c, i, u, warm):
                act.wait_ge(rooted_n, c + 1)
                if warm:
                    act.wait_ge(stored[u], 48 * i)
                act.activation(n_out[:, u, :, :], N[:, :, 0:D], ACT.Tanh).then_inc(tanhed, 1)
                act.wait_ge(multiplied, c + 1)
                act.activation(ad_raw[:, u, :], A[:, :, D], ACT.Copy)
                act.activation(e_out[:, u, :, :], A[:, :, 0:D], ACT.Copy).then_inc(taken, 1)

            def root(c, i, u, warm):
                act.wait_ge(measured, c + 1)
                act.activation(rstd[:, u, :], mv[:, u, :, 1], ACT.Sqrt, bias=eps[:, :]).then_inc(rooted, 1)

            def invert(c, i, u, warm):
                act.wait_ge(totalled, c + 1)
                if warm:
                    act.wait_ge(multiplied, c - 1)
                act.activation(inv[:, u, :], S[:, u, :], ACT.Ln)
                act.drain()
                act.activation(inv[:, u, :], inv[:, u, :], ACT.Exp, scale=-1.0).then_inc(inverted, 1)
            chunks(act, (own, 3), (exps, 1), (root, 4), (rectify, 0), (take, 3), (invert, 1))

        @block.tensor
        def _(pe):
            pe.wait_ge(weights, 80)
            pe.wait_ge(ready, 1)
            pe.matmul(psA[0:D + 1, 0:D], eps_col[:, :], wg[:, 0:D], start=True, stop=True)
            pe.transpose(psX[0:D, 0:D], wn[0:D, :], ident[0:D, 0:D])
            pe.transpose(psN[0:D, 0:D], wg[:, 0:D], ident[0:D, 0:D]).then_inc(set_up, 1)
            pe.wait_ge(widened, 1)
            pe.matmul(psA[0:D, 0:1], wnT[:, :], ad[:, :], start=True, stop=True)
            pe.transpose(psX[0:D, 0:D + 1], wx[:, 0:D], ident[0:D + 1, 0:D + 1]).then_inc(set_up, 1)
            pe.wait_ge(widened, 2)
            pe.matmul(psA[0:D, 0:1], wgT[:, :], v[:, :], start=True, stop=True)
            pe.matmul(psX[0:D + 1, 0:1], wxT[:, :], v[:, :], start=True, stop=True)
            pe.matmul(psN[:, 0:1], ones[:, :], v[:, :], start=True, stop=True).then_inc(set_up, 1)
            pe.wait_ge(widened, 3)

            def head(c, i, u, warm):
                pe.wait_ge(gathered[u], 128 * (i + 1))
                if warm or c == 1:
                    pe.wait_ge(rectified, c)
                turn(pe, psT, G[:, u, :, :], ident, True).then_inc(turned, 1)

            def tail(c, i, u, warm):
                pe.wait_ge(rows_in[u], 16 * LOADS * (i + 1))
                if warm or c == 1:
                    pe.wait_ge(tanhed, c)
                turn(pe, psN, xn[:, u, :, :], ident, False).then_inc(turned_n, 1)
                if warm or c == 1:
                    pe.wait_ge(copied_x, c)
                turn(pe, psX, xs[:, u, :, :], ident, False).then_inc(turned_x, 1)
                pe.wait_ge(copied_n, c + 1)
                for q in range(Q):
                    last = pe.matmul(N[:, q, 0:D], nT[:, q * 128:(q + 1) * 128], wn[:, :],
                                     start=True, stop=True)
                last.then_inc(rooted_n, 1)
                pe.wait_ge(averaged, c + 1)
                pe.wait_ge(copied_x, c + 1)
                if warm or c == 1:
                    pe.wait_ge(taken, c)
                for q in range(Q):
                    pe.matmul(A[:, q, 0:D + 1], inv[:, u, tile_columns(q)], wg[:, :],
                              start=True, stop=False)
                    last = pe.matmul(A[:, q, 0:D + 1], xT[:, q * 128:(q + 1) * 128], wx[:, :],
                                     start=False, stop=True)
                last.then_inc(multiplied, 1)
            chunks(pe, (head, 0), (tail, 3))


def spread(nc, ad_d, next_d, ads_d, ident):
    ctx = ExitStack()
    with ctx:
        def sb(tag, shape, dt=F32):
            return ctx.enter_context(nc.sbuf_tensor(f"sp_{tag}", shape, dt))

        def sem(tag):
            return ctx.enter_context(nc.semaphore(f"sp_{tag}"))

        a = sb("a", [128, J])
        nxt = sb("nxt", [128, J])
        only = sb("only", [128, J])
        ones = sb("ones", [128, J])
        keep = sb("keep", [128, J])
        found = sb("found", [128, J])
        rows = sb("rows", [1, 2, 128])
        carry = sb("carry", [1, 129])
        res = sb("res", [128, J])
        carried = sb("carried", [128, 1])
        ps = ctx.enter_context(nc.psum_tensor("sp_ps", [128, 512], F32))
        filled = sem("filled")
        loaded = sem("loaded")
        scanned = sem("scanned")
        turned = sem("turned")
        chained = sem("chained")
        returned = sem("returned")
        copied = sem("copied")
        done = sem("done")
        stored = sem("stored")
        block = ctx.enter_context(nc.Block())

        @block.sync
        def _(sp):
            sp.dma_start(a[:, :], ad_d.rearrange("a (p j) -> (a p) j", p=128)).then_inc(loaded, 16)
            sp.dma_start(nxt[:, :], next_d.rearrange("a (p j) -> (a p) j", p=128)).then_inc(loaded, 16)
            sp.wait_ge(done, 1)
            sp.dma_start(ads_d.rearrange("a (p j) -> (a p) j", p=128), res[:, :]).then_inc(stored, 16)
            sp.wait_ge(stored, 16)

        @block.vector
        def _(dve):
            dve.wait_ge(filled, 2)
            dve.wait_ge(loaded, 32)
            dve.tensor_tensor(only[:, :], nxt[:, :], a[:, :], ALU.mult)
            dve.drain()
            dve.tensor_tensor(only[:, :], a[:, :], only[:, :], ALU.subtract)
            dve.tensor_tensor_scan(keep[:, ::-1], nxt[:, ::-1], ones[:, ::-1], 1.0, ALU.mult, ALU.mult)
            dve.drain()
            dve.tensor_tensor_scan(found[:, ::-1], nxt[:, ::-1], only[:, ::-1], 0.0, ALU.mult, ALU.add)\
               .then_inc(scanned, 1)
            dve.wait_ge(turned, 1)
            dve.tensor_copy(rows[:, :, :], ps[0:1, 0:256].rearrange("p (a m) -> p a m", a=2))
            dve.drain()
            dve.tensor_tensor_scan(carry[:, 127::-1], rows[:, 0, ::-1], rows[:, 1, ::-1], 0.0,
                                   ALU.mult, ALU.add).then_inc(chained, 1)
            dve.wait_ge(copied, 1)
            dve.scalar_tensor_tensor(res[:, :], keep[:, :], carried[:, 0:1], found[:, :],
                                     ALU.mult, ALU.add).then_inc(done, 1)

        @block.scalar
        def _(act):
            act.wait_ge(returned, 1)
            act.activation(carried[:, :], ps[:, 256:257], ACT.Copy).then_inc(copied, 1)

        @block.gpsimd
        def _(pool):
            pool.memset(ones[:, :], 1.0).then_inc(filled, 1)
            pool.memset(carry[:, :], 0.0).then_inc(filled, 1)

        @block.tensor
        def _(pe):
            pe.wait_ge(scanned, 1)
            pe.transpose(ps[0:1, 0:128], keep[:, 0:1], ident[:, :])
            pe.transpose(ps[0:1, 128:256], found[:, 0:1], ident[:, :]).then_inc(turned, 1)
            pe.wait_ge(chained, 1)
            pe.matmul(ps[:, 256:257], carry[:, 1:129], ident[0:1, 0:1], start=True, stop=True)\
              .then_inc(returned, 1)


def layer3(nc, t3, src_rows, scat_d, ads_d, restart_d, out, Wa, att_s, att_d, ba, ident, eps):
    ctx = ExitStack()
    with ctx:
        def sb(tag, shape, dt=F32):
            return ctx.enter_context(nc.sbuf_tensor(f"l3_{tag}", shape, dt))

        def ps(tag):
            return ctx.enter_context(nc.psum_tensor(f"l3_{tag}", [128, 2 * 512], F32))

        def sem(tag):
            return ctx.enter_context(nc.semaphore(f"l3_{tag}"))

        wh = sb("wh", [D, D + 1])
        wt = sb("wt", [D + 1, D + 1])
        att = sb("att", [D, 2])
        att_wide = sb("att_wide", [D, D + 1])
        waT = sb("waT", [D, D])
        ws_wide = sb("ws_wide", [D + 2, D + 1])
        bar = sb("bar", [128, D])
        idx = sb("idx", [128, 2, Q], I32)
        sidx = sb("sidx", [128, 2, Q], I32)
        G = sb("G", [128, 2, Q, D])
        restart = sb("restart", [D + 1, 2, CH], BF16)
        xs = sb("xs", [128, 2, Q, D])
        res = sb("res", [128, 2, Q, D])
        gT = sb("gT", [D + 2, 2, CH])
        score = sb("score", [D + 1, 2, CH])
        R = sb("R", [D + 1, 2, CH + 1])
        dd = sb("dd", [D + 1, 2, CH])
        P = sb("P", [D + 1, 2, CH])
        T = sb("T", [D + 1, 2, CH])
        xT = sb("xT", [D, CH])
        own = sb("own", [128, 2, Q])
        top = sb("top", [128, Q])
        less = sb("less", [128, 2, Q])
        share = sb("share", [128, 2, Q])
        total = sb("total", [128, Q])
        e_out = sb("e_out", [128, 2, Q, D])
        s_out = sb("s_out", [128, 2, Q, D])
        st = sb("st", [128, Q, 6])
        mv = sb("mv", [128, 2, Q, 2])
        rstd = sb("rstd", [128, 2, Q])
        psT, psA, psX, psH = ps("psT"), ps("psA"), ps("psX"), ps("psH")
        A = psA[:, :].rearrange("p (q d) -> p q d", q=Q)
        Hp = psH[:, :].rearrange("p (q d) -> p q d", q=Q)

        weights = sem("weights")
        ready = sem("ready")
        set_up = sem("set_up")
        widened = sem("widened")
        idx_in = [sem("idx_in0"), sem("idx_in1")]
        restart_in = [sem("restart_in0"), sem("restart_in1")]
        ads_in = [sem("ads_in0"), sem("ads_in1")]
        rows_in = [sem("rows_in0"), sem("rows_in1")]
        res_in = [sem("res_in0"), sem("res_in1")]
        sidx_in = [sem("sidx_in0"), sem("sidx_in1")]
        gathered = [sem("gathered0"), sem("gathered1")]
        scattered = [sem("scattered0"), sem("scattered1")]
        turned = sem("turned")
        copied = sem("copied")
        scored = sem("scored")
        score_out = sem("score_out")
        differed = sem("differed")
        exped = sem("exped")
        mixed = sem("mixed")
        turned_x = sem("turned_x")
        copied_x = sem("copied_x")
        own_ready = sem("own_ready")
        own_out = sem("own_out")
        multiplied = sem("multiplied")
        lessened = sem("lessened")
        shares = sem("shares")
        weighed = sem("weighed")
        scaled = sem("scaled")
        joined = sem("joined")
        biased = sem("biased")
        tanhed = sem("tanhed")
        summed = sem("summed")
        measured = sem("measured")
        rooted = sem("rooted")
        normed = sem("normed")
        block = ctx.enter_context(nc.Block())

        @block.sync
        def _(sp):
            for t, w in ((wh[:, 0:D], Wa), (wt[0:D, 0:D], Wa), (att[:, 0:1], att_s), (att[:, 1:2], att_d),
                         (bar[:, :], ba.to_broadcast([128, D]))):
                sp.dma_start(t, w).then_inc(weights, 16)

            def head(c, i, u, warm):
                if warm:
                    wait(sp, gathered[u], 128 * i)
                sp.dma_start(idx[:, u, :], one(src_rows, c)).then_inc(idx_in[u], 16)
                if warm:
                    wait(sp, differed, c - 1)
                sp.dma_start(restart[:, u, :], span(restart_d, c, CH).to_broadcast([D + 1, CH]))\
                  .then_inc(restart_in[u], 16)
                if warm:
                    wait(sp, mixed, c - 1)
                sp.dma_start(gT[D + 1:D + 2, u, :], span(ads_d, c, CH)).then_inc(ads_in[u], 16)

            def rows(c, i, u, warm):
                if warm:
                    wait(sp, turned_x, c - 1)
                sp.dma_start(halves(xs[:, u, :, :]), rows_of(t3, c)).then_inc(rows_in[u], 16)

            def residual(c, i, u, warm):
                if warm:
                    wait(sp, summed, c - 1)
                sp.dma_start(halves(res[:, u, :, :]), rows_of(t3, c)).then_inc(res_in[u], 16)

            def nodes(c, i, u, warm):
                if warm:
                    wait(sp, scattered[u], 128 * i)
                sp.dma_start(sidx[:, u, :].rearrange("p (a r) -> p a r", a=2), scalars_of(scat_d, c))\
                  .then_inc(sidx_in[u], 16)
            chunks(sp, (head, 0), (rows, 1), (residual, 3), (nodes, 4))

        @block.gpsimd
        def _(pool):
            def head(c, i, u, warm):
                wait(pool, idx_in[u], 16 * (i + 1))
                if warm:
                    wait(pool, turned, c - 1)
                gather(pool, G, u, t3, idx, gathered)

            def scatter(c, i, u, warm):
                wait(pool, sidx_in[u], 16 * (i + 1))
                wait(pool, normed, c + 1)
                for q in range(Q):
                    pool.indirect_dma_start(out, bass.IndirectOffsetOnAxis(sidx[:, u, q:q + 1], 0),
                                            s_out[:, u, q, :], None, bounds_check=NP - 1,
                                            oob_is_err=False).then_inc(scattered[u], 16)
            chunks(pool, (head, 0), (scatter, 5))
            for u in range(2):
                pool.wait_ge(scattered[u], 128 * (NCH // 2 + 1 - u))

        @block.vector
        def _(dve):
            dve.memset(R[:, 1, CH:CH + 1], 0.0)
            dve.memset(T[:, 1, CH - 1:CH], 0.0)
            dve.memset(gT[D:D + 1, :, :], 1.0)
            dve.memset(wt[:, D:D + 1], 0.0)
            dve.memset(wt[D:D + 1, 0:D], 0.0)
            dve.memset(ws_wide[D:D + 2, :], 1.0)
            dve.drain()
            dve.memset(wt[D:D + 1, D:D + 1], 1.0)
            dve.memset(ws_wide[D:D + 1, :], 0.0)
            dve.wait_ge(weights, 80)
            dve.tensor_copy(att_wide[:, :], att[:, 0:1].to_broadcast([D, D + 1])).then_inc(ready, 1)
            dve.wait_ge(set_up, 1)
            dve.tensor_copy(waT[:, :], psX[0:D, 0:D]).then_inc(widened, 1)
            dve.wait_ge(set_up, 2)
            dve.tensor_copy(ws_wide[0:D, :], psA[0:D, 0:D + 1])
            dve.tensor_copy(wh[:, D:D + 1], psH[0:D, 0:1]).then_inc(widened, 1)

            def head(c, i, u, warm):
                dve.wait_ge(score_out, c + 1)
                dve.scalar_tensor_tensor(score[:, u, :], score[:, u, :], LEAK_ATT, score[:, u, :],
                                         ALU.mult, ALU.max)
                dve.drain()
                dve.wait_ge(restart_in[u], 16 * (i + 1))
                if warm:
                    dve.wait_ge(multiplied, c - 1)
                running_softmax(dve, restart[:, u, :], score[:, u, :], R, dd, u, differed)

            def scores(c, i, u, warm):
                dve.wait_ge(own_out, c + 1)
                dve.scalar_tensor_tensor(own[:, u, :], own[:, u, :], LEAK_ATT, own[:, u, :],
                                         ALU.mult, ALU.max)
                dve.drain()
                dve.wait_ge(multiplied, c + 1)
                dve.tensor_tensor(top[:, :], own[:, u, :], A[:, :, D + 1], ALU.max)
                dve.drain()
                dve.tensor_tensor(less[:, 0, :], A[:, :, D + 1], top[:, :], ALU.subtract)
                dve.tensor_tensor(less[:, 1, :], own[:, u, :], top[:, :], ALU.subtract).then_inc(lessened, 1)

            def post(c, i, u, warm):
                dve.wait_ge(tanhed, c + 1)
                dve.wait_ge(res_in[u], 16 * (i + 1))
                dve.tensor_tensor(e_out[:, u, :, :], e_out[:, u, :, :], res[:, u, :, :], ALU.add)\
                   .then_inc(summed, 1)
                dve.drain()
                norm_stats(dve, [e_out[:, u, q, :] for q in range(Q)], st, mv, u, measured)

            def weigh(c, i, u, warm):
                dve.wait_ge(shares, c + 1)
                dve.tensor_tensor(total[:, :], A[:, :, D], share[:, 0, :], ALU.mult)
                dve.drain()
                dve.scalar_tensor_tensor(total[:, :], total[:, :], 1e-16, share[:, 1, :], ALU.add, ALU.add)
                dve.drain()
                dve.reciprocal(total[:, :], total[:, :])
                dve.drain()
                dve.tensor_tensor(share[:, :, :], share[:, :, :],
                                  total[:, :].unsqueeze(1).to_broadcast([128, 2, Q]), ALU.mult)\
                   .then_inc(weighed, 1)

            def sums(c, i, u, warm):
                dve.wait_ge(exped, c + 1)
                dve.tensor_tensor(P[:, 1, :], P[:, 1, :], gT[0:D + 1, u, :], ALU.mult)
                dve.drain()
                if warm:
                    dve.wait_ge(multiplied, c - 1)
                dve.tensor_tensor_scan(T[:, u, :], P[:, 0, :], P[:, 1, :], T[:, 1 - u, CH - 1:CH],
                                       ALU.mult, ALU.add).then_inc(mixed, 1)

            def join(c, i, u, warm):
                dve.wait_ge(scaled, c + 1)
                for q in range(Q):
                    last = dve.scalar_tensor_tensor(e_out[:, u, q, :], Hp[:, q, 0:D], share[:, 1, q:q + 1],
                                                    e_out[:, u, q, :], ALU.mult, ALU.add)
                last.then_inc(joined, 1)
                dve.drain()
                dve.tensor_tensor(e_out[:, u, :, :], e_out[:, u, :, :],
                                  bar[:, :].unsqueeze(1).to_broadcast([128, Q, D]), ALU.add)\
                   .then_inc(biased, 1)

            def apply(c, i, u, warm):
                dve.wait_ge(rooted, c + 1)
                dve.reciprocal(rstd[:, u, :], rstd[:, u, :])
                dve.drain()
                if warm:
                    dve.wait_ge(scattered[u], 128 * i)
                for q in range(Q):
                    last = dve.tensor_scalar(s_out[:, u, q, :], e_out[:, u, q, :], mv[:, u, q, 0:1],
                                             rstd[:, u, q:q + 1], ALU.subtract, ALU.mult)
                last.then_inc(normed, 1)
            chunks(dve, (head, 1), (scores, 3), (post, 4), (weigh, 3), (sums, 1), (join, 3), (apply, 4))

        @block.scalar
        def _(act):
            def copy(c, i, u, warm):
                act.wait_ge(turned, c + 1)
                if warm:
                    act.wait_ge(mixed, c - 1)
                act.activation(gT[0:D, u, :], psT[0:D, :], ACT.Copy).then_inc(copied, 1)

            def own_rows(c, i, u, warm):
                act.wait_ge(turned_x, c + 1)
                if warm or c == 1:
                    act.wait_ge(own_ready, c)
                act.activation(xT[:, :], psX[0:D, :], ACT.Copy).then_inc(copied_x, 1)

            def take(c, i, u, warm):
                act.wait_ge(scored, c + 1)
                if warm:
                    act.wait_ge(differed, c - 1)
                act.activation(score[:, u, :], psT[0:D + 1, :], ACT.Copy).then_inc(score_out, 1)

            def exps(c, i, u, warm):
                act.wait_ge(differed, c + 1)
                if warm or c == 1:
                    act.wait_ge(mixed, c)
                act.activation(P[:, :, :], dd[:, :, :], ACT.Exp).then_inc(exped, 1)

            def join(c, i, u, warm):
                act.wait_ge(lessened, c + 1)
                if warm or c == 1:
                    act.wait_ge(joined, c)
                act.activation(share[:, :, :], less[:, :, :], ACT.Exp).then_inc(shares, 1)

            def scale(c, i, u, warm):
                act.wait_ge(weighed, c + 1)
                if warm:
                    act.wait_ge(normed, c - 1)
                for q in range(Q):
                    last = act.activation(e_out[:, u, q, :], A[:, q, 0:D], ACT.Copy,
                                          scale=share[:, 0, q:q + 1])
                last.then_inc(scaled, 1)

            def root(c, i, u, warm):
                act.wait_ge(measured, c + 1)
                act.activation(rstd[:, u, :], mv[:, u, :, 1], ACT.Sqrt, bias=eps[:, :]).then_inc(rooted, 1)

            def tanh(c, i, u, warm):
                act.wait_ge(biased, c + 1)
                act.activation(e_out[:, u, :, :], e_out[:, u, :, :], ACT.Tanh).then_inc(tanhed, 1)

            def take_own(c, i, u, warm):
                act.wait_ge(own_ready, c + 1)
                if warm:
                    act.wait_ge(lessened, c - 1)
                act.activation(own[:, u, :], Hp[:, :, D], ACT.Copy).then_inc(own_out, 1)
            chunks(act, (copy, 0), (own_rows, 2), (take, 0), (exps, 1), (join, 3), (scale, 3), (root, 4),
                   (tanh, 3), (take_own, 2))

        @block.tensor
        def _(pe):
            pe.wait_ge(weights, 80)
            pe.wait_ge(ready, 1)
            pe.transpose(psX[0:D, 0:D], wh[:, 0:D], ident[0:D, 0:D]).then_inc(set_up, 1)
            pe.wait_ge(widened, 1)
            pe.matmul(psA[0:D, 0:D + 1], waT[:, :], att_wide[:, :], start=True, stop=True)
            pe.matmul(psH[0:D, 0:1], waT[:, :], att[:, 0:1], start=True, stop=False)
            pe.matmul(psH[0:D, 0:1], waT[:, :], att[:, 1:2], start=False, stop=True).then_inc(set_up, 1)
            pe.wait_ge(widened, 2)

            def head(c, i, u, warm):
                pe.wait_ge(gathered[u], 128 * (i + 1))
                if warm or c == 1:
                    pe.wait_ge(score_out, c)
                turn(pe, psT, G[:, u, :, :], ident, True).then_inc(turned, 1)

            def own_rows(c, i, u, warm):
                pe.wait_ge(rows_in[u], 16 * (i + 1))
                if warm or c == 1:
                    pe.wait_ge(copied_x, c)
                turn(pe, psX, xs[:, u, :, :], ident, False).then_inc(turned_x, 1)

            def scores(c, i, u, warm):
                pe.wait_ge(copied, c + 1)
                pe.wait_ge(ads_in[u], 16 * (i + 1))
                for h in range(2):
                    part = slice(h * 512, h * 512 + 512)
                    last = pe.matmul(psT[0:D + 1, part], ws_wide[:, :], gT[:, u, part],
                                     start=True, stop=True)
                last.then_inc(scored, 1)

            def tail(c, i, u, warm):
                pe.wait_ge(copied_x, c + 1)
                if warm or c == 1:
                    pe.wait_ge(joined, c)
                for q in range(Q):
                    last = pe.matmul(Hp[:, q, 0:D + 1], xT[:, q * 128:(q + 1) * 128], wh[:, :],
                                     start=True, stop=True)
                last.then_inc(own_ready, 1)
                pe.wait_ge(mixed, c + 1)
                for q in range(Q):
                    at = tile_columns(q)
                    pe.matmul(A[:, q, 0:D + 1], T[:, u, at], wt[:, :], start=True, stop=True)
                    shifted = slice(at.start + 1, at.stop + 1, H)
                    last = pe.transpose(A[:, q, D + 1:D + 2], R[0:1, u, shifted], ident[0:1, 0:1])
                last.then_inc(multiplied, 1)
            chunks(pe, (head, 0), (own_rows, 2), (scores, 0), (tail, 2))


def kernel(**inputs):
    import concourse.bacc as bacc
    from concourse.bass_utils import run_bass_kernel_spmd

    nc = bacc.Bacc("TRN2", target_bir_lowering=False, num_devices=1)
    arrays = {}

    def put(name, array):
        arrays[name] = np.ascontiguousarray(array)
        return nc.dram_tensor(name, arrays[name].shape, mybir.dt.from_np(arrays[name].dtype),
                              kind="ExternalInput").ap()

    src, dst = (np.concatenate([np.asarray(inputs[k]), np.full(EP - N_EDGES, N_NODES, np.int32)])
                for k in ("src", "dst"))
    x = np.concatenate([np.asarray(inputs["x"]), np.zeros((NP - N_NODES, D), np.float32)])
    ids = np.concatenate([a.reshape(NCH, 2, 128, H).transpose(0, 2, 1, 3).reshape(NCH, 128, Q)
                          for a in (src, dst)], axis=2)
    dst_ext = np.concatenate([np.full(1, -1, np.int32), dst, np.full(1, NP, np.int32)])
    attr = np.concatenate([np.asarray(inputs["edge_attr_32"]), np.zeros((EP - N_EDGES, DE), np.float32)])
    args = [put("x_pad", x), put("ids", ids), put("dst_ext", dst_ext), put("edge_t", attr.T)]
    for name in ("L0_gnn_W", "L0_gnn_b", "L1_gnn_W1_msg", "L1_gnn_W1_edge", "L1_gnn_W1_root", "L1_gnn_b1",
                 "L1_gnn_W2_msg", "L1_gnn_W2_edge", "L1_gnn_W2_root", "L1_gnn_b2", "L2_gnn_W", "L2_gnn_b",
                 "L3_gnn_W", "L3_gnn_att_src", "L3_gnn_att_dst", "L3_gnn_bias"):
        a = np.asarray(inputs[name])
        if a.ndim == 1:
            a = a.reshape((D, 1) if "att" in name else (1, D))
        args.append(put(name, a))
    out = nc.dram_tensor("out", (NP, D), F32, kind="ExternalOutput").ap()
    segment_kernel(nc, *args, out)
    run = run_bass_kernel_spmd(nc, [arrays], core_ids=[0])
    return run.results[0]["out"][:N_NODES]
```

```python
import numpy as np
import concourse.bass as bass
from concourse import mybir
from contextlib import ExitStack

F32 = mybir.dt.float32
I32 = mybir.dt.int32
BF16 = mybir.dt.bfloat16
F16 = mybir.dt.float16
ALU = mybir.AluOpType
ACT = mybir.ActivationFunctionType

D = 96
DE = 32
Q = 8
H = Q // 2
CH = 128 * Q
N_NODES = 50000
N_EDGES = 50000
NCH = -(-N_NODES // CH)
NP = NCH * CH
EP = NCH * CH
ROWS = EP + NP
J = EP // 128
LO = 512
HI = NP // LO
XW = 98
POS, INV_OUT = 96, 97
BIG = 3.0e38
FAR = 1 << 20
LN_EPS = 1e-5
MSG_EPS = 1e-7
LEAK = 0.01
LEAK_ATT = 0.2
assert NCH % 2 == 1 and NCH >= 9 and HI <= 128


def chunks(eng, *stages):
    deep = max(lag for _, lag in stages)

    def step(c):
        for stage, lag in stages:
            if 0 <= c - lag < NCH:
                stage(c - lag, (c - lag) // 2, (c - lag) % 2, c - lag >= 2)

    start = (deep + 3) // 2
    for c in range(2 * start):
        step(c)
    with eng.Fori(start, NCH // 2) as i:
        for odd in range(2):
            for stage, lag in stages:
                stage(i * 2 + (odd - lag), i + (odd - lag) // 2, (odd - lag) % 2, True)
    for c in range(NCH - 1, NCH + deep):
        step(c)


def wait(eng, sem, value):
    eng.wait_ge(sem, value)
    if not isinstance(value, int):
        eng.nop(nofuse=True)


def rows_of(table, c, base=0):
    if isinstance(c, int):
        part = table[base + c * CH:base + c * CH + CH, :]
    else:
        part = table[bass.ds(c * CH + base, CH), :]
    return part.rearrange("(a p r) d -> p a (r d)", a=2, r=H)


def halves(tile):
    return tile.rearrange("p (a r) d -> p a (r d)", a=2)


def scalars_of(row, c):
    part = row[:, c * CH:(c + 1) * CH] if isinstance(c, int) else row[:, bass.ds(c * CH, CH)]
    return part.rearrange("o (a p r) -> (o p) a r", a=2, r=H)


def tile_columns(q):
    at = q // H * 512 + q % H
    return slice(at, at + 509, H)


def span(view, c, width):
    if isinstance(c, int):
        return view[:, c * width:(c + 1) * width]
    return view[:, bass.ds(c * width, width)]


def one(view, c):
    part = view[c:c + 1] if isinstance(c, int) else view[bass.ds(c, 1)]
    return part.rearrange("a p q -> p (a q)")


def clear(nc, sems):
    numbers = sorted(s.num for s in sems)
    firsts = [n for n in numbers if n - 1 not in numbers]
    lasts = [n for n in numbers if n + 1 not in numbers]
    block = nc.Block()
    with block:
        @block.sync
        def _(sp):
            for first, last in zip(firsts, lasts):
                sp.sem_clear(range(first, last + 1))

        @block.scalar
        def _(act):
            act.nop()

        @block.vector
        def _(dve):
            dve.nop()

        @block.gpsimd
        def _(pool):
            pool.nop()

        @block.tensor
        def _(pe):
            pe.nop()


def segment_kernel(nc, x, ids, dst_ext, edge_t, W0, b0, W1m, W1e, W1r, b1, W2m, W2e, W2r, b2, Wg, bg,
                   Wa, att_s, att_d, ba, out):
    ctx = ExitStack()
    with ctx:
        def sb(name, shape, dt=F32):
            return ctx.enter_context(nc.sbuf_tensor(name, shape, dt))

        dram = lambda name, shape, dt=F32: nc.dram_tensor(name, shape, dt).ap()
        xa = dram("xa", (NP, XW))
        xd = dram("xd", (EP, D))
        mask_d = dram("mask_d", (1, EP), BF16)
        restart_d = dram("restart_d", (1, EP), BF16)
        next_d = dram("next_d", (1, EP))
        scat_d = dram("scat_d", (1, EP), I32)
        src_rows = dram("src_rows", (NCH, 128, Q), I32)
        t1 = dram("t1", (ROWS, D))
        tc = dram("tc", (ROWS, D))
        tcT = dram("tcT", (D, EP))
        t2 = dram("t2", (ROWS, D))
        t3 = dram("t3", (ROWS, D))
        ad_d = dram("ad_d", (1, EP))
        ads_d = dram("ads_d", (1, EP))

        ident = sb("ident", [128, 128])
        eps = sb("eps", [128, 1])

        gathered, gathered_own, gathered_a, gathered_b, gathered_2, gathered_3, scattered = (
            [ctx.enter_context(nc.semaphore(f"{n}{u}")) for u in range(2)]
            for n in ("l0_gathered", "dg_gathered", "l1a_gathered", "l1b_gathered", "l2_gathered",
                      "l3_gathered", "l3_scattered"))

        degrees(nc, x, ids, dst_ext, xa, xd, mask_d, restart_d, next_d, scat_d, ident, eps, gathered_own)
        layer0(nc, x, ids, xa, xd, src_rows, t1, tc, W0, b0, W1r, b1, mask_d, ident, eps, gathered)
        layer1(nc, "a", t1, t1, tc, tcT, src_rows, edge_t, W1m, W1e, W1r, b1, restart_d, ident, eps,
               gathered_a, node=(tc, t1, t2, W2r, b2))
        layer1(nc, "b", tc, t1, t2, tcT, src_rows, edge_t, W2m, W2e, W2r, b2, restart_d, ident, eps,
               gathered_b, node=(t2, t2, t3, Wg, bg))
        layer2(nc, t2, t3, src_rows, ad_d, Wg, bg, Wa, att_d, restart_d, ident, eps,
               gathered_2, node=(t3, out, Wa, ba))
        spread(nc, ad_d, next_d, ads_d, ident)
        layer3(nc, t3, src_rows, scat_d, ads_d, restart_d, out, Wa, att_s, att_d, ba, ident, eps,
               gathered_3, scattered)


def degrees(nc, x, ids, dst_ext, xa, xd, mask_d, restart_d, next_d, scat_d, ident, eps, gathered):
    ctx, sems = ExitStack(), ExitStack()
    with sems, ctx:
        def sb(name, shape, dt=F32):
            return ctx.enter_context(nc.sbuf_tensor(name, shape, dt))

        used = []

        def sem(name):
            used.append(sems.enter_context(nc.semaphore("dg_" + name)))
            return used[-1]

        idall = sb("idall", [128, NCH, 2 * Q], I32)
        shifted = sb("shifted", [128, NCH, 2 * Q], I32)
        hi = sb("hi", [128, NCH, 2 * Q], BF16)
        lo = sb("lo", [128, NCH, 2 * Q])
        iota_lo = sb("iota_lo", [128, LO], F16)
        iota_hi = sb("iota_hi", [128, HI], BF16)
        hot_lo = sb("hot_lo", [128, 2, 2 * Q, LO], BF16)
        hot_hi = sb("hot_hi", [128, 2, 2 * Q, HI], BF16)
        zero = sb("zero", [128, LO], BF16)
        before = sb("before", [HI, HI])
        nid = sb("nid", [HI, LO])
        ends = sb("ends", [HI, LO])
        offs = sb("offs", [HI, 1])
        has = sb("has", [HI, 2, LO])
        root = sb("root", [HI, LO])
        fac = sb("fac", [HI, LO, 2])
        idx = sb("idx", [128, 2, 2 * Q], I32)
        G = sb("G", [128, 2, Q, D])
        dprev = sb("dprev", [128, J], I32)
        dcur = sb("dcur", [128, J], I32)
        dnext = sb("dnext", [128, J], I32)
        same = sb("same", [128, J], BF16)
        restart = sb("restart", [128, J], BF16)
        same_next = sb("same_next", [128, J])
        scat = sb("scat", [128, J], I32)
        counts = ctx.enter_context(nc.psum_tensor("counts", [128, 2, LO], F32))
        off_ps = ctx.enter_context(nc.psum_tensor("off_ps", [128, LO], F32))

        ids_in = sem("ids_in")
        dst_in = sem("dst_in")
        x_out = sem("x_out")
        info_out = sem("info_out")
        consts = sem("consts")
        id_zero = sem("id_zero")
        split = sem("split")
        hot_ready = sem("hot_ready")
        counted = sem("counted")
        totals = sem("totals")
        offsets = sem("offsets")
        rooted_in = sem("rooted_in")
        rooted = sem("rooted")
        facs = sem("facs")
        flags = sem("flags")
        flags_out = sem("flags_out")
        idx_in = [sem("idx_in0"), sem("idx_in1")]
        own_out = [sem("own_out0"), sem("own_out1")]
        block = ctx.enter_context(nc.Block())
        flat = lambda at: dst_ext[at:at + EP].rearrange("(p j) -> p j", p=128)

        @block.sync
        def _(sp):
            def indices(c, i, u, warm):
                if warm:
                    wait(sp, gathered[u], 128 * i)
                sp.dma_start(idx[:, u, :], one(ids, c)).then_inc(idx_in[u], 16)

            def copy(c, i, u, warm):
                rows = slice(c * CH, (c + 1) * CH) if isinstance(c, int) else bass.ds(c * CH, CH)
                sp.dma_start(xa[rows, 0:D], x[rows, :]).then_inc(x_out, 16)

            def own(c, i, u, warm):
                wait(sp, gathered[u], 128 * (i + 1))
                sp.dma_start(rows_of(xd, c), halves(G[:, u, :, :])).then_inc(own_out[u], 16)
            chunks(sp, (indices, 0), (copy, 0), (own, 1))
            sp.wait_ge(x_out, 16 * NCH)
            for u in range(2):
                sp.wait_ge(own_out[u], 16 * (NCH // 2 + 1 - u))

        @block.gpsimd
        def _(pool):
            pool.iota(iota_lo[:, :], [[1, LO]], base=0, channel_multiplier=0,
                      allow_small_or_imprecise_dtypes=True).then_inc(consts, 1)
            pool.iota(iota_hi[:, :], [[1, HI]], base=0, channel_multiplier=0,
                      allow_small_or_imprecise_dtypes=True).then_inc(consts, 1)
            pool.iota(nid[:, :], [[1, LO]], base=EP, channel_multiplier=LO,
                      allow_small_or_imprecise_dtypes=True).then_inc(consts, 1)
            pool.memset(ident[:, :], 0.0).then_inc(id_zero, 1)
            pool.memset(before[:, :], 1.0).then_inc(id_zero, 1)
            pool.wait_ge(id_zero, 2)
            pool.affine_select(out=ident[:, :], in_=ident[:, :], compare_op=ALU.not_equal, fill=1.0,
                               base=0, pattern=[[-1, 128]], channel_multiplier=1).then_inc(consts, 1)
            pool.affine_select(out=before[:, :], in_=before[:, :], compare_op=ALU.is_gt, fill=0.0,
                               base=0, pattern=[[1, HI]], channel_multiplier=-1).then_inc(consts, 1)

            def head(c, i, u, warm):
                wait(pool, idx_in[u], 16 * (i + 1))
                if warm:
                    wait(pool, own_out[u], 16 * i)
                gather(pool, G, u, x, idx[:, :, Q:2 * Q], gathered)
            chunks(pool, (head, 0))

        @block.vector
        def _(dve):
            dve.memset(zero[:, :], 0.0)
            dve.memset(eps[:, :], LN_EPS)
            dve.wait_ge(ids_in, 16)
            dve.tensor_scalar(shifted[:, :, :], idall[:, :, :], 9, None, ALU.logical_shift_right)
            dve.drain()
            dve.tensor_copy(hi[:, :, :], shifted[:, :, :]).then_inc(split, 1)
            dve.drain()
            dve.tensor_scalar(shifted[:, :, :], idall[:, :, :], LO - 1, None, ALU.bitwise_and)
            dve.drain()
            dve.tensor_copy(lo[:, :, :], shifted[:, :, :]).then_inc(split, 1)
            dve.drain()
            dve.wait_ge(dst_in, 48)
            dve.tensor_tensor(same[:, :], dcur[:, :], dprev[:, :], ALU.is_equal).then_inc(flags, 1)
            dve.tensor_tensor(same_next[:, :], dcur[:, :], dnext[:, :], ALU.is_equal).then_inc(flags, 1)
            dve.drain()
            dve.scalar_tensor_tensor(scat[:, :], same_next[:, :], float(FAR), dcur[:, :],
                                     ALU.mult, ALU.add).then_inc(flags, 1)
            dve.tensor_scalar(restart[:, :], same[:, :], -1.0, BIG, ALU.add, ALU.mult).then_inc(flags, 1)
            dve.wait_ge(consts, 5)

            def head(c, i, u, warm):
                if warm:
                    dve.wait_ge(counted, c)
                for q in range(2 * Q):
                    l = lo[:, c, q:q + 1] if isinstance(c, int) else \
                        lo[:, bass.ds(c, 1), q:q + 1].rearrange("p a q -> p (a q)")
                    dve.tensor_scalar(hot_lo[:, u, q, :], iota_lo[:, :], l, None, ALU.is_equal)
                h = hi[:, c:c + 1, :] if isinstance(c, int) else hi[:, bass.ds(c, 1), :]
                h = h.rearrange("p a q -> p (a q)").unsqueeze(2).to_broadcast([128, 2 * Q, HI])
                dve.tensor_tensor(hot_hi[:, u, :, :], h,
                                  iota_hi[:, :].unsqueeze(1).to_broadcast([128, 2 * Q, HI]),
                                  ALU.is_equal).then_inc(hot_ready, 1)
            chunks(dve, (head, 0))

            dve.wait_ge(counted, NCH + 1)
            dve.tensor_scalar(root[:, :], counts[0:HI, 0, :], 1.0, None, ALU.max).then_inc(rooted_in, 1)
            dve.tensor_scalar(has[:, :, :], counts[0:HI, :, :], 0.0, None, ALU.is_gt)
            dve.drain()
            dve.tensor_tensor_scan(ends[:, :], zero[0:HI, :], counts[0:HI, 1, :], 0.0,
                                   ALU.add, ALU.add).then_inc(totals, 1)
            dve.wait_ge(offsets, 1)
            dve.tensor_scalar(offs[:, :], off_ps[0:HI, 0:1], -1.0, None, ALU.add)
            dve.drain()
            dve.scalar_tensor_tensor(ends[:, :], ends[:, :], offs[:, 0:1], nid[:, :],
                                     ALU.add, ALU.subtract)
            dve.drain()
            dve.tensor_tensor(ends[:, :], ends[:, :], has[:, 1, :], ALU.mult)
            dve.drain()
            dve.tensor_tensor(fac[:, :, 0], ends[:, :], nid[:, :], ALU.add).then_inc(facs, 1)
            dve.wait_ge(rooted, 1)
            dve.reciprocal(root[:, :], root[:, :])
            dve.drain()
            dve.tensor_tensor(fac[:, :, 1], root[:, :], has[:, 0, :], ALU.mult).then_inc(facs, 1)

        @block.scalar
        def _(act):
            act.dma_start(idall[:, :, :], ids.rearrange("c p q -> p c q")).then_inc(ids_in, 16)
            act.dma_start(dprev[:, :], flat(0)).then_inc(dst_in, 16)
            act.dma_start(dcur[:, :], flat(1)).then_inc(dst_in, 16)
            act.dma_start(dnext[:, :], flat(2)).then_inc(dst_in, 16)
            act.wait_ge(flags, 4)
            act.dma_start(restart_d.rearrange("a (p j) -> (a p) j", p=128), restart[:, :])\
              .then_inc(flags_out, 16)
            act.dma_start(mask_d.rearrange("a (p j) -> (a p) j", p=128), same[:, :]).then_inc(flags_out, 16)
            act.dma_start(next_d.rearrange("a (p j) -> (a p) j", p=128), same_next[:, :])\
              .then_inc(flags_out, 16)
            act.dma_start(scat_d.rearrange("a (p j) -> (a p) j", p=128), scat[:, :])\
              .then_inc(flags_out, 16)
            act.wait_ge(rooted_in, 1)
            act.activation(root[:, :], root[:, :], ACT.Sqrt).then_inc(rooted, 1)
            act.wait_ge(facs, 2)
            act.dma_start(xa[:, D:XW].rearrange("(h l) k -> h l k", l=LO), fac[:, :, :])\
               .then_inc(info_out, 16)
            act.wait_ge(info_out, 16)
            act.wait_ge(flags_out, 64)

        @block.tensor
        def _(pe):
            pe.wait_ge(consts, 5)
            pe.wait_ge(split, 2)
            for k in range(2):
                last = pe.matmul(counts[0:HI, k, :], zero[:, 0:HI], zero[:, :], start=True, stop=False,
                                 skip_group_check=True)
            last.then_inc(counted, 1)

            def head(c, i, u, warm):
                pe.wait_ge(hot_ready, c + 1)
                for q in range(2 * Q):
                    last = pe.matmul(counts[0:HI, q // Q, :], hot_hi[:, u, q, :], hot_lo[:, u, q, :],
                                     start=False, stop=False, skip_group_check=True)
                last.then_inc(counted, 1)
            chunks(pe, (head, 0))
            pe.wait_ge(totals, 1)
            pe.matmul(off_ps[0:HI, 0:1], before[:, :], ends[:, LO - 1:LO], start=True, stop=True)\
              .then_inc(offsets, 1)
        ctx.close()
        clear(nc, used)


def norm_stats(dve, tiles, st, mv, u, done):
    for k, t in enumerate(tiles):
        dve.bn_stats(st[:, k, :], t)
    dve.drain()
    for k in range(len(tiles)):
        last = dve.bn_aggr(mv[:, u, k, :], st[:, k, :])
    last.then_inc(done, 1)


def norm_factors(dve, mv, rstd, shift, u, done):
    dve.reciprocal(rstd[:, u, :], rstd[:, u, :])
    dve.drain()
    dve.scalar_tensor_tensor(shift[:, u, :], mv[:, u, :, 0], -1.0, rstd[:, u, :], ALU.mult, ALU.mult)\
       .then_inc(done, 1)


def norm_apply(act, tiles, outs, rstd, shift, u):
    for k, (t, o) in enumerate(zip(tiles, outs)):
        last = act.activation(o, t, ACT.Identity, bias=shift[:, u, k:k + 1], scale=rstd[:, u, k:k + 1])
    return last


def gather(pool, tile, u, table, idx, done):
    for q in range(Q):
        pool.indirect_dma_start(tile[:, u, q, :], None, table,
                                bass.IndirectOffsetOnAxis(idx[:, u, q:q + 1], 0)).then_inc(done[u], 16)


def turn(pe, psum, tile, ident, by_edge):
    for q in range(Q):
        to = psum[0:D, tile_columns(q)] if by_edge else psum[0:D, q * 128:(q + 1) * 128]
        last = pe.transpose(to, tile[:, q, :], ident[:, :])
    return last


def layer0(nc, x, ids, xa, xd, src_rows, t1, tc, W0, b0, W1r, b1, mask_d, ident, eps, gs_in):
    ctx, sems = ExitStack(), ExitStack()
    with sems, ctx:
        def sb(name, shape, dt=F32):
            return ctx.enter_context(nc.sbuf_tensor("l0_" + name, shape, dt))

        def ps(name):
            return ctx.enter_context(nc.psum_tensor("l0_" + name, [128, 2 * 512], F32))

        used = []

        def sem(name):
            used.append(sems.enter_context(nc.semaphore("l0_" + name)))
            return used[-1]

        w0 = sb("w0", [D + 1, D + 1])
        wr = sb("wr", [D + 1, D])
        b0r = sb("b0r", [128, D])
        idx = sb("idx", [128, 2, 2 * Q], I32)
        gs = sb("gs", [128, 2, Q, XW])
        xd_in = sb("xd_in", [128, 2, Q, D])
        xn = sb("xn", [128, 2, Q, D])
        y = sb("y", [128, 2, Q, D + 1])
        S = sb("S", [D + 1, 2, CH])
        mask = sb("mask", [D + 1, 2, CH], BF16)
        inv_in = sb("inv_in", [128, Q])
        st = sb("st", [128, 2 * Q, 6])
        mv = sb("mv", [128, 2, 2 * Q, 2])
        rstd = sb("rstd", [128, 2, 2 * Q])
        shift = sb("shift", [128, 2, 2 * Q])
        xe_out = sb("xe_out", [128, 2, Q, D])
        xn_out = sb("xn_out", [128, 2, Q, D])
        cn_out = sb("cn_out", [128, 2, Q, D])
        cn_small = sb("cn_small", [128, Q, D])
        row_out = sb("row_out", [128, 2, Q], I32)
        xnT = sb("xnT", [D + 1, CH])
        psT, psA, psX, psN = ps("psT"), ps("psA"), ps("psX"), ps("psN")
        A = psA[:, :].rearrange("p (q d) -> p q d", q=Q)
        N = psN[:, :].rearrange("p (q d) -> p q d", q=Q)

        ready = sem("ready")
        scaled = sem("scaled")
        turned = sem("turned")
        scanned = sem("scanned")
        multiplied = sem("multiplied")
        counted = sem("counted")
        summed_n = sem("summed_n")
        summed_e = sem("summed_e")
        measured = sem("measured")
        rooted = sem("rooted")
        factored = sem("factored")
        normed = sem("normed")
        turned_n = sem("turned_n")
        copied_n = sem("copied_n")
        rooted_n = sem("rooted_n")
        small_n = sem("small_n")
        conv_n = sem("conv_n")
        weights = sem("weights")
        idx_in = [sem("idx_in0"), sem("idx_in1")]
        mask_in = [sem("mask_in0"), sem("mask_in1")]
        xn_in = [sem("xn_in0"), sem("xn_in1")]
        stored = [sem("stored0"), sem("stored1")]
        stored_n = [sem("stored_n0"), sem("stored_n1")]
        rows_stored = [sem("rows_stored0"), sem("rows_stored1")]

        def tiles_of(u):
            return [xn_out[:, u, q, :] for q in range(Q)] + [xe_out[:, u, q, :] for q in range(Q)]

        block = ctx.enter_context(nc.Block())

        @block.sync
        def _(sp):
            sp.dma_start(w0[0:D, 0:D], W0).then_inc(weights, 16)
            sp.dma_start(wr[0:D, :], W1r).then_inc(weights, 16)
            sp.dma_start(wr[D:D + 1, :], b1).then_inc(weights, 16)
            sp.dma_start(b0r[:, :], b0.to_broadcast([128, D])).then_inc(weights, 16)

            def indices(c, i, u, warm):
                if warm:
                    wait(sp, gs_in[u], 128 * i)
                sp.dma_start(idx[:, u, :], one(ids, c)).then_inc(idx_in[u], 16)

            def head(c, i, u, warm):
                if warm:
                    wait(sp, scanned, c - 1)
                sp.dma_start(mask[:, u, :], span(mask_d, c, CH).to_broadcast([D + 1, CH]))\
                  .then_inc(mask_in[u], 16)
                if warm:
                    wait(sp, summed_n, c - 1)
                sp.dma_start(halves(xn[:, u, :, :]), rows_of(x, c))\
                  .then_inc(xn_in[u], 16)
                if warm:
                    wait(sp, summed_e, c - 1)
                sp.dma_start(halves(xd_in[:, u, :, :]), rows_of(xd, c)).then_inc(xn_in[u], 16)

            def tail(c, i, u, warm):
                wait(sp, normed, c + 1)
                sp.dma_start(rows_of(t1, c, EP), halves(xn_out[:, u, :, :]))\
                  .then_inc(stored[u], 16)
                sp.dma_start(rows_of(t1, c), halves(xe_out[:, u, :, :]))\
                  .then_inc(stored[u], 16)

            def rows(c, i, u, warm):
                wait(sp, scaled, c + 1)
                sp.dma_start(one(src_rows, c), row_out[:, u, :]).then_inc(rows_stored[u], 16)

            def last(c, i, u, warm):
                wait(sp, conv_n, c + 1)
                sp.dma_start(rows_of(tc, c, EP), halves(cn_out[:, u, :, :]))\
                  .then_inc(stored_n[u], 16)
            chunks(sp, (indices, 0), (head, 1), (rows, 2), (tail, 4), (last, 6))
            for u in range(2):
                sp.wait_ge(rows_stored[u], 16 * (NCH // 2 + 1 - u))
                sp.wait_ge(stored[u], 32 * (NCH // 2 + 1 - u))
                sp.wait_ge(stored_n[u], 16 * (NCH // 2 + 1 - u))

        @block.gpsimd
        def _(pool):
            def head(c, i, u, warm):
                wait(pool, idx_in[u], 16 * (i + 1))
                if warm:
                    wait(pool, scaled, c - 1)
                for q in range(Q):
                    pool.indirect_dma_start(gs[:, u, q, :], None, xa,
                                            bass.IndirectOffsetOnAxis(idx[:, u, q:q + 1], 0))\
                        .then_inc(gs_in[u], 16)
            chunks(pool, (head, 0))

        @block.vector
        def _(dve):
            dve.memset(S[:, 1, CH - 1:CH], 0.0)
            dve.memset(y[:, :, :, D:D + 1], 1.0)
            dve.memset(w0[D:D + 1, 0:D], 0.0)
            dve.memset(w0[0:D, D:D + 1], 0.0)
            dve.memset(w0[D:D + 1, D:D + 1], 1.0)
            dve.memset(xnT[D:D + 1, :], 1.0).then_inc(ready, 1)
            dve.wait_ge(weights, 64)

            def scale(c, i, u, warm):
                dve.wait_ge(gs_in[u], 128 * (i + 1))
                if warm:
                    dve.wait_ge(turned, c - 1)
                    dve.wait_ge(rows_stored[u], 16 * i)
                dve.tensor_copy(row_out[:, u, :], gs[:, u, :, POS])
                dve.tensor_tensor(y[:, u, :, 0:D], gs[:, u, :, 0:D],
                                  gs[:, u, :, INV_OUT:INV_OUT + 1].to_broadcast([128, Q, D]),
                                  ALU.mult).then_inc(scaled, 1)

            def scan(c, i, u, warm):
                dve.wait_ge(turned, c + 1)
                dve.wait_ge(mask_in[u], 16 * (i + 1))
                if warm:
                    dve.wait_ge(multiplied, c - 1)
                dve.tensor_tensor_scan(S[:, u, :], mask[:, u, :], psT[0:D + 1, :],
                                       S[:, 1 - u, CH - 1:CH], ALU.mult, ALU.add).then_inc(scanned, 1)

            def stats(c, i, u, warm):
                dve.wait_ge(xn_in[u], 32 * (i + 1))
                if warm:
                    dve.wait_ge(stored[u], 32 * i)
                    dve.wait_ge(turned_n, c - 1)
                dve.tensor_tensor(xn_out[:, u, :, :], xn[:, u, :, :],
                                  b0r[:, :].unsqueeze(1).to_broadcast([128, Q, D]), ALU.add)\
                   .then_inc(summed_n, 1)
                dve.wait_ge(counted, c + 1)
                dve.reciprocal(inv_in[:, :], inv_in[:, :])
                dve.drain()
                dve.wait_ge(multiplied, c + 1)
                for q in range(Q):
                    dve.scalar_tensor_tensor(xe_out[:, u, q, :], A[:, q, 0:D],
                                             inv_in[:, q:q + 1], xd_in[:, u, q, :],
                                             ALU.mult, ALU.add)
                dve.drain()
                dve.tensor_tensor(xe_out[:, u, :, :], xe_out[:, u, :, :],
                                  b0r[:, :].unsqueeze(1).to_broadcast([128, Q, D]), ALU.add)\
                   .then_inc(summed_e, 1)
                dve.drain()
                norm_stats(dve, tiles_of(u), st, mv, u, measured)

            def factors(c, i, u, warm):
                dve.wait_ge(rooted, c + 1)
                norm_factors(dve, mv, rstd, shift, u, factored)

            def leaky(c, i, u, warm):
                dve.wait_ge(small_n, c + 1)
                if warm:
                    dve.wait_ge(stored_n[u], 16 * i)
                dve.tensor_tensor(cn_out[:, u, :, :], N[:, :, 0:D], cn_small[:, :, :], ALU.max)\
                   .then_inc(conv_n, 1)
            chunks(dve, (scan, 1), (scale, 0), (factors, 2), (leaky, 4), (stats, 1))

        @block.scalar
        def _(act):
            act.wait_ge(ready, 1)

            def tail(c, i, u, warm):
                act.wait_ge(measured, c + 1)
                act.activation(rstd[:, u, :], mv[:, u, :, 1], ACT.Sqrt, bias=eps[:, :]).then_inc(rooted, 1)

            def copy_nodes(c, i, u, warm):
                act.wait_ge(turned_n, c + 1)
                if warm or c == 1:
                    act.wait_ge(rooted_n, c)
                act.activation(xnT[0:D, :], psX[0:D, :], ACT.Copy).then_inc(copied_n, 1)

            def last(c, i, u, warm):
                if warm or c == 1:
                    act.wait_ge(conv_n, c)
                act.wait_ge(rooted_n, c + 1)
                act.activation(cn_small[:, :, :], N[:, :, 0:D], ACT.Copy, scale=LEAK)\
                   .then_inc(small_n, 1)

            def apply(c, i, u, warm):
                act.wait_ge(factored, c + 1)
                norm_apply(act, tiles_of(u), tiles_of(u), rstd, shift, u).then_inc(normed, 1)

            def count(c, i, u, warm):
                act.wait_ge(multiplied, c + 1)
                if warm or c == 1:
                    act.wait_ge(summed_e, c)
                act.activation(inv_in[:, :], A[:, :, D], ACT.Sqrt).then_inc(counted, 1)
            chunks(act, (tail, 2), (copy_nodes, 3), (count, 1), (apply, 2), (last, 3))

        @block.tensor
        def _(pe):
            pe.wait_ge(weights, 64)
            pe.wait_ge(ready, 1)

            def head(c, i, u, warm):
                pe.wait_ge(scaled, c + 1)
                if warm or c == 1:
                    pe.wait_ge(scanned, c)
                for q in range(Q):
                    last = pe.transpose(psT[0:D + 1, tile_columns(q)], y[:, u, q, :], ident[:, :])
                last.then_inc(turned, 1)

            def tail(c, i, u, warm):
                pe.wait_ge(scanned, c + 1)
                if warm or c == 1:
                    pe.wait_ge(summed_e, c)
                for q in range(Q):
                    last = pe.matmul(A[:, q, 0:D + 1], S[:, u, tile_columns(q)], w0[:, :],
                                     start=True, stop=True)
                last.then_inc(multiplied, 1)

            def turn_nodes(c, i, u, warm):
                pe.wait_ge(normed, c + 1)
                if warm or c == 1:
                    pe.wait_ge(copied_n, c)
                turn(pe, psX, xn_out[:, u, :, :], ident, False).then_inc(turned_n, 1)

            def root(c, i, u, warm):
                pe.wait_ge(copied_n, c + 1)
                if warm or c == 1:
                    pe.wait_ge(conv_n, c)
                for q in range(Q):
                    last = pe.matmul(N[:, q, 0:D], xnT[:, q * 128:(q + 1) * 128], wr[:, :],
                                     start=True, stop=True)
                last.then_inc(rooted_n, 1)
            chunks(pe, (turn_nodes, 3), (tail, 1), (head, 0), (root, 3))
        ctx.close()
        clear(nc, used)


def layer1(nc, name, table, own, to, ownT, src_rows, edge_t, Wm, We, Wr, b, restart_d,
           ident, eps, gathered, node):
    first = name == "a"
    n_rows, n_res, n_to, Wn, bn = node
    LOADS = 4
    ctx, sems = ExitStack(), ExitStack()
    with sems, ctx:
        def sb(tag, shape, dt=F32):
            return ctx.enter_context(nc.sbuf_tensor(f"l1{name}_{tag}", shape, dt))

        def ps(tag):
            return ctx.enter_context(nc.psum_tensor(f"l1{name}_{tag}", [128, 2 * 512], F32))

        used = []

        def sem(tag):
            used.append(sems.enter_context(nc.semaphore(f"l1{name}_{tag}")))
            return used[-1]

        wme = sb("wme", [D + DE, D])
        wr = sb("wr", [D + 1, D])
        wn = sb("wn", [D + 1, D])
        idx = sb("idx", [128, 2, Q], I32)
        G = sb("G", [128, 2, Q, D])
        xs = sb("xs", [128, 2, Q, D])
        res = sb("res", [128, 2, Q, D])
        xn = sb("xn", [128, 2, Q, D])
        geT = sb("geT", [D + DE, 2, CH])
        xT = sb("xT", [D + 1, 2, CH])
        nT = sb("nT", [D + 1, CH])
        restart = sb("restart", [D, 2, CH], BF16)
        S = sb("S", [D, 2, CH])
        z = sb("z", [D, CH])
        conv = sb("conv", [D, 2, CH])
        e_out = sb("e_out", [128, 2, Q, D])
        n_out = sb("n_out", [128, 2, Q, D])
        normal = sb("normal", [128, 2, 1 if first else 2, Q, D])
        NT = Q if first else 2 * Q
        st = sb("st", [128, NT, 6])
        mv = sb("mv", [128, 2, NT, 2])
        rstd = sb("rstd", [128, 2, NT])
        shift = sb("shift", [128, 2, NT])
        psT, psA, psX, psN = ps("psT"), ps("psA"), ps("psX"), ps("psN")
        A = psA[:, :].rearrange("p (q d) -> p q d", q=Q)
        N = psN[:, :].rearrange("p (q d) -> p q d", q=Q)

        weights = sem("weights")
        ready = sem("ready")
        idx_in = [sem("idx_in0"), sem("idx_in1")]
        rows_in = [sem("rows_in0"), sem("rows_in1")]
        res_in = [sem("res_in0"), sem("res_in1")]
        stored = [sem("stored0"), sem("stored1")]
        kept = [sem("kept0"), sem("kept1")]
        turned = sem("turned")
        turned_x = sem("turned_x")
        turned_n = sem("turned_n")
        copied = sem("copied")
        copied_x = sem("copied_x")
        copied_n = sem("copied_n")
        messages = sem("messages")
        own_ready = sem("own_ready")
        rooted_n = sem("rooted_n")
        scanned = sem("scanned")
        added = sem("added")
        leaked = sem("leaked")
        returned = sem("returned")
        taken = sem("taken")
        noded = sem("noded")
        summed = sem("summed")
        measured = sem("measured")
        rooted = sem("rooted")
        factored = sem("factored")
        normed = sem("normed")
        STORES = 1 if first else 2

        def tiles_of(u):
            tiles = [n_out[:, u, q, :] for q in range(Q)]
            return tiles if first else tiles + [e_out[:, u, q, :] for q in range(Q)]

        block = ctx.enter_context(nc.Block())

        @block.sync
        def _(sp):
            for t, w in ((wme[0:D, :], Wm), (wme[D:D + DE, :], We), (wr[0:D, :], Wr), (wr[D:D + 1, :], b),
                         (wn[0:D, :], Wn), (wn[D:D + 1, :], bn)):
                sp.dma_start(t, w).then_inc(weights, 16)

            def indices(c, i, u, warm):
                if warm:
                    wait(sp, gathered[u], 128 * i)
                sp.dma_start(idx[:, u, :], one(src_rows, c)).then_inc(idx_in[u], 16)

            def head(c, i, u, warm):
                if warm:
                    wait(sp, scanned, c - 1)
                    wait(sp, own_ready, c - 1)
                sp.dma_start(restart[:, u, :], span(restart_d, c, CH).to_broadcast([D, CH]))\
                  .then_inc(rows_in[u], 16)
                sp.dma_start(geT[D:D + DE, u, :], span(edge_t, c, CH)).then_inc(rows_in[u], 16)
                if first:
                    sp.dma_start(halves(xs[:, u, :, :]), rows_of(own, c)).then_inc(rows_in[u], 16)
                else:
                    sp.dma_start(xT[0:D, u, :], span(ownT, c, CH)).then_inc(rows_in[u], 16)
                if warm:
                    wait(sp, turned_n, c - 1)
                sp.dma_start(halves(xn[:, u, :, :]), rows_of(n_rows, c, EP)).then_inc(rows_in[u], 16)

            def residual(c, i, u, warm):
                if warm:
                    wait(sp, summed, c - 1)
                rows = rows_of(n_res, c, EP) if first else rows_of(own, c)
                sp.dma_start(halves(res[:, u, :, :]), rows).then_inc(res_in[u], 16)

            def keep(c, i, u, warm):
                wait(sp, leaked, c + 1)
                sp.dma_start(span(ownT, c, CH), conv[:, u, :]).then_inc(kept[u], 16)
                wait(sp, taken, c + 1)
                sp.dma_start(rows_of(to, c), halves(e_out[:, u, :, :])).then_inc(kept[u], 16)

            def tail(c, i, u, warm):
                wait(sp, normed, c + 1)
                sp.dma_start(rows_of(n_to, c, EP), halves(normal[:, u, 0, :, :])).then_inc(stored[u], 16)
                if not first:
                    sp.dma_start(rows_of(to, c), halves(normal[:, u, 1, :, :])).then_inc(stored[u], 16)
            if first:
                chunks(sp, (indices, 0), (head, 1), (residual, 1), (keep, 3), (tail, 4))
            else:
                chunks(sp, (indices, 0), (head, 1), (residual, 1), (tail, 4))
            for u in range(2):
                sp.wait_ge(stored[u], 16 * STORES * (NCH // 2 + 1 - u))
                if first:
                    sp.wait_ge(kept[u], 32 * (NCH // 2 + 1 - u))

        @block.gpsimd
        def _(pool):
            def head(c, i, u, warm):
                wait(pool, idx_in[u], 16 * (i + 1))
                if warm:
                    wait(pool, turned, c - 1)
                gather(pool, G, u, table, idx, gathered)
            chunks(pool, (head, 0))

        @block.vector
        def _(dve):
            dve.memset(S[:, 1, CH - 1:CH], 0.0)
            dve.memset(nT[D:D + 1, :], 1.0)
            dve.memset(xT[D:D + 1, :, :], 1.0).then_inc(ready, 1)
            dve.wait_ge(weights, 96)
            if not first:
                dve.tensor_tensor(wn[0:D, :], wn[0:D, :], ident[0:D, 0:D], ALU.add)
            dve.drain().then_inc(ready, 1)

            def head(c, i, u, warm):
                dve.wait_ge(rows_in[u], 16 * LOADS * (i + 1))
                dve.wait_ge(messages, c + 1)
                dve.tensor_tensor_scan(S[:, u, :], restart[:, u, :], psT[0:D, :], S[:, 1 - u, CH - 1:CH],
                                       ALU.add, ALU.max).then_inc(scanned, 1)
                dve.drain()
                dve.wait_ge(own_ready, c + 1)
                dve.tensor_tensor(z[:, :], S[:, u, :], psX[0:D, :], ALU.add).then_inc(added, 1)
                dve.drain()
                if warm:
                    dve.wait_ge(returned, c - 1)
                    if first:
                        dve.wait_ge(kept[u], 32 * i)
                dve.scalar_tensor_tensor(conv[:, u, :], z[:, :], LEAK, z[:, :], ALU.mult, ALU.max)\
                   .then_inc(leaked, 1)

            def stats(c, i, u, warm):
                dve.wait_ge(res_in[u], 16 * (i + 1))
                if warm and not first:
                    dve.wait_ge(normed, c - 1)
                dve.wait_ge(noded, c + 1)
                if first:
                    dve.scalar_tensor_tensor(n_out[:, u, :, :], n_out[:, u, :, :], LEAK,
                                             n_out[:, u, :, :], ALU.mult, ALU.max)
                    dve.drain()
                    dve.tensor_tensor(n_out[:, u, :, :], n_out[:, u, :, :], res[:, u, :, :], ALU.add)\
                       .then_inc(summed, 1)
                else:
                    dve.wait_ge(returned, c + 1)
                    dve.tensor_tensor(e_out[:, u, :, :], A[:, :, 0:D], res[:, u, :, :], ALU.add)\
                       .then_inc(summed, 1)
                dve.drain()
                norm_stats(dve, tiles_of(u), st, mv, u, measured)

            def factors(c, i, u, warm):
                dve.wait_ge(rooted, c + 1)
                norm_factors(dve, mv, rstd, shift, u, factored)
            chunks(dve, (factors, 2), (stats, 1), (head, 0))

        @block.scalar
        def _(act):
            act.wait_ge(ready, 2)

            def root(c, i, u, warm):
                act.wait_ge(measured, c + 1)
                act.activation(rstd[:, u, :], mv[:, u, :, 1], ACT.Sqrt, bias=eps[:, :]).then_inc(rooted, 1)

            def take(c, i, u, warm):
                act.wait_ge(returned, c + 1)
                if warm:
                    act.wait_ge(kept[u], 32 * i)
                act.activation(e_out[:, u, :, :], A[:, :, 0:D], ACT.Copy).then_inc(taken, 1)

            def head(c, i, u, warm):
                act.wait_ge(turned, c + 1)
                if warm:
                    act.wait_ge(messages, c - 1)
                act.activation(geT[0:D, u, :], psT[0:D, :], ACT.Copy).then_inc(copied, 1)
                act.wait_ge(turned_n, c + 1)
                if warm or c == 1:
                    act.wait_ge(rooted_n, c)
                act.activation(nT[0:D, :], psN[0:D, :], ACT.Copy).then_inc(copied_n, 1)
                if first:
                    act.wait_ge(turned_x, c + 1)
                    if warm:
                        act.wait_ge(own_ready, c - 1)
                    act.activation(xT[0:D, u, :], psX[0:D, :], ACT.Copy).then_inc(copied_x, 1)

            def nodes(c, i, u, warm):
                act.wait_ge(rooted_n, c + 1)
                if warm:
                    act.wait_ge(normed, c - 1)
                act.activation(n_out[:, u, :, :], N[:, :, 0:D], ACT.Copy).then_inc(noded, 1)

            def apply(c, i, u, warm):
                act.wait_ge(factored, c + 1)
                if warm:
                    act.wait_ge(stored[u], 16 * STORES * i)
                norm_apply(act, tiles_of(u), [normal[:, u, q // Q, q % Q, :] for q in range(NT)], rstd,
                           shift, u).then_inc(normed, 1)
            if first:
                chunks(act, (root, 2), (head, 0), (apply, 2), (take, 1), (nodes, 0))
            else:
                chunks(act, (root, 2), (head, 0), (apply, 2), (nodes, 0))

        @block.tensor
        def _(pe):
            pe.wait_ge(weights, 96)
            pe.wait_ge(ready, 2)

            def back(c, i, u, warm):
                pe.wait_ge(leaked, c + 1)
                if warm or c == 1:
                    pe.wait_ge(taken if first else summed, c)
                for q in range(Q):
                    last = pe.transpose(A[:, q, 0:D], conv[:, u, tile_columns(q)], ident[0:D, 0:D])
                last.then_inc(returned, 1)

            def head(c, i, u, warm):
                pe.wait_ge(gathered[u], 128 * (i + 1))
                if warm or c == 1:
                    pe.wait_ge(scanned, c)
                turn(pe, psT, G[:, u, :, :], ident, True).then_inc(turned, 1)
                pe.wait_ge(rows_in[u], 16 * LOADS * (i + 1))
                if warm or c == 1:
                    pe.wait_ge(noded, c)
                turn(pe, psN, xn[:, u, :, :], ident, False).then_inc(turned_n, 1)
                if first:
                    if warm or c == 1:
                        pe.wait_ge(added, c)
                    turn(pe, psX, xs[:, u, :, :], ident, True).then_inc(turned_x, 1)

            def products(c, i, u, warm):
                pe.wait_ge(copied, c + 1)
                for h in range(2):
                    part = slice(h * 512, h * 512 + 512)
                    last = pe.matmul(psT[0:D, part], wme[:, :], geT[:, u, part], start=True, stop=True)
                last.then_inc(messages, 1)
                if first:
                    pe.wait_ge(copied_x, c + 1)
                else:
                    pe.wait_ge(rows_in[u], 16 * LOADS * (i + 1))
                    if warm or c == 1:
                        pe.wait_ge(added, c)
                for h in range(2):
                    part = slice(h * 512, h * 512 + 512)
                    last = pe.matmul(psX[0:D, part], wr[:, :], xT[:, u, part], start=True, stop=True)
                last.then_inc(own_ready, 1)
                pe.wait_ge(copied_n, c + 1)
                for q in range(Q):
                    last = pe.matmul(N[:, q, 0:D], nT[:, q * 128:(q + 1) * 128], wn[:, :],
                                     start=True, stop=True)
                last.then_inc(rooted_n, 1)
            chunks(pe, (head, 0), (back, 1), (products, 0))
        ctx.close()
        clear(nc, used)


def running_softmax(dve, restart, values, R, dd, u, differed):
    dve.tensor_copy(R[:, u, 0:1], R[:, 1 - u, CH:CH + 1])
    dve.drain()
    dve.tensor_tensor_scan(R[:, u, 1:CH + 1], restart, values, R[:, u, 0:1], ALU.add, ALU.max)
    dve.drain()
    dve.tensor_tensor(dd[:, 0, :], R[:, u, 0:CH], restart, ALU.add)
    dve.tensor_tensor(dd[:, 1, :], values, R[:, u, 1:CH + 1], ALU.subtract)
    dve.drain()
    dve.tensor_tensor(dd[:, 0, :], dd[:, 0, :], R[:, u, 1:CH + 1], ALU.subtract).then_inc(differed, 1)


def layer2(nc, t2, t3, src_rows, ad_d, Wg, bg, Wa, att_d, restart_d, ident, eps, gathered,
           node):
    n_rows, n_to, Wn, bn = node
    LOADS = 2
    ctx = ExitStack()
    with ctx:
        def sb(tag, shape, dt=F32):
            return ctx.enter_context(nc.sbuf_tensor(f"l2_{tag}", shape, dt))

        def ps(tag):
            return ctx.enter_context(nc.psum_tensor(f"l2_{tag}", [128, 2 * 512], F32))

        def sem(tag):
            return ctx.enter_context(nc.semaphore(f"l2_{tag}"))

        wg = sb("wg", [D, D + 1])
        wx = sb("wx", [D + 1, D + 1])
        wn = sb("wn", [D + 1, D])
        ad = sb("ad", [D, 1])
        v = sb("v", [D, 1])
        v_sum = sb("v_sum", [128, 1])
        wnT = sb("wnT", [D, D])
        wgT = sb("wgT", [D, D])
        wxT = sb("wxT", [D, D + 1])
        eps_col = sb("eps_col", [D, D + 1])
        ones = sb("ones", [D, 128])
        idx = sb("idx", [128, 2, Q], I32)
        G = sb("G", [128, 2, Q, D])
        restart = sb("restart", [D, 2, CH], BF16)
        xs = sb("xs", [128, 2, Q, D])
        xn = sb("xn", [128, 2, Q, D])
        m = sb("m", [D, 2, CH])
        R = sb("R", [D, 2, CH + 1])
        dd = sb("dd", [D, 2, CH])
        P = sb("P", [D, 2, CH])
        S = sb("S", [D, 2, CH])
        T = sb("T", [D, 2, CH])
        inv = sb("inv", [D, 2, CH])
        xT = sb("xT", [D + 1, CH])
        nT = sb("nT", [D + 1, CH])
        e_out = sb("e_out", [128, 2, Q, D])
        n_out = sb("n_out", [128, 2, Q, D])
        normal = sb("normal", [128, 2, 2, Q, D])
        ad_raw = sb("ad_raw", [128, 2, Q])
        ad_part = sb("ad_part", [128, Q])
        ad_out = sb("ad_out", [128, 2, Q])
        st = sb("st", [128, 2 * Q, 6])
        mv = sb("mv", [128, 2, 2 * Q, 2])
        rstd = sb("rstd", [128, 2, 2 * Q])
        shift = sb("shift", [128, 2, 2 * Q])
        psT, psA, psX, psN = ps("psT"), ps("psA"), ps("psX"), ps("psN")
        A = psA[:, :].rearrange("p (q d) -> p q d", q=Q)
        N = psN[:, :].rearrange("p (q d) -> p q d", q=Q)

        weights = sem("weights")
        ready = sem("ready")
        set_up = sem("set_up")
        widened = sem("widened")
        idx_in = [sem("idx_in0"), sem("idx_in1")]
        restart_in = [sem("restart_in0"), sem("restart_in1")]
        rows_in = [sem("rows_in0"), sem("rows_in1")]
        stored = [sem("stored0"), sem("stored1")]
        turned = sem("turned")
        rectified = sem("rectified")
        differed = sem("differed")
        exped = sem("exped")
        totalled = sem("totalled")
        mixed = sem("mixed")
        inverted = sem("inverted")
        averaged = sem("averaged")
        turned_x = sem("turned_x")
        turned_n = sem("turned_n")
        copied_x = sem("copied_x")
        copied_n = sem("copied_n")
        rooted_n = sem("rooted_n")
        tanhed = sem("tanhed")
        multiplied = sem("multiplied")
        taken = sem("taken")
        summed = sem("summed")
        measured = sem("measured")
        rooted = sem("rooted")
        ad_ready = sem("ad_ready")
        factored = sem("factored")
        normed = sem("normed")

        def tiles_of(u):
            return [n_out[:, u, q, :] for q in range(Q)] + [e_out[:, u, q, :] for q in range(Q)]

        block = ctx.enter_context(nc.Block())

        @block.sync
        def _(sp):
            for t, w in ((wg[:, 0:D], Wg), (wx[D:D + 1, 0:D], bg), (wn[0:D, :], Wn), (wn[D:D + 1, :], bn),
                         (ad[:, :], att_d)):
                sp.dma_start(t, w).then_inc(weights, 16)

            def indices(c, i, u, warm):
                if warm:
                    wait(sp, gathered[u], 128 * i)
                sp.dma_start(idx[:, u, :], one(src_rows, c)).then_inc(idx_in[u], 16)

            def head(c, i, u, warm):
                if warm:
                    wait(sp, differed, c - 1)
                sp.dma_start(restart[:, u, :], span(restart_d, c, CH).to_broadcast([D, CH]))\
                  .then_inc(restart_in[u], 16)

            def rows(c, i, u, warm):
                if warm:
                    wait(sp, turned_n, c - 1)
                    wait(sp, turned_x, c - 1)
                    wait(sp, summed, c - 1)
                sp.dma_start(halves(xn[:, u, :, :]), rows_of(n_rows, c, EP)).then_inc(rows_in[u], 16)
                sp.dma_start(halves(xs[:, u, :, :]), rows_of(t2, c)).then_inc(rows_in[u], 16)

            def tail(c, i, u, warm):
                wait(sp, ad_ready, c + 1)
                wait(sp, normed, c + 1)
                sp.dma_start(rows_of(t3, c), halves(normal[:, u, 1, :, :])).then_inc(stored[u], 16)
                sp.dma_start(rows_of(n_to, c), halves(normal[:, u, 0, :, :])).then_inc(stored[u], 16)
                sp.dma_start(scalars_of(ad_d, c), ad_out[:, u, :].rearrange("p (a r) -> p a r", a=2))\
                  .then_inc(stored[u], 16)
            chunks(sp, (indices, 0), (head, 1), (rows, 3), (tail, 7))
            for u in range(2):
                sp.wait_ge(stored[u], 48 * (NCH // 2 + 1 - u))

        @block.gpsimd
        def _(pool):
            def head(c, i, u, warm):
                wait(pool, idx_in[u], 16 * (i + 1))
                if warm:
                    wait(pool, turned, c - 1)
                gather(pool, G, u, t2, idx, gathered)

            def average(c, i, u, warm):
                wait(pool, inverted, c + 1)
                wait(pool, mixed, c + 1)
                pool.tensor_tensor(inv[:, u, :], T[:, u, :], inv[:, u, :], ALU.mult).then_inc(averaged, 1)

            def residual(c, i, u, warm):
                wait(pool, tanhed, c + 1)
                pool.tensor_tensor(n_out[:, u, :, :], n_out[:, u, :, :], xn[:, u, :, :], ALU.add)\
                    .then_inc(summed, 1)
            chunks(pool, (residual, 4), (average, 2), (head, 0))

        @block.vector
        def _(dve):
            dve.memset(R[:, 1, CH:CH + 1], 0.0)
            dve.memset(S[:, 1, CH - 1:CH], 0.0)
            dve.memset(T[:, 1, CH - 1:CH], 0.0)
            dve.memset(eps_col[:, 0:D], 0.0)
            dve.memset(eps_col[:, D:D + 1], MSG_EPS)
            dve.memset(ones[:, :], 1.0)
            dve.memset(xT[D:D + 1, :], 1.0)
            dve.memset(nT[D:D + 1, :], 1.0)
            dve.wait_ge(weights, 80)
            dve.tensor_tensor(wx[0:D, 0:D], wg[:, 0:D], ident[0:D, 0:D], ALU.add).then_inc(ready, 1)
            dve.wait_ge(set_up, 1)
            dve.tensor_tensor(wx[D:D + 1, 0:D], wx[D:D + 1, 0:D], psA[D:D + 1, 0:D], ALU.add)
            dve.tensor_copy(wnT[:, :], psX[0:D, 0:D])
            dve.tensor_copy(wgT[:, :], psN[0:D, 0:D]).then_inc(widened, 1)
            dve.wait_ge(set_up, 2)
            dve.tensor_copy(v[:, :], psA[0:D, 0:1])
            dve.tensor_copy(wxT[:, :], psX[0:D, 0:D + 1]).then_inc(widened, 1)
            dve.wait_ge(set_up, 3)
            dve.tensor_copy(wg[:, D:D + 1], psA[0:D, 0:1])
            dve.tensor_copy(wx[:, D:D + 1], psX[0:D + 1, 0:1])
            dve.tensor_copy(v_sum[:, :], psN[:, 0:1]).then_inc(widened, 1)
            dve.drain()

            def head(c, i, u, warm):
                dve.wait_ge(restart_in[u], 16 * (i + 1))
                dve.wait_ge(rectified, c + 1)
                running_softmax(dve, restart[:, u, :], m[:, u, :], R, dd, u, differed)

            def stats(c, i, u, warm):
                dve.wait_ge(summed, c + 1)
                dve.wait_ge(taken, c + 1)
                norm_stats(dve, tiles_of(u), st, mv, u, measured)

            def totals(c, i, u, warm):
                dve.wait_ge(exped, c + 1)
                if warm:
                    dve.wait_ge(averaged, c - 1)
                dve.tensor_tensor_scan(S[:, u, :], P[:, 0, :], P[:, 1, :], S[:, 1 - u, CH - 1:CH],
                                       ALU.mult, ALU.add).then_inc(totalled, 1)

            def sums(c, i, u, warm):
                dve.tensor_tensor(P[:, 1, :], P[:, 1, :], m[:, u, :], ALU.mult)
                dve.drain()
                dve.tensor_tensor_scan(T[:, u, :], P[:, 0, :], P[:, 1, :], T[:, 1 - u, CH - 1:CH],
                                       ALU.mult, ALU.add).then_inc(mixed, 1)

            def factors(c, i, u, warm):
                dve.wait_ge(rooted, c + 1)
                dve.scalar_tensor_tensor(shift[:, u, :], mv[:, u, :, 0], -1.0, rstd[:, u, :],
                                         ALU.mult, ALU.mult).then_inc(factored, 1)

            def nodes(c, i, u, warm):
                if warm:
                    dve.wait_ge(stored[u], 48 * i)
                for q in range(Q):
                    dve.tensor_scalar(normal[:, u, 0, q, :], n_out[:, u, q, :], mv[:, u, q, 0:1],
                                      rstd[:, u, q:q + 1], ALU.subtract, ALU.mult)
                dve.tensor_tensor(ad_part[:, :], ad_raw[:, u, :], rstd[:, u, Q:2 * Q], ALU.mult)
                dve.drain()
                dve.scalar_tensor_tensor(ad_out[:, u, :], shift[:, u, Q:2 * Q], v_sum[:, 0:1],
                                         ad_part[:, :], ALU.mult, ALU.add).then_inc(ad_ready, 1)
            chunks(dve, (factors, 5), (head, 1), (nodes, 5), (totals, 1), (stats, 4), (sums, 1))

        @block.scalar
        def _(act):
            act.wait_ge(ready, 1)

            def own(c, i, u, warm):
                act.wait_ge(turned_n, c + 1)
                if warm or c == 1:
                    act.wait_ge(rooted_n, c)
                act.activation(nT[0:D, :], psN[0:D, :], ACT.Copy).then_inc(copied_n, 1)
                act.wait_ge(turned_x, c + 1)
                if warm or c == 1:
                    act.wait_ge(multiplied, c)
                act.activation(xT[0:D, :], psX[0:D, :], ACT.Copy).then_inc(copied_x, 1)

            def exps(c, i, u, warm):
                act.wait_ge(differed, c + 1)
                if warm or c == 1:
                    act.wait_ge(mixed, c)
                act.activation(P[:, :, :], dd[:, :, :], ACT.Exp).then_inc(exped, 1)

            def rectify(c, i, u, warm):
                act.wait_ge(turned, c + 1)
                if warm:
                    act.wait_ge(mixed, c - 1)
                act.activation(m[:, u, :], psT[0:D, :], ACT.Relu).then_inc(rectified, 1)

            def take(c, i, u, warm):
                act.wait_ge(rooted_n, c + 1)
                if warm:
                    act.wait_ge(normed, c - 1)
                    act.wait_ge(ad_ready, c - 1)
                act.activation(n_out[:, u, :, :], N[:, :, 0:D], ACT.Tanh).then_inc(tanhed, 1)
                act.wait_ge(multiplied, c + 1)
                act.activation(ad_raw[:, u, :], A[:, :, D], ACT.Copy)
                act.activation(e_out[:, u, :, :], A[:, :, 0:D], ACT.Copy).then_inc(taken, 1)

            def logs(c, i, u, warm):
                act.wait_ge(totalled, c + 1)
                if warm:
                    act.wait_ge(multiplied, c - 1)
                act.activation(inv[:, u, :], S[:, u, :], ACT.Ln)

            def root_log(c, i, u, warm):
                act.wait_ge(measured, c + 1)
                act.activation(rstd[:, u, :], mv[:, u, :, 1], ACT.Ln, bias=eps[:, :])

            def root(c, i, u, warm):
                act.drain()
                act.activation(rstd[:, u, :], rstd[:, u, :], ACT.Exp, scale=-0.5).then_inc(rooted, 1)

            def invert(c, i, u, warm):
                act.drain()
                act.activation(inv[:, u, :], inv[:, u, :], ACT.Exp, scale=-1.0).then_inc(inverted, 1)

            def apply(c, i, u, warm):
                act.wait_ge(factored, c + 1)
                if warm:
                    act.wait_ge(stored[u], 48 * i)
                norm_apply(act, [e_out[:, u, q, :] for q in range(Q)], [normal[:, u, 1, q, :] for q in range(Q)],
                           rstd[:, :, Q:2 * Q], shift[:, :, Q:2 * Q], u).then_inc(normed, 1)
            chunks(act, (own, 3), (apply, 5), (exps, 1), (take, 3), (logs, 1), (root_log, 4), (root, 4),
                   (invert, 1), (rectify, 0))

        @block.tensor
        def _(pe):
            pe.wait_ge(weights, 80)
            pe.wait_ge(ready, 1)
            pe.matmul(psA[0:D + 1, 0:D], eps_col[:, :], wg[:, 0:D], start=True, stop=True)
            pe.transpose(psX[0:D, 0:D], wn[0:D, :], ident[0:D, 0:D])
            pe.transpose(psN[0:D, 0:D], wg[:, 0:D], ident[0:D, 0:D]).then_inc(set_up, 1)
            pe.wait_ge(widened, 1)
            pe.matmul(psA[0:D, 0:1], wnT[:, :], ad[:, :], start=True, stop=True)
            pe.transpose(psX[0:D, 0:D + 1], wx[:, 0:D], ident[0:D + 1, 0:D + 1]).then_inc(set_up, 1)
            pe.wait_ge(widened, 2)
            pe.matmul(psA[0:D, 0:1], wgT[:, :], v[:, :], start=True, stop=True)
            pe.matmul(psX[0:D + 1, 0:1], wxT[:, :], v[:, :], start=True, stop=True)
            pe.matmul(psN[:, 0:1], ones[:, :], v[:, :], start=True, stop=True).then_inc(set_up, 1)
            pe.wait_ge(widened, 3)

            def head(c, i, u, warm):
                pe.wait_ge(gathered[u], 128 * (i + 1))
                if warm or c == 1:
                    pe.wait_ge(rectified, c)
                turn(pe, psT, G[:, u, :, :], ident, True).then_inc(turned, 1)

            def tail(c, i, u, warm):
                pe.wait_ge(rows_in[u], 16 * LOADS * (i + 1))
                if warm or c == 1:
                    pe.wait_ge(tanhed, c)
                turn(pe, psN, xn[:, u, :, :], ident, False).then_inc(turned_n, 1)
                if warm or c == 1:
                    pe.wait_ge(copied_x, c)
                turn(pe, psX, xs[:, u, :, :], ident, False).then_inc(turned_x, 1)
                pe.wait_ge(copied_n, c + 1)
                for q in range(Q):
                    last = pe.matmul(N[:, q, 0:D], nT[:, q * 128:(q + 1) * 128], wn[:, :],
                                     start=True, stop=True)
                last.then_inc(rooted_n, 1)
                pe.wait_ge(averaged, c + 1)
                pe.wait_ge(copied_x, c + 1)
                if warm or c == 1:
                    pe.wait_ge(taken, c)
                for q in range(Q):
                    pe.matmul(A[:, q, 0:D + 1], inv[:, u, tile_columns(q)], wg[:, :],
                              start=True, stop=False)
                    last = pe.matmul(A[:, q, 0:D + 1], xT[:, q * 128:(q + 1) * 128], wx[:, :],
                                     start=False, stop=True)
                last.then_inc(multiplied, 1)
            chunks(pe, (tail, 3), (head, 0))


def spread(nc, ad_d, next_d, ads_d, ident):
    ctx = ExitStack()
    with ctx:
        def sb(tag, shape, dt=F32):
            return ctx.enter_context(nc.sbuf_tensor(f"sp_{tag}", shape, dt))

        def sem(tag):
            return ctx.enter_context(nc.semaphore(f"sp_{tag}"))

        a = sb("a", [128, J])
        nxt = sb("nxt", [128, J])
        only = sb("only", [128, J])
        ones = sb("ones", [128, J])
        keep = sb("keep", [128, J])
        found = sb("found", [128, J])
        rows = sb("rows", [1, 2, 128])
        carry = sb("carry", [1, 129])
        res = sb("res", [128, J])
        carried = sb("carried", [128, 1])
        ps = ctx.enter_context(nc.psum_tensor("sp_ps", [128, 512], F32))
        filled = sem("filled")
        loaded = sem("loaded")
        scanned = sem("scanned")
        turned = sem("turned")
        chained = sem("chained")
        returned = sem("returned")
        copied = sem("copied")
        done = sem("done")
        stored = sem("stored")
        block = ctx.enter_context(nc.Block())

        @block.sync
        def _(sp):
            sp.dma_start(a[:, :], ad_d.rearrange("a (p j) -> (a p) j", p=128)).then_inc(loaded, 16)
            sp.dma_start(nxt[:, :], next_d.rearrange("a (p j) -> (a p) j", p=128)).then_inc(loaded, 16)
            sp.wait_ge(done, 1)
            sp.dma_start(ads_d.rearrange("a (p j) -> (a p) j", p=128), res[:, :]).then_inc(stored, 16)
            sp.wait_ge(stored, 16)

        @block.vector
        def _(dve):
            dve.wait_ge(filled, 2)
            dve.wait_ge(loaded, 32)
            dve.tensor_tensor(only[:, :], nxt[:, :], a[:, :], ALU.mult)
            dve.drain()
            dve.tensor_tensor(only[:, :], a[:, :], only[:, :], ALU.subtract)
            dve.tensor_tensor_scan(keep[:, ::-1], nxt[:, ::-1], ones[:, ::-1], 1.0, ALU.mult, ALU.mult)
            dve.drain()
            dve.tensor_tensor_scan(found[:, ::-1], nxt[:, ::-1], only[:, ::-1], 0.0, ALU.mult, ALU.add)\
               .then_inc(scanned, 1)
            dve.wait_ge(turned, 1)
            dve.tensor_copy(rows[:, :, :], ps[0:1, 0:256].rearrange("p (a m) -> p a m", a=2))
            dve.drain()
            dve.tensor_tensor_scan(carry[:, 127::-1], rows[:, 0, ::-1], rows[:, 1, ::-1], 0.0,
                                   ALU.mult, ALU.add).then_inc(chained, 1)
            dve.wait_ge(copied, 1)
            dve.scalar_tensor_tensor(res[:, :], keep[:, :], carried[:, 0:1], found[:, :],
                                     ALU.mult, ALU.add).then_inc(done, 1)

        @block.scalar
        def _(act):
            act.wait_ge(returned, 1)
            act.activation(carried[:, :], ps[:, 256:257], ACT.Copy).then_inc(copied, 1)

        @block.gpsimd
        def _(pool):
            pool.memset(ones[:, :], 1.0).then_inc(filled, 1)
            pool.memset(carry[:, :], 0.0).then_inc(filled, 1)

        @block.tensor
        def _(pe):
            pe.wait_ge(scanned, 1)
            pe.transpose(ps[0:1, 0:128], keep[:, 0:1], ident[:, :])
            pe.transpose(ps[0:1, 128:256], found[:, 0:1], ident[:, :]).then_inc(turned, 1)
            pe.wait_ge(chained, 1)
            pe.matmul(ps[:, 256:257], carry[:, 1:129], ident[0:1, 0:1], start=True, stop=True)\
              .then_inc(returned, 1)


def layer3(nc, t3, src_rows, scat_d, ads_d, restart_d, out, Wa, att_s, att_d, ba, ident, eps,
           gathered, scattered):
    ctx = ExitStack()
    with ctx:
        def sb(tag, shape, dt=F32):
            return ctx.enter_context(nc.sbuf_tensor(f"l3_{tag}", shape, dt))

        def ps(tag):
            return ctx.enter_context(nc.psum_tensor(f"l3_{tag}", [128, 2 * 512], F32))

        def sem(tag):
            return ctx.enter_context(nc.semaphore(f"l3_{tag}"))

        wh = sb("wh", [D + 1, D + 1])
        wt = sb("wt", [D + 1, D + 1])
        att = sb("att", [D, 2])
        att_wide = sb("att_wide", [D, D + 1])
        waT = sb("waT", [D, D])
        ws_wide = sb("ws_wide", [D + 2, D + 1])
        idx = sb("idx", [128, 2, Q], I32)
        sidx = sb("sidx", [128, 2, Q], I32)
        G = sb("G", [128, 2, Q, D])
        restart = sb("restart", [D + 1, 2, CH], BF16)
        xs = sb("xs", [128, 2, Q, D])
        res = sb("res", [128, 2, Q, D])
        gT = sb("gT", [D + 2, 2, CH])
        score = sb("score", [D + 1, 2, CH])
        R = sb("R", [D + 1, 2, CH + 1])
        dd = sb("dd", [D + 1, 2, CH])
        P = sb("P", [D + 1, 2, CH])
        T = sb("T", [D + 1, 2, CH])
        xT = sb("xT", [D + 1, CH])
        own = sb("own", [128, 2, Q])
        top = sb("top", [128, Q])
        less = sb("less", [128, 2, Q])
        share = sb("share", [128, 2, Q])
        total = sb("total", [128, Q])
        e_out = sb("e_out", [128, 2, Q, D])
        t_out = sb("t_out", [128, 2, Q, D])
        s_out = sb("s_out", [128, 2, Q, D])
        st = sb("st", [128, Q, 6])
        mv = sb("mv", [128, 2, Q, 2])
        rstd = sb("rstd", [128, 2, Q])
        shift = sb("shift", [128, 2, Q])
        psT, psA, psX, psH = ps("psT"), ps("psA"), ps("psX"), ps("psH")
        A = psA[:, :].rearrange("p (q d) -> p q d", q=Q)
        Hp = psH[:, :].rearrange("p (q d) -> p q d", q=Q)

        weights = sem("weights")
        ready = sem("ready")
        set_up = sem("set_up")
        widened = sem("widened")
        idx_in = [sem("idx_in0"), sem("idx_in1")]
        restart_in = [sem("restart_in0"), sem("restart_in1")]
        ads_in = [sem("ads_in0"), sem("ads_in1")]
        rows_in = [sem("rows_in0"), sem("rows_in1")]
        res_in = [sem("res_in0"), sem("res_in1")]
        sidx_in = [sem("sidx_in0"), sem("sidx_in1")]
        turned = sem("turned")
        copied = sem("copied")
        scored = sem("scored")
        score_out = sem("score_out")
        differed = sem("differed")
        exped = sem("exped")
        mixed = sem("mixed")
        turned_x = sem("turned_x")
        copied_x = sem("copied_x")
        own_ready = sem("own_ready")
        own_out = sem("own_out")
        multiplied = sem("multiplied")
        lessened = sem("lessened")
        shares = sem("shares")
        weighed = sem("weighed")
        scaled = sem("scaled")
        joined = sem("joined")
        tanhed = sem("tanhed")
        summed = sem("summed")
        measured = sem("measured")
        rooted = sem("rooted")
        factored = sem("factored")
        normed = sem("normed")
        block = ctx.enter_context(nc.Block())

        @block.sync
        def _(sp):
            for t, w in ((wh[0:D, 0:D], Wa), (wh[D:D + 1, 0:D], ba), (wt[0:D, 0:D], Wa), (wt[D:D + 1, 0:D], ba),
                         (att[:, 0:1], att_s), (att[:, 1:2], att_d)):
                sp.dma_start(t, w).then_inc(weights, 16)

            def indices(c, i, u, warm):
                if warm:
                    wait(sp, gathered[u], 128 * i)
                sp.dma_start(idx[:, u, :], one(src_rows, c)).then_inc(idx_in[u], 16)

            def head(c, i, u, warm):
                if warm:
                    wait(sp, differed, c - 1)
                sp.dma_start(restart[:, u, :], span(restart_d, c, CH).to_broadcast([D + 1, CH]))\
                  .then_inc(restart_in[u], 16)
                if warm:
                    wait(sp, mixed, c - 1)
                sp.dma_start(gT[D + 1:D + 2, u, :], span(ads_d, c, CH)).then_inc(ads_in[u], 16)

            def rows(c, i, u, warm):
                if warm:
                    wait(sp, turned_x, c - 1)
                sp.dma_start(halves(xs[:, u, :, :]), rows_of(t3, c)).then_inc(rows_in[u], 16)

            def residual(c, i, u, warm):
                if warm:
                    wait(sp, summed, c - 1)
                sp.dma_start(halves(res[:, u, :, :]), rows_of(t3, c)).then_inc(res_in[u], 16)

            def nodes(c, i, u, warm):
                if warm:
                    wait(sp, scattered[u], 128 * i)
                sp.dma_start(sidx[:, u, :].rearrange("p (a r) -> p a r", a=2), scalars_of(scat_d, c))\
                  .then_inc(sidx_in[u], 16)
            chunks(sp, (indices, 0), (head, 1), (rows, 2), (residual, 4), (nodes, 6))

        @block.gpsimd
        def _(pool):
            def head(c, i, u, warm):
                wait(pool, idx_in[u], 16 * (i + 1))
                if warm:
                    wait(pool, turned, c - 1)
                gather(pool, G, u, t3, idx, gathered)

            def scatter(c, i, u, warm):
                wait(pool, sidx_in[u], 16 * (i + 1))
                wait(pool, normed, c + 1)
                for q in range(Q):
                    pool.indirect_dma_start(out, bass.IndirectOffsetOnAxis(sidx[:, u, q:q + 1], 0),
                                            s_out[:, u, q, :], None, bounds_check=NP - 1,
                                            oob_is_err=False).then_inc(scattered[u], 16)
            chunks(pool, (head, 0), (scatter, 6))
            for u in range(2):
                pool.wait_ge(scattered[u], 128 * (NCH // 2 + 1 - u))

        @block.vector
        def _(dve):
            dve.memset(R[:, 1, CH:CH + 1], 0.0)
            dve.memset(T[:, 1, CH - 1:CH], 0.0)
            dve.memset(gT[D:D + 1, :, :], 1.0)
            dve.memset(xT[D:D + 1, :], 1.0)
            dve.memset(wh[D:D + 1, D:D + 1], 0.0)
            dve.memset(wt[0:D, D:D + 1], 0.0)
            dve.memset(ws_wide[D:D + 2, :], 1.0)
            dve.drain()
            dve.memset(wt[D:D + 1, D:D + 1], 1.0)
            dve.memset(ws_wide[D:D + 1, :], 0.0)
            dve.wait_ge(weights, 96)
            dve.tensor_copy(att_wide[:, :], att[:, 0:1].to_broadcast([D, D + 1])).then_inc(ready, 1)
            dve.wait_ge(set_up, 1)
            dve.tensor_copy(waT[:, :], psX[0:D, 0:D]).then_inc(widened, 1)
            dve.wait_ge(set_up, 2)
            dve.tensor_copy(ws_wide[0:D, :], psA[0:D, 0:D + 1])
            dve.tensor_copy(wh[0:D, D:D + 1], psH[0:D, 0:1]).then_inc(widened, 1)

            def head(c, i, u, warm):
                dve.wait_ge(score_out, c + 1)
                dve.scalar_tensor_tensor(score[:, u, :], score[:, u, :], LEAK_ATT, score[:, u, :],
                                         ALU.mult, ALU.max)
                dve.drain()
                dve.wait_ge(restart_in[u], 16 * (i + 1))
                if warm:
                    dve.wait_ge(multiplied, c - 1)
                running_softmax(dve, restart[:, u, :], score[:, u, :], R, dd, u, differed)

            def scores(c, i, u, warm):
                dve.wait_ge(own_out, c + 1)
                dve.scalar_tensor_tensor(own[:, u, :], own[:, u, :], LEAK_ATT, own[:, u, :],
                                         ALU.mult, ALU.max)
                dve.drain()
                dve.wait_ge(multiplied, c + 1)
                dve.tensor_tensor(top[:, :], own[:, u, :], A[:, :, D + 1], ALU.max)
                dve.drain()
                dve.tensor_tensor(less[:, 0, :], A[:, :, D + 1], top[:, :], ALU.subtract)
                dve.tensor_tensor(less[:, 1, :], own[:, u, :], top[:, :], ALU.subtract).then_inc(lessened, 1)

            def post(c, i, u, warm):
                dve.wait_ge(tanhed, c + 1)
                dve.wait_ge(res_in[u], 16 * (i + 1))
                dve.tensor_tensor(t_out[:, u, :, :], t_out[:, u, :, :], res[:, u, :, :], ALU.add)\
                   .then_inc(summed, 1)
                dve.drain()
                norm_stats(dve, [t_out[:, u, q, :] for q in range(Q)], st, mv, u, measured)

            def weigh(c, i, u, warm):
                dve.wait_ge(shares, c + 1)
                dve.tensor_tensor(total[:, :], A[:, :, D], share[:, 0, :], ALU.mult)
                dve.drain()
                dve.scalar_tensor_tensor(total[:, :], total[:, :], 1e-16, share[:, 1, :], ALU.add, ALU.add)
                dve.drain()
                dve.reciprocal(total[:, :], total[:, :])
                dve.drain()
                dve.tensor_tensor(share[:, :, :], share[:, :, :],
                                  total[:, :].unsqueeze(1).to_broadcast([128, 2, Q]), ALU.mult)\
                   .then_inc(weighed, 1)

            def sums(c, i, u, warm):
                dve.wait_ge(exped, c + 1)
                dve.tensor_tensor(P[:, 1, :], P[:, 1, :], gT[0:D + 1, u, :], ALU.mult)
                dve.drain()
                if warm:
                    dve.wait_ge(multiplied, c - 1)
                dve.tensor_tensor_scan(T[:, u, :], P[:, 0, :], P[:, 1, :], T[:, 1 - u, CH - 1:CH],
                                       ALU.mult, ALU.add).then_inc(mixed, 1)

            def join(c, i, u, warm):
                dve.wait_ge(scaled, c + 1)
                for q in range(Q):
                    last = dve.scalar_tensor_tensor(e_out[:, u, q, :], Hp[:, q, 0:D], share[:, 1, q:q + 1],
                                                    e_out[:, u, q, :], ALU.mult, ALU.add)
                last.then_inc(joined, 1)

            def factors(c, i, u, warm):
                dve.wait_ge(rooted, c + 1)
                norm_factors(dve, mv, rstd, shift, u, factored)
            chunks(dve, (scores, 3), (weigh, 3), (head, 1), (join, 3), (post, 4), (sums, 1),
                   (factors, 4))

        @block.scalar
        def _(act):
            def copy(c, i, u, warm):
                act.wait_ge(turned, c + 1)
                if warm:
                    act.wait_ge(mixed, c - 1)
                act.activation(gT[0:D, u, :], psT[0:D, :], ACT.Copy).then_inc(copied, 1)

            def own_rows(c, i, u, warm):
                act.wait_ge(turned_x, c + 1)
                if warm or c == 1:
                    act.wait_ge(own_ready, c)
                act.activation(xT[0:D, :], psX[0:D, :], ACT.Copy).then_inc(copied_x, 1)

            def take(c, i, u, warm):
                act.wait_ge(scored, c + 1)
                if warm:
                    act.wait_ge(differed, c - 1)
                act.activation(score[:, u, :], psT[0:D + 1, :], ACT.Copy).then_inc(score_out, 1)

            def exps(c, i, u, warm):
                act.wait_ge(differed, c + 1)
                if warm or c == 1:
                    act.wait_ge(mixed, c)
                act.activation(P[:, :, :], dd[:, :, :], ACT.Exp).then_inc(exped, 1)

            def join(c, i, u, warm):
                act.wait_ge(lessened, c + 1)
                if warm or c == 1:
                    act.wait_ge(joined, c)
                act.activation(share[:, :, :], less[:, :, :], ACT.Exp).then_inc(shares, 1)

            def scale(c, i, u, warm):
                act.wait_ge(weighed, c + 1)
                if warm:
                    act.wait_ge(tanhed, c - 1)
                for q in range(Q):
                    last = act.activation(e_out[:, u, q, :], A[:, q, 0:D], ACT.Copy,
                                          scale=share[:, 0, q:q + 1])
                last.then_inc(scaled, 1)

            def root(c, i, u, warm):
                act.wait_ge(measured, c + 1)
                act.activation(rstd[:, u, :], mv[:, u, :, 1], ACT.Sqrt, bias=eps[:, :]).then_inc(rooted, 1)

            def apply(c, i, u, warm):
                act.wait_ge(factored, c + 1)
                if warm:
                    act.wait_ge(scattered[u], 128 * i)
                norm_apply(act, [t_out[:, u, q, :] for q in range(Q)], [s_out[:, u, q, :] for q in range(Q)],
                           rstd, shift, u).then_inc(normed, 1)

            def tanh(c, i, u, warm):
                act.wait_ge(joined, c + 1)
                if warm:
                    act.wait_ge(normed, c - 1)
                act.activation(t_out[:, u, :, :], e_out[:, u, :, :], ACT.Tanh).then_inc(tanhed, 1)

            def take_own(c, i, u, warm):
                act.wait_ge(own_ready, c + 1)
                if warm:
                    act.wait_ge(lessened, c - 1)
                act.activation(own[:, u, :], Hp[:, :, D], ACT.Copy).then_inc(own_out, 1)
            chunks(act, (join, 3), (scale, 3), (copy, 0), (own_rows, 2), (apply, 5), (exps, 1), (tanh, 3),
                   (take, 0), (root, 4), (take_own, 2))

        @block.tensor
        def _(pe):
            pe.wait_ge(weights, 96)
            pe.wait_ge(ready, 1)
            pe.transpose(psX[0:D, 0:D], wh[0:D, 0:D], ident[0:D, 0:D]).then_inc(set_up, 1)
            pe.wait_ge(widened, 1)
            pe.matmul(psA[0:D, 0:D + 1], waT[:, :], att_wide[:, :], start=True, stop=True)
            pe.matmul(psH[0:D, 0:1], waT[:, :], att[:, 0:1], start=True, stop=False)
            pe.matmul(psH[0:D, 0:1], waT[:, :], att[:, 1:2], start=False, stop=True).then_inc(set_up, 1)
            pe.wait_ge(widened, 2)

            def head(c, i, u, warm):
                pe.wait_ge(gathered[u], 128 * (i + 1))
                if warm or c == 1:
                    pe.wait_ge(score_out, c)
                turn(pe, psT, G[:, u, :, :], ident, True).then_inc(turned, 1)

            def own_rows(c, i, u, warm):
                pe.wait_ge(rows_in[u], 16 * (i + 1))
                if warm or c == 1:
                    pe.wait_ge(copied_x, c)
                turn(pe, psX, xs[:, u, :, :], ident, False).then_inc(turned_x, 1)

            def scores(c, i, u, warm):
                pe.wait_ge(copied, c + 1)
                pe.wait_ge(ads_in[u], 16 * (i + 1))
                for h in range(2):
                    part = slice(h * 512, h * 512 + 512)
                    last = pe.matmul(psT[0:D + 1, part], ws_wide[:, :], gT[:, u, part],
                                     start=True, stop=True)
                last.then_inc(scored, 1)

            def tail(c, i, u, warm):
                pe.wait_ge(mixed, c + 1)
                if warm or c == 1:
                    pe.wait_ge(scaled, c)
                for q in range(Q):
                    at = tile_columns(q)
                    pe.matmul(A[:, q, 0:D + 1], T[:, u, at], wt[:, :], start=True, stop=True)
                    shifted = slice(at.start + 1, at.stop + 1, H)
                    last = pe.transpose(A[:, q, D + 1:D + 2], R[0:1, u, shifted], ident[0:1, 0:1])
                last.then_inc(multiplied, 1)

            def own_products(c, i, u, warm):
                pe.wait_ge(copied_x, c + 1)
                if warm or c == 1:
                    pe.wait_ge(joined, c)
                for q in range(Q):
                    last = pe.matmul(Hp[:, q, 0:D + 1], xT[:, q * 128:(q + 1) * 128], wh[:, :],
                                     start=True, stop=True)
                last.then_inc(own_ready, 1)
            chunks(pe, (head, 0), (own_rows, 2), (tail, 2), (scores, 0), (own_products, 2))


def kernel(**inputs):
    import concourse.bacc as bacc
    from concourse.bass_utils import run_bass_kernel_spmd

    nc = bacc.Bacc("TRN2", target_bir_lowering=False, num_devices=1)
    arrays = {}

    def put(name, array):
        arrays[name] = np.ascontiguousarray(array)
        return nc.dram_tensor(name, arrays[name].shape, mybir.dt.from_np(arrays[name].dtype),
                              kind="ExternalInput").ap()

    src, dst = (np.concatenate([np.asarray(inputs[k]), np.full(EP - N_EDGES, N_NODES, np.int32)])
                for k in ("src", "dst"))
    x = np.concatenate([np.asarray(inputs["x"]), np.zeros((NP - N_NODES, D), np.float32)])
    ids = np.concatenate([a.reshape(NCH, 2, 128, H).transpose(0, 2, 1, 3).reshape(NCH, 128, Q)
                          for a in (src, dst)], axis=2)
    dst_ext = np.concatenate([np.full(1, -1, np.int32), dst, np.full(1, NP, np.int32)])
    attr = np.concatenate([np.asarray(inputs["edge_attr_32"]), np.zeros((EP - N_EDGES, DE), np.float32)])
    args = [put("x_pad", x), put("ids", ids), put("dst_ext", dst_ext), put("edge_t", attr.T)]
    for name in ("L0_gnn_W", "L0_gnn_b", "L1_gnn_W1_msg", "L1_gnn_W1_edge", "L1_gnn_W1_root", "L1_gnn_b1",
                 "L1_gnn_W2_msg", "L1_gnn_W2_edge", "L1_gnn_W2_root", "L1_gnn_b2", "L2_gnn_W", "L2_gnn_b",
                 "L3_gnn_W", "L3_gnn_att_src", "L3_gnn_att_dst", "L3_gnn_bias"):
        a = np.asarray(inputs[name])
        if a.ndim == 1:
            a = a.reshape((D, 1) if "att" in name else (1, D))
        args.append(put(name, a))
    out = nc.dram_tensor("out", (NP, D), F32, kind="ExternalOutput").ap()
    segment_kernel(nc, *args, out)
    run = run_bass_kernel_spmd(nc, [arrays], core_ids=[0])
    return run.results[0]["out"][:N_NODES]
```
